# Optimizing a Trainium2 kernel written in Bass

```python
import numpy as np
import jax
import jax.numpy as jnp

def _softmax(x, axis=-1):
    return jax.nn.softmax(x, axis=axis)

def _gelu(x):
    return jax.nn.gelu(x, approximate=True)

def _silu(x):
    return jax.nn.silu(x)

def _sigmoid(x):
    return jax.nn.sigmoid(x)

def _layernorm(x, axis=-1, eps=1e-05):
    m = jnp.mean(x, axis=axis, keepdims=True)
    v = jnp.var(x, axis=axis, keepdims=True)
    return (x - m) / jnp.sqrt(v + eps)

def _scatter_add(tgt, idx, src, axis=0):
    return tgt.at[idx].add(src)

def _segment_sum(src, seg, n):
    return jax.ops.segment_sum(src, seg, n)
kernel_name = 'mk_macaron_d1_jaxref_r4_83dea8'

def setup_inputs(seed: int=0):
    np.random.seed(seed)
    _w = jnp.asarray

    def _L0_attn_setup():
        import jax, jax.numpy as jnp
        import numpy as np
        from jax import lax
        SPLIT = 8
        DIM = 16
        EPS = 1e-05

        def _branch(q, k, v, cw, cb, H_sp, W_sp, Hg, Wg):
            B, N, C = q.shape
            hd = C
            scale = hd ** (-0.5)
            wsz = H_sp * W_sp
            nh, nw = (Hg // H_sp, Wg // W_sp)

            def part(t):
                t = t.reshape(B, nh, H_sp, nw, W_sp, C).transpose(0, 1, 3, 2, 4, 5)
                return t.reshape(-1, wsz, 1, hd).transpose(0, 2, 1, 3)
            vimg = v.reshape(B, nh, H_sp, nw, W_sp, C).transpose(0, 1, 3, 5, 2, 4)
            vimg = vimg.reshape(-1, C, H_sp, W_sp)
            lepe = lax.conv_general_dilated(vimg, cw, (1, 1), [(1, 1), (1, 1)], dimension_numbers=('NCHW', 'OIHW', 'NCHW'), feature_group_count=C)
            lepe = lepe + cb[None, :, None, None]
            lepe = lepe.reshape(-1, 1, hd, wsz).transpose(0, 1, 3, 2)
            vw = vimg.reshape(-1, 1, hd, wsz).transpose(0, 1, 3, 2)
            attn = jax.nn.softmax(part(q) * scale @ jnp.swapaxes(part(k), -1, -2), axis=-1)
            out = attn @ vw + lepe
            out = out.transpose(0, 2, 1, 3).reshape(B, nh, nw, H_sp, W_sp, C)
            out = out.transpose(0, 1, 3, 2, 4, 5).reshape(B, N, C)
            return out
        key = jax.random.key(seed)
        ks = jax.random.split(key, 8)
        B, H, W = (8, 512, 512)
        d = DIM
        h = d // 2
        return {'x': jax.random.normal(ks[0], (B, H, W), jnp.float32), 'qkv_w': jax.random.normal(ks[1], (d, 3 * d), jnp.float32) * d ** (-0.5), 'conv_w0': jax.random.normal(ks[2], (h, 1, 3, 3), jnp.float32) * 0.3, 'conv_b0': jax.random.normal(ks[3], (h,), jnp.float32) * 0.02, 'conv_w1': jax.random.normal(ks[4], (h, 1, 3, 3), jnp.float32) * 0.3, 'conv_b1': jax.random.normal(ks[5], (h,), jnp.float32) * 0.02, 'proj_w': jax.random.normal(ks[6], (d, d), jnp.float32) * d ** (-0.5), 'proj_b': jax.random.normal(ks[7], (d,), jnp.float32) * 0.02, 'ln_w': jnp.ones((d,), jnp.float32), 'ln_b': jnp.zeros((d,), jnp.float32)}
    _L0_attn_in = _L0_attn_setup()

    def _L0_ffn_setup():
        import jax, jax.numpy as jnp
        import numpy as np
        B, S, D = (2, 512, 512)
        E = 8
        TOPK = 2
        H_SHARED = 2048
        H_ROUTED = 256
        STD = 0.02
        key = jax.random.key(seed)
        ks = jax.random.split(key, 7)
        return {'x': jax.random.normal(ks[0], (B, S, D), jnp.float32), 'w12': jax.random.normal(ks[1], (E, 2 * H_ROUTED, D), jnp.float32) * STD, 'w3': jax.random.normal(ks[2], (E, D, H_ROUTED), jnp.float32) * STD, 'router_w': jax.random.normal(ks[3], (E, D), jnp.float32) * STD, 'expert_bias': jnp.zeros((E,), jnp.float32), 'sw1': jax.random.normal(ks[4], (H_SHARED, D), jnp.float32) * STD, 'sw2': jax.random.normal(ks[5], (H_SHARED, D), jnp.float32) * STD, 'sw3': jax.random.normal(ks[6], (D, H_SHARED), jnp.float32) * STD}
    _L0_ffn_in = _L0_ffn_setup()
    _d = {'L0_attn_x': _L0_attn_in['x'], 'L0_attn_qkv_w': _L0_attn_in['qkv_w'], 'L0_attn_conv_w0': _L0_attn_in['conv_w0'], 'L0_attn_conv_b0': _L0_attn_in['conv_b0'], 'L0_attn_conv_w1': _L0_attn_in['conv_w1'], 'L0_attn_conv_b1': _L0_attn_in['conv_b1'], 'L0_attn_proj_w': _L0_attn_in['proj_w'], 'L0_attn_proj_b': _L0_attn_in['proj_b'], 'L0_attn_ln_w': _L0_attn_in['ln_w'], 'L0_attn_ln_b': _L0_attn_in['ln_b'], 'L0_ffn_w12': _L0_ffn_in['w12'], 'L0_ffn_w3': _L0_ffn_in['w3'], 'L0_ffn_router_w': _L0_ffn_in['router_w'], 'L0_ffn_expert_bias': _L0_ffn_in['expert_bias'], 'L0_ffn_sw1': _L0_ffn_in['sw1'], 'L0_ffn_sw2': _L0_ffn_in['sw2'], 'L0_ffn_sw3': _L0_ffn_in['sw3']}
    _x0 = _d['L0_attn_x']
    _d['L0_attn_x'] = jax.random.normal(jax.random.fold_in(jax.random.key(seed), 1), (4, 512, 512), dtype=_x0.dtype)
    del _x0
    return _d

def reference(L0_attn_x, L0_attn_qkv_w, L0_attn_conv_w0, L0_attn_conv_b0, L0_attn_conv_w1, L0_attn_conv_b1, L0_attn_proj_w, L0_attn_proj_b, L0_attn_ln_w, L0_attn_ln_b, L0_ffn_w12, L0_ffn_w3, L0_ffn_router_w, L0_ffn_expert_bias, L0_ffn_sw1, L0_ffn_sw2, L0_ffn_sw3):

    def _L0_attn_ref(x, qkv_w, conv_w0, conv_b0, conv_w1, conv_b1, proj_w, proj_b, ln_w, ln_b):
        import jax, jax.numpy as jnp
        import numpy as np
        from jax import lax
        SPLIT = 8
        DIM = 16
        EPS = 1e-05

        def _branch(q, k, v, cw, cb, H_sp, W_sp, Hg, Wg):
            B, N, C = q.shape
            hd = C
            scale = hd ** (-0.5)
            wsz = H_sp * W_sp
            nh, nw = (Hg // H_sp, Wg // W_sp)

            def part(t):
                t = t.reshape(B, nh, H_sp, nw, W_sp, C).transpose(0, 1, 3, 2, 4, 5)
                return t.reshape(-1, wsz, 1, hd).transpose(0, 2, 1, 3)
            vimg = v.reshape(B, nh, H_sp, nw, W_sp, C).transpose(0, 1, 3, 5, 2, 4)
            vimg = vimg.reshape(-1, C, H_sp, W_sp)
            lepe = lax.conv_general_dilated(vimg, cw, (1, 1), [(1, 1), (1, 1)], dimension_numbers=('NCHW', 'OIHW', 'NCHW'), feature_group_count=C)
            lepe = lepe + cb[None, :, None, None]
            lepe = lepe.reshape(-1, 1, hd, wsz).transpose(0, 1, 3, 2)
            vw = vimg.reshape(-1, 1, hd, wsz).transpose(0, 1, 3, 2)
            attn = jax.nn.softmax(part(q) * scale @ jnp.swapaxes(part(k), -1, -2), axis=-1)
            out = attn @ vw + lepe
            out = out.transpose(0, 2, 1, 3).reshape(B, nh, nw, H_sp, W_sp, C)
            out = out.transpose(0, 1, 3, 2, 4, 5).reshape(B, N, C)
            return out
        B, H, W = x.shape
        Hg, Wg = (H // 4, W // 4)
        C = DIM
        tok = x.reshape(B, H * W // C, C)
        qkv = (tok @ qkv_w).reshape(B, -1, 3, C)
        q, k, v = (qkv[:, :, 0], qkv[:, :, 1], qkv[:, :, 2])
        h = C // 2
        x1 = _branch(q[..., :h], k[..., :h], v[..., :h], conv_w0, conv_b0, 1, SPLIT, Hg, Wg)
        x2 = _branch(q[..., h:], k[..., h:], v[..., h:], conv_w1, conv_b1, SPLIT, 1, Hg, Wg)
        att = jnp.concatenate([x1, x2], axis=-1) @ proj_w + proj_b
        mu = att.mean(-1, keepdims=True)
        var = ((att - mu) ** 2).mean(-1, keepdims=True)
        normed = (att - mu) * lax.rsqrt(var + EPS) * ln_w + ln_b
        tok = tok + normed
        return jnp.transpose(tok, (0, 2, 1)).reshape(B, H, W)

    def _L0_ffn_ref(x, w12, w3, router_w, expert_bias, sw1, sw2, sw3):
        import jax, jax.numpy as jnp
        import numpy as np
        B, S, D = (2, 512, 512)
        E = 8
        TOPK = 2
        H_SHARED = 2048
        H_ROUTED = 256
        STD = 0.02
        b, s, d = x.shape
        g = x @ sw1.T
        u = x @ sw2.T
        shared_out = jax.nn.silu(g) * u @ sw3.T
        scores = jax.nn.sigmoid(x @ router_w.T)
        selection_scores = scores + expert_bias
        _, top_idx = jax.lax.top_k(selection_scores, TOPK)
        top_scores = jnp.take_along_axis(scores, top_idx, axis=-1)
        top_scores = top_scores / (top_scores.sum(-1, keepdims=True) + 1e-09)
        flat_x = x.reshape(-1, d)
        T = flat_x.shape[0]
        flat_idx = top_idx.reshape(T, TOPK)
        flat_sc = top_scores.reshape(T, TOPK)
        combine = jnp.zeros((T, E), x.dtype).at[jnp.arange(T)[:, None], flat_idx].add(flat_sc)
        h12 = jnp.einsum('td,ehd->teh', flat_x, w12)
        h1, h2 = jnp.split(h12, 2, axis=-1)
        h = jax.nn.silu(h1) * h2
        out_e = jnp.einsum('teh,edh->ted', h, w3)
        routed_out = jnp.einsum('ted,te->td', out_e, combine).reshape(b, s, d)
        return shared_out + routed_out
    x = L0_attn_x
    x = x + 0.5 * _L0_ffn_ref(_layernorm(x, axis=-1), L0_ffn_w12, L0_ffn_w3, L0_ffn_router_w, L0_ffn_expert_bias, L0_ffn_sw1, L0_ffn_sw2, L0_ffn_sw3)
    x = x + _L0_attn_ref(_layernorm(x, axis=-1), L0_attn_qkv_w, L0_attn_conv_w0, L0_attn_conv_b0, L0_attn_conv_w1, L0_attn_conv_b1, L0_attn_proj_w, L0_attn_proj_b, L0_attn_ln_w, L0_attn_ln_b)
    x = x + 0.5 * _L0_ffn_ref(_layernorm(x, axis=-1), L0_ffn_w12, L0_ffn_w3, L0_ffn_router_w, L0_ffn_expert_bias, L0_ffn_sw1, L0_ffn_sw2, L0_ffn_sw3)
    return x

_drawn_inputs = setup_inputs


def setup_inputs(seed=0):
    import zlib

    import numpy as np

    out = dict(_drawn_inputs(seed))
    spreads = {'L0_attn_ln_w': (1.0, 0.2), 'L0_attn_ln_b': (0.0, 0.1), 'L0_ffn_expert_bias': (0.0, 0.432)}
    factors = {'L0_attn_conv_b1': 3.855,
     'L0_attn_proj_b': 2.912,
     'L0_ffn_w12': 2.919,
     'L0_ffn_router_w': 3.572}
    for name, (base, spread) in spreads.items():
        noise = np.random.default_rng([zlib.crc32(name.encode()), seed]).standard_normal(out[name].shape)
        drawn = base * np.exp(spread * noise) if base else spread * noise
        out[name] = jnp.asarray(drawn.astype(out[name].dtype))
    for name, factor in factors.items():
        out[name] = (out[name] * factor).astype(out[name].dtype)
    return out
```

```python
from contextlib import ExitStack

import concourse.bass as bass
from concourse import mybir

ALU = mybir.AluOpType
ACT = mybir.ActivationFunctionType
AX = mybir.AxisListType
F32 = mybir.dt.float32
BF16 = mybir.dt.bfloat16
I32 = mybir.dt.int32

P = 128
EPS = 1e-5


class Count:

    def __init__(self, sem):
        self.sem = sem
        self.n = 0


class Own:

    def __init__(self, eng, count):
        self.eng, self.c, self.reg, self.k = eng, count, None, 0

    def do(self, ins):
        ins.then_inc(self.c.sem, 1)
        self.k += 1
        return ins

    def value(self):
        return self.c.n + self.k if self.reg is None else self.reg + (self.c.n + self.k)

    def sync(self):
        if self.reg is None and self.c.n + self.k == 0:
            return
        self.eng.wait_ge(self.c.sem, self.value())

    def loop(self, count, per_turn, body):
        self.c.n += self.k
        self.k = 0
        with self.eng.Fori(0, count) as i:
            self.reg = i * per_turn
            body(i)
            assert self.k == per_turn, (self.k, per_turn)
        self.reg, self.k = None, 0
        self.c.n += count * per_turn


def macaron(nc, x, wsh, wrt, rwT, ebias, qkvw, projw, projb, convw, convb, lnw, lnb, out):
    ROWS, D = x.shape
    NDC = D // P
    E = rwT.shape[1]
    NU = wsh.shape[0]
    WW = wsh.shape[2]
    HC = 256
    KT = HC // P
    UROWS = 1024
    NT = UROWS // P
    HALF = 512
    TH = HALF // P
    NB = (2 * UROWS + E * (P - 1)) // P
    NIMG = 4
    C = qkvw.shape[0]
    H = C // 2
    SP_ = 8
    NPI = 8
    NPJ = 16
    NTOK = NPI * NPJ
    NW = NTOK // SP_
    SCALE = float(H) ** -0.5
    W3OFF = 2 * NDC * HC
    assert W3OFF + KT * D == WW and NB == 23

    x1d = nc.dram_tensor("x1d", [ROWS, D], F32).ap()
    xln2 = nc.dram_tensor("xln2", [ROWS, D], F32).ap()
    attd = nc.dram_tensor("attd", [ROWS, D], F32).ap()
    x2d = nc.dram_tensor("x2d", [ROWS, D], F32).ap()
    sorted_x = nc.dram_tensor("sorted_x", [(NB + 1) * P, D], F32).ap()
    sorted_y = nc.dram_tensor("sorted_y", [NB * P, D], F32).ap()
    wsplit = nc.dram_tensor("wsplit", [NU, P, 2 * WW], BF16).ap()

    ctx = ExitStack()
    with ctx:
        def sb(name, shape, dt=F32):
            return ctx.enter_context(nc.sbuf_tensor(name, shape, dt))

        def counter(name):
            return Count(ctx.enter_context(nc.semaphore(name)))

        banks = [ctx.enter_context(nc.psum_tensor(f"bank{i}", [P, 512], F32)) for i in range(8)]

        wr = sb("wr", [P, E, 2, WW], BF16)
        wb = sb("wb", [P, 2, 2, WW], BF16)
        acc = sb("acc", [P, NT, D])
        xT = sb("xT", [P, 2, NDC, UROWS], BF16)
        hs = sb("hs", [P, 2, 2, KT, HALF], BF16)
        region = sb("region", [P, 10624])
        ident = sb("ident", [P, P])
        identb = sb("identb", [P, P], BF16)
        tri = sb("tri", [P, P])
        ones = sb("ones", [P, P])
        rw = sb("rw", [P, NDC, E])
        eb = sb("eb", [P, E])
        iota8 = sb("iota8", [P, E])
        steps8 = sb("steps8", [P, NT])
        bidx = sb("bidx", [P, NB])
        wqkv = sb("wqkv", [P, 8 * 3 * C])
        wproj = sb("wproj", [P, 8 * C])
        pbrow = sb("pbrow", [P, 8 * C])
        cw = sb("cw", [P, 3, C])
        cb = sb("cb", [P, C])
        lw = sb("lw", [P, C])
        lb = sb("lb", [P, C])
        nhalf = sb("nhalf", [P, NTOK])
        mv = sb("mv", [P, 2, 2])
        rstd = sb("rstd", [P, 2, 1])
        stats = sb("stats", [P, 2, 6])
        scores = sb("scores", [P, NT, E])
        coef = sb("coef", [P, 2, NT])
        slots = sb("slots", [P, 2, NT], I32)
        bexp = sb("bexp", [P, NB], I32)

        own = {n: counter(f"own_{n}") for n in ("dve", "act", "pool")}

        reg_at = [0]

        def take(n, dt=F32):
            a = region[:, reg_at[0]:reg_at[0] + n]
            reg_at[0] += n
            assert reg_at[0] <= 10624
            return a if dt == F32 else a.bitcast(dt)

        sems = {}

        def S(name):
            if name not in sems:
                sems[name] = counter(name)
            return sems[name]

        class Arrivals:

            def __init__(self, name, per=1):
                self.pair = [S(f"{name}_{q}") for q in range(2)]
                self.per = 16 * per
                self.base = [c.n for c in self.pair]

            def sem(self, k):
                return self.pair[k % 2].sem

            def wait(self, e, k, i=None, step=2):
                n = self.base[k % 2] + self.per * (k // 2 + 1)
                e.wait_ge(self.sem(k), n if i is None else i * (self.per * step // 2) + n)

            def end(self, items):
                for q in range(2):
                    self.pair[q].n += self.per * ((items + 1 - q) // 2)

        s_const, s_zero = counter("const_loaded"), counter("const_zeroed")
        s_hi, s_lo = counter("w_high"), counter("w_low")
        w_loaded, w_stored = Arrivals("w_loaded"), Arrivals("w_stored")
        raw_w = [take(WW) for _ in range(2)]
        zero = take(D)
        NW_ALL = NU + E

        with nc.Block() as blk:
            @blk.gpsimd
            def _(e):
                o = Own(e, own["pool"])
                o.do(e.memset(wqkv[:], 0.0))
                o.do(e.memset(wproj[:], 0.0))
                o.do(e.memset(zero, 0.0))
                o.do(e.memset(ones[:], 1.0))
                o.do(e.memset(nhalf[:], -0.5))
                o.do(e.iota(iota8[:], pattern=[[1, E]], base=-E, channel_multiplier=0, allow_small_or_imprecise_dtypes=True))
                o.do(e.iota(steps8[:], pattern=[[P, NT]], base=0, channel_multiplier=0, allow_small_or_imprecise_dtypes=True))
                o.do(e.iota(bidx[:], pattern=[[1, NB]], base=0, channel_multiplier=0, allow_small_or_imprecise_dtypes=True))
                o.sync()
                e.engine_nop().then_inc(s_zero.sem, 1)
                o.do(e.affine_select(out=ident[:], in_=ones[:], pattern=[[-1, P]], compare_op=ALU.is_equal,
                                     fill=0.0, base=0, channel_multiplier=1))
                o.do(e.affine_select(out=tri[:], in_=ones[:], pattern=[[1, P]], compare_op=ALU.is_gt,
                                     fill=0.0, base=0, channel_multiplier=-1))
                o.sync()
                o.do(e.tensor_copy(identb[:], ident[:]))
                o.sync()
                own["pool"].n += o.k

            @blk.sync
            def _(e):
                for n in range(NW_ALL):
                    src = wsh[n] if n < NU else wrt[n - NU]
                    if n >= 2:
                        e.wait_ge(s_hi.sem, n - 1)
                        e.wait_ge(s_lo.sem, n - 1)
                    e.dma_start(raw_w[n % 2], src).then_inc(w_loaded.sem(n), 16)
                w_stored.wait(e, NU - 2)
                w_stored.wait(e, NU - 1)

            @blk.scalar
            def _(e):
                c = s_const

                def load(dst, src):
                    e.dma_start(dst, src).then_inc(c.sem, 16)
                    c.n += 16

                load(rw[:], rwT.rearrange("(c p) e -> p c e", p=P))
                for dst, src in ((eb[:], ebias), (cb[:], convb), (lw[:], lnw), (lb[:], lnb)):
                    load(dst, src.partition_broadcast(P))
                load(cw[:].rearrange("p a c -> p (a c)"), convw.rearrange("a c -> (a c)").partition_broadcast(P))
                e.wait_ge(s_zero.sem, 1)
                for t in range(8):
                    load(wqkv[C * t:C * t + C, 3 * C * t:3 * C * t + 3 * C], qkvw)
                    load(wproj[C * t:C * t + C, C * t:C * t + C], projw)
                    load(pbrow[0:1, C * t:C * t + C], projb.rearrange("(a c) -> a c", a=1))
                for b in range(NB + 1):
                    load(sorted_x[b * P:(b + 1) * P, :], zero)
                for n in range(NW_ALL):
                    w_loaded.wait(e, n)
                    if n >= 2 and n < NU:
                        w_stored.wait(e, n - 2)
                    dst = wb[:, n % 2] if n < NU else wr[:, n - NU]
                    e.activation(dst[:, 0, :], raw_w[n % 2], ACT.Copy).then_inc(s_hi.sem, 1)
                    if n < NU:
                        e.wait_ge(s_hi.sem, n + 1)
                        e.wait_ge(s_lo.sem, n + 1)
                        e.dma_start(wsplit[n], wb[:, n % 2].rearrange("p a w -> p (a w)")).then_inc(w_stored.sem(n), 16)
                e.wait_ge(c.sem, c.n)

            @blk.vector
            def _(e):
                for n in range(NW_ALL):
                    e.wait_ge(s_hi.sem, n + 1)
                    dst = wb[:, n % 2] if n < NU else wr[:, n - NU]
                    e.tensor_tensor(dst[:, 1, :], raw_w[n % 2], dst[:, 0, :], ALU.subtract).then_inc(s_lo.sem, 1)

        def prepare(f, u):
            reg_at[0] = 0
            xr = [take(D) for _ in range(2)]
            xT32 = [take(D) for _ in range(2)]
            xn = take(NT * D).rearrange("p (t d) -> p t d", t=NT)
            sel = take(NT * E).rearrange("p (t e) -> p t e", t=NT)
            eq = take(NT * E).rearrange("p (t e) -> p t e", t=NT)
            oh = [take(NT * E).rearrange("p (t e) -> p t e", t=NT) for _ in range(2)]
            sel2 = take(NT * E).rearrange("p (t e) -> p t e", t=NT)
            msum = take(NT * E).rearrange("p (t e) -> p t e", t=NT)
            rank = take(NT * E).rearrange("p (t e) -> p t e", t=NT)
            tp = take((NT + 1) * E).rearrange("p (t e) -> p t e", t=NT + 1)
            mx = take(NT)
            mn = take(NT)
            wsel = [take(NT) for _ in range(2)]
            den = take(NT)
            cmp8 = take(NT * E)
            nblk = take(E)
            bend = take(E)
            cmpb = take(NB * E).rearrange("p (b e) -> p b e", b=NB)
            bexpf = take(NB)
            slotf = take(NT)
            psT, psR, psK = banks[0:2], banks[2:4], banks[4]
            src = x if f == 0 else x2d
            r0 = u * UROWS
            rows_in = Arrivals("rows_loaded")
            base = {n: S(n).n for n in ("p_xn", "p_T", "p_hi", "p_lo", "p_R", "p_sc", "p_var", "p_rstd",
                                        "p_m", "p_k", "p_slot", "p_scat", "p_t32")}

            def wait(e, name, k):
                e.wait_ge(S(name).sem, base[name] + k)

            with nc.Block() as blk:
                @blk.sync
                def _(e):
                    for t in range(NT):
                        if t >= 2:
                            wait(e, "p_xn", t - 1)
                        rr = slice(r0 + t * P, r0 + t * P + P)
                        e.dma_start(xr[t % 2], src[rr, :]).then_inc(rows_in.sem(t), 16)

                @blk.scalar
                def _(e):
                    for t in range(NT):
                        b = psT[t % 2]
                        tt = slice(t * P, t * P + P)
                        wait(e, "p_T", t + 1)
                        if t >= 2:
                            wait(e, "p_R", t - 1)
                        e.activation(xT32[t % 2], b[:], ACT.Copy).then_inc(S("p_t32").sem, 1)
                        e.activation(xT[:, 0, :, tt], b[:].rearrange("p (c r) -> p c r", c=NDC),
                                     ACT.Copy).then_inc(S("p_hi").sem, 1)
                        wait(e, "p_R", t + 1)
                        e.activation(scores[:, t, :], psR[t % 2][:, 0:E], ACT.Sigmoid).then_inc(S("p_sc").sem, 1)

                @blk.gpsimd
                def _(e):
                    for t in range(NT):
                        wait(e, "p_var", t + 1)
                        e.tensor_tensor(rstd[:, t % 2, :], mv[:, t % 2, 1:2], nhalf[:, 0:1],
                                        ALU.pow).then_inc(S("p_rstd").sem, 1)
                    wait(e, "p_slot", 1)
                    for k in range(2):
                        for t in range(NT):
                            e.indirect_dma_start(out=sorted_x,
                                                 out_offset=bass.IndirectOffsetOnAxis(ap=slots[:, k, t:t + 1], axis=0),
                                                 in_=xn[:, t, :], in_offset=None).then_inc(S("p_scat").sem, 16)
                    wait(e, "p_scat", 32 * NT)

                @blk.tensor
                def _(e):
                    for t in range(NT):
                        wait(e, "p_xn", t + 1)
                        if t >= 2:
                            wait(e, "p_hi", t - 1)
                            wait(e, "p_lo", t - 1)
                        for c in range(NDC):
                            m = e.transpose(psT[t % 2][:, c * P:(c + 1) * P], xn[:, t, c * P:(c + 1) * P], ident[:])
                        m.then_inc(S("p_T").sem, 1)
                        wait(e, "p_t32", t + 1)
                        if t >= 2:
                            wait(e, "p_sc", t - 1)
                        for c in range(NDC):
                            m = e.matmul(psR[t % 2][:, 0:E], xT32[t % 2][:, c * P:(c + 1) * P], rw[:, c, :],
                                         start=(c == 0), stop=(c == NDC - 1))
                        m.then_inc(S("p_R").sem, 1)
                    wait(e, "p_m", 1)
                    e.matmul(psK[:, 0:NT * E], tri[:], msum.rearrange("p t e -> p (t e)"), start=True, stop=True)
                    e.matmul(psK[:, NT * E:2 * NT * E], ones[:], msum.rearrange("p t e -> p (t e)"), start=True,
                             stop=True, skip_group_check=True).then_inc(S("p_k").sem, 1)

                @blk.vector
                def _(e):
                    o = Own(e, own["dve"])
                    for t in range(NT):
                        xx = xr[t % 2]
                        rows_in.wait(e, t)
                        o.do(e.bn_stats(stats[:, t % 2, :], xx))
                        o.sync()
                        o.do(e.bn_aggr(mv[:, t % 2, :], stats[:, t % 2, :]))
                        o.sync()
                        e.tensor_scalar(mv[:, t % 2, 1:2], mv[:, t % 2, 1:2], EPS, None,
                                        ALU.add).then_inc(S("p_var").sem, 1)
                        wait(e, "p_rstd", t + 1)
                        e.tensor_scalar(xn[:, t, :], xx, mv[:, t % 2, 0:1], rstd[:, t % 2, :],
                                        ALU.subtract, ALU.mult).then_inc(S("p_xn").sem, 1)
                        wait(e, "p_hi", t + 1)
                        tt = slice(t * P, t * P + P)
                        e.tensor_tensor(xT[:, 1, :, tt], psT[t % 2][:].rearrange("p (c r) -> p c r", c=NDC),
                                        xT[:, 0, :, tt], ALU.subtract).then_inc(S("p_lo").sem, 1)
                    wait(e, "p_sc", NT)
                    big = [P, NT, E]

                    def over_e(a):
                        return a[:, None, :].to_broadcast(big)

                    def over_t(a):
                        return a[:, :, None].to_broadcast(big)

                    o.do(e.tensor_tensor(sel, scores[:], over_e(eb[:]), ALU.add))
                    o.sync()
                    cur = sel
                    for k in range(2):
                        o.do(e.tensor_reduce(mx, cur, AX.X, ALU.max))
                        o.sync()
                        o.do(e.tensor_tensor(eq, cur, over_t(mx), ALU.is_ge))
                        o.sync()
                        o.do(e.tensor_tensor(eq, eq, over_e(iota8[:]), ALU.mult))
                        o.sync()
                        o.do(e.tensor_reduce(mn, eq, AX.X, ALU.min))
                        o.sync()
                        o.do(e.tensor_tensor(oh[k], over_e(iota8[:]), over_t(mn), ALU.is_equal))
                        o.sync()
                        o.do(e.tensor_tensor(eq, oh[k], scores[:], ALU.mult))
                        o.sync()
                        o.do(e.tensor_reduce(wsel[k], eq, AX.X, ALU.add))
                        if k == 0:
                            o.do(e.tensor_scalar(sel2, oh[0], -1e30, None, ALU.mult))
                            o.sync()
                            o.do(e.tensor_tensor(sel2, sel2, sel, ALU.add))
                            cur = sel2
                        o.sync()
                    e.tensor_tensor(msum, oh[0], oh[1], ALU.add).then_inc(S("p_m").sem, 1)
                    o.do(e.tensor_tensor(den, wsel[0], wsel[1], ALU.add))
                    o.sync()
                    o.do(e.tensor_scalar(den, den, 1e-9, None, ALU.add))
                    o.sync()
                    o.do(e.reciprocal(den, den))
                    o.sync()
                    for k in range(2):
                        o.do(e.tensor_tensor(coef[:, k, :], wsel[k], den, ALU.mult))
                    wait(e, "p_k", 1)
                    tot = psK[:, NT * E:2 * NT * E].rearrange("p (t e) -> p t e", t=NT)
                    o.do(e.memset(tp[:, 0, :], 0.0))
                    o.sync()
                    for t in range(NT):
                        o.do(e.tensor_tensor(tp[:, t + 1, :], tp[:, t, :], tot[:, t, :], ALU.add))
                        o.sync()
                    c8 = cmp8.rearrange("p (e k) -> p e k", e=E)
                    o.do(e.tensor_tensor(c8, tp[:, NT, :][:, :, None].to_broadcast([P, E, NT]),
                                         steps8[:][:, None, :].to_broadcast([P, E, NT]), ALU.is_gt))
                    o.sync()
                    o.do(e.tensor_reduce(nblk, c8, AX.X, ALU.add))
                    o.sync()
                    o.do(e.tensor_copy(bend[:, 0:1], nblk[:, 0:1]))
                    o.sync()
                    for k in range(1, E):
                        o.do(e.tensor_tensor(bend[:, k:k + 1], bend[:, k - 1:k], nblk[:, k:k + 1], ALU.add))
                        o.sync()
                    o.do(e.tensor_tensor(cmpb, bidx[:][:, :, None].to_broadcast([P, NB, E]),
                                         bend[:, None, :].to_broadcast([P, NB, E]), ALU.is_ge))
                    o.sync()
                    o.do(e.tensor_reduce(bexpf, cmpb, AX.X, ALU.add))
                    o.sync()
                    o.do(e.tensor_scalar(bexp[:], bexpf, float(E - 1), None, ALU.min))
                    o.do(e.tensor_tensor(nblk, bend, nblk, ALU.subtract))
                    o.sync()
                    o.do(e.tensor_scalar(nblk, nblk, float(P), None, ALU.mult))
                    o.do(e.tensor_tensor(rank, tp[:, 0:NT, :], psK[:, 0:NT * E].rearrange("p (t e) -> p t e", t=NT),
                                         ALU.add))
                    o.sync()
                    o.do(e.tensor_tensor(rank, rank, over_e(nblk), ALU.add))
                    o.sync()
                    for k in range(2):
                        o.do(e.tensor_tensor(eq, oh[k], rank, ALU.mult))
                        o.sync()
                        o.do(e.tensor_reduce(slotf, eq, AX.X, ALU.add))
                        o.sync()
                        o.do(e.tensor_copy(slots[:, k, :], slotf))
                        o.sync()
                    e.engine_nop().then_inc(S("p_slot").sem, 1)
                    own["dve"].n += o.k
            rows_in.end(NT)
            for n, k in (("p_xn", NT), ("p_T", NT), ("p_hi", NT), ("p_lo", NT), ("p_R", NT),
                         ("p_sc", NT), ("p_var", NT), ("p_rstd", NT), ("p_m", 1), ("p_k", 1), ("p_slot", 1),
                         ("p_scat", 32 * NT), ("p_t32", NT)):
                S(n).n += k

        def add_attention(u):
            reg_at[0] = 0
            a = [take(D) for _ in range(2)]
            b = [take(D) for _ in range(2)]
            ld, st, d0 = Arrivals("rows_loaded", 2), Arrivals("rows_stored"), S("a_add").n
            with nc.Block() as blk:
                @blk.sync
                def _(e):
                    for t in range(NT):
                        rr = slice(u * UROWS + t * P, u * UROWS + t * P + P)
                        if t >= 2:
                            st.wait(e, t - 2)
                        e.dma_start(a[t % 2], x1d[rr, :]).then_inc(ld.sem(t), 16)
                        e.dma_start(b[t % 2], attd[rr, :]).then_inc(ld.sem(t), 16)
                    st.wait(e, NT - 2)
                    st.wait(e, NT - 1)

                @blk.vector
                def _(e):
                    for t in range(NT):
                        ld.wait(e, t)
                        e.tensor_tensor(a[t % 2], a[t % 2], b[t % 2], ALU.add).then_inc(S("a_add").sem, 1)

                @blk.scalar
                def _(e):
                    for t in range(NT):
                        rr = slice(u * UROWS + t * P, u * UROWS + t * P + P)
                        e.wait_ge(S("a_add").sem, d0 + t + 1)
                        e.dma_start(x2d[rr, :], a[t % 2]).then_inc(st.sem(t), 16)
            ld.end(NT)
            st.end(NT)
            S("a_add").n += NT

        def shared(f, u):
            reg_at[0] = 0
            sg = [take(HALF) for _ in range(2)]
            hf = [take(HALF) for _ in range(2)]
            psG, psU, psD = banks[0:2], banks[2:4], banks[4:6]
            NSLOT = NU * 2 * KT
            chunk_in = Arrivals("chunk_loaded")
            base = {n: S(n).n for n in ("h_g", "h_u", "h_silu", "h_mul", "h_hi", "h_lo", "h_d", "h_acc")}

            def wait(e, name, k):
                e.wait_ge(S(name).sem, base[name] + k)

            with nc.Block() as blk:
                @blk.sync
                def _(e):
                    for n in range(NU):
                        if n >= 2:
                            wait(e, "h_d", 8 * (n - 1))
                        e.dma_start(wb[:, n % 2].rearrange("p a w -> p (a w)"), wsplit[n]).then_inc(
                            chunk_in.sem(n), 16)

                @blk.tensor
                def _(e):
                    passes = ((0, 0), (0, 1), (1, 0))

                    def up(j, reg, par):
                        hg, half, k = (j // 4) % 2, (j // 2) % 2, j % 2
                        if j >= 2 or reg is not None:
                            n = j - 1
                            wait(e, "h_mul", n if reg is None else reg * 8 + n)
                        for gu, ps, name in ((0, psG, "h_g"), (1, psU, "h_u")):
                            i = 0
                            for c in range(NDC):
                                for wp, xp in passes:
                                    o = gu * NDC * HC + c * HC + k * P
                                    m = e.matmul(ps[j % 2][:], wb[:, hg, wp, o:o + P],
                                                 xT[:, xp, c, half * HALF:(half + 1) * HALF],
                                                 start=(i == 0), stop=(i == 3 * NDC - 1))
                                    i += 1
                            m.then_inc(S(name).sem, 1)

                    def down(g, tt, reg):
                        n = 4 * g + tt - 1
                        if n > 0 or reg is not None:
                            wait(e, "h_acc", n if reg is None else reg * 16 + n)
                        i = 0
                        for kt in range(KT):
                            for wp, hp in passes:
                                o = W3OFF + kt * D
                                m = e.matmul(psD[tt % 2][:], hs[:, g % 2, hp, kt, tt * P:(tt + 1) * P],
                                             wb[:, (g // 2) % 2, wp, o:o + D], start=(i == 0), stop=(i == 5))
                                i += 1
                        m.then_inc(S("h_d").sem, 1)

                    def slot(j, reg):
                        if j % 4 == 0:
                            chunk_in.wait(e, j // 4, reg)
                        up(j, reg, None)
                        g = j // 2 - 1
                        if g >= 0:
                            if j % 2 == 0:
                                n = 2 * g + 2
                                wait(e, "h_lo", n if reg is None else reg * 8 + n)
                            down(g, 2 * (j % 2), reg)
                            down(g, 2 * (j % 2) + 1, reg)

                    def slots_of(j0, n, reg):
                        for j in range(j0, j0 + n):
                            slot(j, reg)

                    slots_of(0, 8, None)
                    with e.Fori(0, NSLOT // 8 - 1) as r:
                        slots_of(8, 8, r)
                    wait(e, "h_lo", NSLOT)
                    for tt in range(4):
                        g = NSLOT // 2 - 1
                        down(g, tt, None)

                @blk.scalar
                def _(e):
                    def slot(j, r):
                        def at(n):
                            return n if r is None else r * 8 + n
                        wait(e, "h_g", at(j + 1))
                        if j >= 2:
                            wait(e, "h_mul", at(j - 1))
                        e.activation(sg[j % 2], psG[j % 2][:], ACT.Silu).then_inc(S("h_silu").sem, 1)
                        wait(e, "h_mul", at(j + 1))
                        if j >= 4:
                            n = 4 * (j // 2 - 1)
                            wait(e, "h_d", n if r is None else r * 16 + n)
                        e.activation(hs[:, (j // 2) % 2, 0, j % 2, :], hf[j % 2], ACT.Copy).then_inc(S("h_hi").sem, 1)

                    for j in range(8):
                        slot(j, None)
                    with e.Fori(0, NSLOT // 8 - 1) as r:
                        for j in range(8, 16):
                            slot(j, r)

                @blk.gpsimd
                def _(e):
                    def slot(j, r):
                        wait(e, "h_hi", (j + 1) if r is None else r * 8 + (j + 1))
                        e.tensor_tensor(hs[:, (j // 2) % 2, 1, j % 2, :], hf[j % 2],
                                        hs[:, (j // 2) % 2, 0, j % 2, :], ALU.subtract).then_inc(S("h_lo").sem, 1)

                    for j in range(8):
                        slot(j, None)
                    with e.Fori(0, NSLOT // 8 - 1) as r:
                        for j in range(8, 16):
                            slot(j, r)

                @blk.vector
                def _(e):
                    def slot(j, r, first):
                        def at(n):
                            return n if r is None else r * 8 + n
                        wait(e, "h_silu", at(j + 1))
                        wait(e, "h_u", at(j + 1))
                        if j >= 2:
                            wait(e, "h_lo", at(j - 1))
                        e.tensor_tensor(hf[j % 2], psU[j % 2][:], sg[j % 2], ALU.mult).then_inc(S("h_mul").sem, 1)
                        if j >= 2:
                            g = j // 2 - 1
                            for tt in (2 * (j % 2), 2 * (j % 2) + 1):
                                evac(g, tt, r, first)

                    def evac(g, tt, r, first):
                        half = g % 2
                        n = 4 * g + tt + 1
                        wait(e, "h_d", n if r is None else r * 16 + n)
                        a = acc[:, half * TH + tt, :]
                        if first:
                            e.tensor_copy(a, psD[tt % 2][:]).then_inc(S("h_acc").sem, 1)
                        else:
                            n = 4 * (g - 2) + tt + 1
                            wait(e, "h_acc", n if r is None else r * 16 + n)
                            e.tensor_tensor(a, psD[tt % 2][:], a, ALU.add).then_inc(S("h_acc").sem, 1)

                    for j in range(8):
                        slot(j, None, j // 2 - 1 < 2)
                    with e.Fori(0, NSLOT // 8 - 1) as r:
                        for j in range(8, 16):
                            slot(j, r, False)
                    for tt in range(4):
                        evac(NSLOT // 2 - 1, tt, None, False)
            chunk_in.end(NU)
            for n, k in (("h_g", NSLOT), ("h_u", NSLOT), ("h_silu", NSLOT), ("h_mul", NSLOT),
                         ("h_hi", NSLOT), ("h_lo", NSLOT), ("h_d", 2 * NSLOT), ("h_acc", 2 * NSLOT)):
                S(n).n += k

        def routed():
            reg_at[0] = 0
            xs = [take(D) for _ in range(2)]
            xsT = [take(D, BF16).rearrange("p (a n) -> p a n", a=2) for _ in range(2)]
            sg = [take(HC) for _ in range(2)]
            hf = [take(HC) for _ in range(2)]
            hb = [take(HC, BF16).rearrange("p (a n) -> p a n", a=2) for _ in range(2)]
            hT = [take(HC, BF16).rearrange("p (a k n) -> p a k n", a=2, k=KT) for _ in range(2)]
            yo = [take(D) for _ in range(2)]
            psX, psH, psY = banks[0:2], banks[2:4], banks[6:8]
            psHT = [banks[4 + k][:].bitcast(BF16)[:, 0:2 * HC] for k in range(2)]
            passes = ((0, 0), (0, 1), (1, 0))
            rows_in, rows_out = Arrivals("rows_loaded"), Arrivals("rows_stored")
            names = ("r_T", "r_hi", "r_lo", "r_h", "r_silu", "r_mul", "r_hbh", "r_hbl", "r_HT", "r_hT", "r_y",
                     "r_yo")
            base = {n: S(n).n for n in names}

            def wait(e, name, k, i=None, per=2):
                e.wait_ge(S(name).sem, base[name] + k if i is None else i * per + (base[name] + k))

            with nc.Block() as blk:
                @blk.sync
                def _(e):
                    def load(k, i):
                        row = k * P if i is None else i * (2 * P) + k * P
                        if i is not None or k >= 2:
                            wait(e, "r_T", k - 1, i)
                        e.dma_start(xs[k % 2], sorted_x[bass.ds(row, P), :]).then_inc(
                            rows_in.sem(k), 16)

                    def store(k, i):
                        row = k * P if i is None else i * (2 * P) + k * P
                        wait(e, "r_yo", k + 1, i)
                        e.dma_start(sorted_y[bass.ds(row, P), :], yo[k % 2]).then_inc(
                            rows_out.sem(k), 16)

                    load(0, None)
                    load(1, None)
                    with e.Fori(0, NB // 2) as i:
                        load(2, i)
                        store(0, i)
                        load(3, i)
                        store(1, i)
                    store(NB - 1, None)
                    rows_out.wait(e, NB - 2)
                    rows_out.wait(e, NB - 1)

                @blk.tensor
                def _(e):
                    def rows_T(k, i):
                        rows_in.wait(e, k, i)
                        if i is not None or k >= 2:
                            wait(e, "r_lo", k - 1, i)
                        for c in range(NDC):
                            m = e.transpose(psX[k % 2][:, c * P:(c + 1) * P], xs[k % 2][:, c * P:(c + 1) * P],
                                            ident[:])
                        m.then_inc(S("r_T").sem, 1)

                    def expert(k, i):
                        col = k if i is None else i * 2 + k
                        return e.value_load(bexp[0:1, bass.ds(col, 1)], min_val=0, max_val=E - 1)

                    def weights(ex, wp, o):
                        return wr[:, bass.ds(ex, 1), wp, o:o + D].rearrange("p o n -> p (o n)")

                    def up(k, i):
                        ex = expert(k, i)
                        wait(e, "r_lo", k + 1, i)
                        if i is not None or k >= 2:
                            wait(e, "r_mul", k - 1, i)
                        n = 0
                        for c in range(NDC):
                            for wp, xp in passes:
                                m = e.matmul(psH[k % 2][:], xsT[k % 2][:, xp, c * P:(c + 1) * P],
                                             weights(ex, wp, c * D), start=(n == 0), stop=(n == 3 * NDC - 1))
                                n += 1
                        m.then_inc(S("r_h").sem, 1)

                    def hidden_T(k, i):
                        wait(e, "r_hbl", k + 1, i)
                        if i is not None or k >= 2:
                            wait(e, "r_hT", k - 1, i)
                        for a in range(2):
                            for kt in range(KT):
                                n = a * KT + kt
                                m = e.transpose(psHT[k % 2][:, n * P:(n + 1) * P],
                                                hb[k % 2][:, a, kt * P:(kt + 1) * P], identb[:])
                        m.then_inc(S("r_HT").sem, 1)

                    def down(k, i):
                        ex = expert(k, i)
                        wait(e, "r_hT", k + 1, i)
                        if i is not None or k >= 2:
                            wait(e, "r_yo", k - 1, i)
                        n = 0
                        for kt in range(KT):
                            for wp, hp in passes:
                                m = e.matmul(psY[k % 2][:], hT[k % 2][:, hp, kt, :],
                                             weights(ex, wp, W3OFF + kt * D), start=(n == 0), stop=(n == 3 * KT - 1))
                                n += 1
                        m.then_inc(S("r_y").sem, 1)

                    rows_T(0, None)
                    rows_T(1, None)
                    up(0, None)
                    rows_T(2, None)
                    hidden_T(0, None)
                    up(1, None)
                    down(0, None)
                    rows_T(3, None)
                    hidden_T(1, None)
                    up(2, None)
                    down(1, None)
                    with e.Fori(0, NB // 2 - 1) as i:
                        for k in (3, 4):
                            rows_T(k + 1, i)
                            hidden_T(k - 1, i)
                            up(k, i)
                            down(k - 1, i)
                    hidden_T(NB - 1, None)
                    down(NB - 1, None)

                def engine_loop(e, body):
                    for k in range(3):
                        body(k, None)
                    with e.Fori(0, NB // 2 - 1) as i:
                        for k in (3, 4):
                            body(k, i)

                @blk.scalar
                def _(e):
                    def rows_hi(k, i):
                        wait(e, "r_T", k + 1, i)
                        if i is not None or k >= 2:
                            wait(e, "r_h", k - 1, i)
                        e.activation(xsT[k % 2][:, 0, :], psX[k % 2][:], ACT.Copy).then_inc(S("r_hi").sem, 1)

                    def hidden(k, i):
                        wait(e, "r_h", k + 1, i)
                        if i is not None or k >= 2:
                            wait(e, "r_mul", k - 1, i)
                        e.activation(sg[k % 2], psH[k % 2][:, 0:HC], ACT.Silu).then_inc(S("r_silu").sem, 1)
                        wait(e, "r_mul", k + 1, i)
                        if i is not None or k >= 2:
                            wait(e, "r_HT", k - 1, i)
                        e.activation(hb[k % 2][:, 0, :], hf[k % 2], ACT.Copy).then_inc(S("r_hbh").sem, 1)

                    def result(k, i):
                        wait(e, "r_y", k + 1, i)
                        if i is not None or k >= 2:
                            rows_out.wait(e, k - 2, i)
                        e.activation(yo[k % 2], psY[k % 2][:], ACT.Copy).then_inc(S("r_yo").sem, 1)

                    rows_hi(0, None)
                    for k in range(3):
                        rows_hi(k + 1, None)
                        hidden(k, None)
                        if k:
                            result(k - 1, None)
                    with e.Fori(0, NB // 2 - 1) as i:
                        for k in (3, 4):
                            rows_hi(k + 1, i)
                            hidden(k, i)
                            result(k - 1, i)
                    result(NB - 1, None)

                @blk.vector
                def _(e):
                    def rows_lo(k, i):
                        wait(e, "r_hi", k + 1, i)
                        e.tensor_tensor(xsT[k % 2][:, 1, :], psX[k % 2][:], xsT[k % 2][:, 0, :],
                                        ALU.subtract).then_inc(S("r_lo").sem, 1)

                    def hidden(k, i):
                        wait(e, "r_silu", k + 1, i)
                        if i is not None or k >= 2:
                            wait(e, "r_hbl", k - 1, i)
                        e.tensor_tensor(hf[k % 2], psH[k % 2][:, HC:2 * HC], sg[k % 2], ALU.mult).then_inc(
                            S("r_mul").sem, 1)
                        wait(e, "r_hbh", k + 1, i)
                        e.tensor_tensor(hb[k % 2][:, 1, :], hf[k % 2], hb[k % 2][:, 0, :],
                                        ALU.subtract).then_inc(S("r_hbl").sem, 1)

                    def hidden_T(k, i):
                        wait(e, "r_HT", k + 1, i)
                        if i is not None or k >= 2:
                            wait(e, "r_y", k - 1, i)
                        e.tensor_copy(hT[k % 2].rearrange("p a k n -> p (a k n)"), psHT[k % 2]).then_inc(
                            S("r_hT").sem, 1)

                    rows_lo(0, None)
                    for k in range(3):
                        rows_lo(k + 1, None)
                        if k:
                            hidden_T(k - 1, None)
                        hidden(k, None)
                    with e.Fori(0, NB // 2 - 1) as i:
                        for k in (3, 4):
                            rows_lo(k + 1, i)
                            hidden_T(k - 1, i)
                            hidden(k, i)
                    hidden_T(NB - 1, None)

            for n in names:
                S(n).n += {"r_T": NB + 1, "r_hi": NB + 1, "r_lo": NB + 1}.get(n, NB)
            rows_in.end(NB + 1)
            rows_out.end(NB)

        def finish(f, u):
            reg_at[0] = 0
            y = [[take(D) for _ in range(2)] for _ in range(2)]
            xr = [take(D) for _ in range(2)]
            xo = [take(D) for _ in range(2)]
            ln = [take(D) for _ in range(2)]
            src, dst = (x, x1d) if f == 0 else (x2d, out)
            rows_in, y_in = Arrivals("rows_loaded"), Arrivals("y_gathered", 2)
            rows_out = Arrivals("rows_stored", 1 if f else 2)
            names = ("f_sum", "f_var", "f_rstd", "f_ln")
            base = {n: S(n).n for n in names}

            def wait(e, name, k):
                e.wait_ge(S(name).sem, base[name] + k)

            with nc.Block() as blk:
                @blk.gpsimd
                def _(e):
                    def gather(t):
                        if t >= 2:
                            wait(e, "f_sum", t - 1)
                        for k in range(2):
                            e.indirect_dma_start(out=y[k][t % 2], out_offset=None, in_=sorted_y,
                                                 in_offset=bass.IndirectOffsetOnAxis(ap=slots[:, k, t:t + 1], axis=0)
                                                 ).then_inc(y_in.sem(t), 16)
                    gather(0)
                    for t in range(NT):
                        if t + 1 < NT:
                            gather(t + 1)
                        if f == 0:
                            wait(e, "f_var", t + 1)
                            e.tensor_tensor(rstd[:, t % 2, :], mv[:, t % 2, 1:2], nhalf[:, 0:1],
                                            ALU.pow).then_inc(S("f_rstd").sem, 1)

                @blk.sync
                def _(e):
                    for t in range(NT):
                        rr = slice(u * UROWS + t * P, u * UROWS + (t + 1) * P)
                        if t >= 2:
                            wait(e, "f_sum", t - 1)
                        e.dma_start(xr[t % 2], src[rr, :]).then_inc(rows_in.sem(t), 16)
                    rows_out.wait(e, NT - 2)
                    rows_out.wait(e, NT - 1)

                @blk.scalar
                def _(e):
                    for t in range(NT):
                        rr = slice(u * UROWS + t * P, u * UROWS + (t + 1) * P)
                        wait(e, "f_sum", t + 1)
                        e.dma_start(dst[rr, :], xo[t % 2]).then_inc(rows_out.sem(t), 16)
                        if f == 0:
                            wait(e, "f_ln", t + 1)
                            e.dma_start(xln2[rr, :], ln[t % 2]).then_inc(rows_out.sem(t), 16)

                @blk.vector
                def _(e):
                    o = Own(e, own["dve"])
                    for t in range(NT):
                        y_in.wait(e, t)
                        rows_in.wait(e, t)
                        if t >= 2:
                            rows_out.wait(e, t - 2)
                        a, b = y[0][t % 2], y[1][t % 2]
                        o.do(e.scalar_tensor_tensor(out=a, in0=a, scalar=coef[:, 0, t:t + 1], in1=acc[:, t, :],
                                                    op0=ALU.mult, op1=ALU.add))
                        o.sync()
                        o.do(e.scalar_tensor_tensor(out=b, in0=b, scalar=coef[:, 1, t:t + 1], in1=a,
                                                    op0=ALU.mult, op1=ALU.add))
                        o.sync()
                        e.scalar_tensor_tensor(out=xo[t % 2], in0=b, scalar=0.5, in1=xr[t % 2],
                                               op0=ALU.mult, op1=ALU.add).then_inc(S("f_sum").sem, 1)
                        if f == 0:
                            wait(e, "f_sum", t + 1)
                            o.do(e.bn_stats(stats[:, t % 2, :], xo[t % 2]))
                            o.sync()
                            o.do(e.bn_aggr(mv[:, t % 2, :], stats[:, t % 2, :]))
                            o.sync()
                            e.tensor_scalar(mv[:, t % 2, 1:2], mv[:, t % 2, 1:2], EPS, None,
                                            ALU.add).then_inc(S("f_var").sem, 1)
                            wait(e, "f_rstd", t + 1)
                            e.tensor_scalar(ln[t % 2], xo[t % 2], mv[:, t % 2, 0:1], rstd[:, t % 2, :],
                                            ALU.subtract, ALU.mult).then_inc(S("f_ln").sem, 1)
                    own["dve"].n += o.k
            for n in names:
                S(n).n += NT if n == "f_sum" else NT * (f == 0)
            for a in (rows_in, y_in, rows_out):
                a.end(NT)

        def attention(b):
            reg_at[0] = 0
            tok = take(NTOK * C)
            qkv = take(NTOK * 3 * C)
            sco = take(2 * NW * SP_ * SP_)
            tmp = [tok[:, k * 1024:(k + 1) * 1024] for k in range(2)]
            small = take(2 * NW * SP_)
            small2 = take(NTOK)
            tokT = [acc[:, k, :] for k in range(2)]
            psT, psQ = banks[0:2], banks[2:6]
            img = xln2[b * 512:(b + 1) * 512, :].rearrange("r c -> (r c)").rearrange(
                "(s i g e) -> s g i e", s=16, i=NPI, g=8)
            res = attd[b * 512:(b + 1) * 512, :].rearrange("r c -> (r c)").rearrange(
                "(c s i g j) -> s g c i j", c=C, s=16, i=NPI, g=8)
            q4 = qkv.rearrange("p (i j c) -> p i j c", i=NPI, j=NPJ)
            q3 = qkv.rearrange("p (t c) -> p t c", c=3 * C)
            s5 = sco.rearrange("p (r w a b) -> p r w a b", r=2, w=NW, a=SP_)
            sum3 = sco.rearrange("p (t c) -> p t c", c=C)
            att3 = qkv[:, 0:NTOK * C].rearrange("p (t c) -> p t c", c=C)
            done = qkv[:, 2 * NTOK * C:3 * NTOK * C]
            tok3 = tok.rearrange("p (t c) -> p t c", c=C)
            names = ("t_x", "t_T", "t_Tc", "t_q", "t_qc", "t_s", "t_e", "t_o", "t_cv", "t_lep", "t_oT", "t_oTc", "t_pr",
                     "t_prc", "t_x2", "t_var", "t_rstd", "t_out", "t_st", "t_sum")
            base = {n: S(n).n for n in names}
            tok_free = [0]

            def wait(e, name, k):
                e.wait_ge(S(name).sem, base[name] + k)

            def window(r, lo, n):
                if r == 0:
                    return q3[:, :, lo:lo + n].rearrange("p (w a) c -> p w a c", a=SP_)
                return q4[:, :, :, lo:lo + n].rearrange("p a w c -> p w a c")

            with nc.Block() as blk:
                @blk.sync
                def _(e):
                    def load(name):
                        for s in range(16):
                            e.dma_start(tok[8 * s:8 * s + 8, :].rearrange("p (i e) -> p i e", i=NPI), img[s]).then_inc(
                                S(name).sem, 16)
                    load("t_x")
                    wait(e, "t_o", 1)
                    load("t_x2")
                    wait(e, "t_out", 1)
                    for s in range(16):
                        for c in range(C):
                            e.dma_start(res[s, :, c], done[8 * s:8 * s + 8, c * NTOK:(c + 1) * NTOK].rearrange(
                                "p (i j) -> p i j", i=NPI)).then_inc(S("t_st").sem, 16)
                    wait(e, "t_st", 16 * 16 * C)

                @blk.tensor
                def _(e):
                    wait(e, "t_x", 256)
                    for m in range(4):
                        if m >= 2:
                            wait(e, "t_Tc", m - 1)
                        for n in range(4):
                            g = 4 * m + n
                            mm = e.transpose(psT[m % 2][:, n * P:(n + 1) * P], tok[:, g * P:(g + 1) * P], ident[:])
                        mm.then_inc(S("t_T").sem, 1)
                        wait(e, "t_Tc", m + 1)
                        for n in range(4):
                            g = 4 * m + n
                            if g >= 4:
                                wait(e, "t_qc", g - 3)
                            e.matmul(psQ[g % 4][:, 0:24 * C], tokT[m % 2][:, n * P:(n + 1) * P], wqkv[:],
                                     start=True, stop=True).then_inc(S("t_q").sem, 1)
                    wait(e, "t_sum", 1)
                    for m in range(4):
                        if m >= 2:
                            wait(e, "t_oTc", m - 1)
                        for n in range(4):
                            g = 4 * m + n
                            mm = e.transpose(psT[m % 2][:, n * P:(n + 1) * P], sco[:, g * P:(g + 1) * P], ident[:])
                        mm.then_inc(S("t_oT").sem, 1)
                        wait(e, "t_oTc", m + 1)
                        if m >= 1:
                            wait(e, "t_prc", m)
                        for n in range(4):
                            e.matmul(psQ[0][:, n * P:(n + 1) * P], tokT[m % 2][:, n * P:(n + 1) * P], wproj[:],
                                     start=True, stop=False, skip_group_check=True)
                            mm = e.matmul(psQ[0][:, n * P:(n + 1) * P], ones[0:1, :], pbrow[0:1, :],
                                          start=False, stop=True, skip_group_check=True)
                        mm.then_inc(S("t_pr").sem, 1)

                @blk.scalar
                def _(e):
                    for m in range(4):
                        wait(e, "t_T", m + 1)
                        if m >= 2:
                            wait(e, "t_q", 4 * (m - 1))
                        e.activation(tokT[m % 2], psT[m % 2][:], ACT.Copy).then_inc(S("t_Tc").sem, 1)
                        for n in range(4):
                            g = 4 * m + n
                            wait(e, "t_q", g + 1)
                            e.activation(qkv[:, g * 24 * C:(g + 1) * 24 * C], psQ[g % 4][:, 0:24 * C],
                                         ACT.Copy).then_inc(S("t_qc").sem, 1)
                    wait(e, "t_s", 1)
                    e.activation(sco, sco, ACT.Exp, scale=SCALE).then_inc(S("t_e").sem, 1)
                    for m in range(4):
                        wait(e, "t_oT", m + 1)
                        if m >= 2:
                            wait(e, "t_pr", m - 1)
                        e.activation(tokT[m % 2], psT[m % 2][:], ACT.Copy).then_inc(S("t_oTc").sem, 1)
                        wait(e, "t_pr", m + 1)
                        e.activation(qkv[:, m * 512:(m + 1) * 512], psQ[0][:], ACT.Copy).then_inc(S("t_prc").sem, 1)

                @blk.gpsimd
                def _(e):
                    wait(e, "t_var", 1)
                    e.tensor_tensor(small2, small2, nhalf[:], ALU.pow).then_inc(S("t_rstd").sem, 1)

                @blk.vector
                def _(e):
                    o = Own(e, own["dve"])
                    wait(e, "t_qc", 16)
                    shape = [P, NW, SP_, H]
                    for r in range(2):
                        for a in range(SP_):
                            qa = window(r, H * r, H)[:, :, a:a + 1, :].to_broadcast(shape)
                            kk = window(r, C + H * r, H)
                            t = tmp[a % 2].rearrange("p (w b c) -> p w b c", w=NW, b=SP_)
                            o.do(e.tensor_tensor(t, qa, kk, ALU.mult))
                            o.sync()
                            o.do(e.tensor_reduce(s5[:, r, :, a, :], t, AX.X, ALU.add))
                    o.sync()
                    s3 = sco.rearrange("p (n b) -> p n b", b=SP_)
                    NR = 2 * NW * SP_

                    def rows(v):
                        return v[:, :, None].to_broadcast([P, NR, SP_])

                    o.do(e.tensor_reduce(small, s3, AX.X, ALU.max))
                    o.sync()
                    e.tensor_tensor(s3, s3, rows(small), ALU.subtract).then_inc(S("t_s").sem, 1)
                    k4 = q4[:, :, :, C:2 * C]
                    v4 = q4[:, :, :, 2 * C:3 * C]
                    allc = [P, NTOK, C]
                    k3, v3 = q3[:, :, C:2 * C], q3[:, :, 2 * C:3 * C]
                    o.do(e.tensor_tensor(k3, v3, cw[:, 1:2, :].to_broadcast(allc), ALU.mult))
                    o.sync()
                    o.do(e.tensor_tensor(k3, k3, cb[:][:, None, :].to_broadcast(allc), ALU.add))
                    o.sync()
                    for r in range(2):
                        kw, vw = window(r, C + H * r, H), window(r, 2 * C + H * r, H)
                        for tap, to, of in ((0, slice(1, SP_), slice(0, SP_ - 1)), (2, slice(0, SP_ - 1), slice(1, SP_))):
                            n = SP_ - 1
                            t = tmp[tap // 2][:, 0:NW * n * H].rearrange("p (w b c) -> p w b c", w=NW, b=n)
                            wt = cw[:, tap:tap + 1, H * r:H * r + H][:, None].to_broadcast([P, NW, n, H])
                            o.do(e.tensor_tensor(t, vw[:, :, of, :], wt, ALU.mult))
                            o.sync()
                            o.do(e.tensor_tensor(kw[:, :, to, :], kw[:, :, to, :], t, ALU.add))
                            o.sync()
                    wait(e, "t_e", 1)
                    o.do(e.tensor_reduce(small, s3, AX.X, ALU.add))
                    o.sync()
                    o.do(e.reciprocal(small, small))
                    o.sync()
                    o.do(e.tensor_tensor(s3, s3, rows(small), ALU.mult))
                    o.sync()
                    for r in range(2):
                        for a in range(SP_):
                            pa = s5[:, r, :, a:a + 1, :].to_broadcast(shape)
                            vv = window(r, 2 * C + H * r, H).rearrange("p w b c -> p w c b")
                            t = tmp[a % 2].rearrange("p (w c b) -> p w c b", w=NW, c=H)
                            o.do(e.tensor_tensor(t, pa, vv, ALU.mult))
                            o.sync()
                            o.do(e.tensor_reduce(window(r, H * r, H)[:, :, a, :], t, AX.X, ALU.add))
                    o.sync()
                    e.tensor_tensor(sum3, q3[:, :, 0:C], k3, ALU.add).then_inc(S("t_sum").sem, 1)
                    e.engine_nop().then_inc(S("t_o").sem, 1)
                    wait(e, "t_prc", 4)
                    tk = [P, NTOK, C]

                    def per_tok(v):
                        return v[:, :, None].to_broadcast(tk)

                    def per_ch(v):
                        return v[:][:, None, :].to_broadcast(tk)
                    mean = small[:, 0:NTOK]
                    sq = qkv[:, NTOK * C:2 * NTOK * C].rearrange("p (t c) -> p t c", c=C)
                    o.do(e.tensor_reduce(mean, att3, AX.X, ALU.add))
                    o.sync()
                    o.do(e.tensor_scalar(mean, mean, 1.0 / C, None, ALU.mult))
                    o.sync()
                    o.do(e.tensor_tensor(att3, att3, per_tok(mean), ALU.subtract))
                    o.sync()
                    o.do(e.tensor_tensor(sq, att3, att3, ALU.mult))
                    o.sync()
                    o.do(e.tensor_reduce(small2, sq, AX.X, ALU.add))
                    o.sync()
                    e.tensor_scalar(small2, small2, 1.0 / C, EPS, ALU.mult, ALU.add).then_inc(S("t_var").sem, 1)
                    wait(e, "t_rstd", 1)
                    o.do(e.tensor_tensor(att3, att3, per_tok(small2), ALU.mult))
                    o.sync()
                    o.do(e.tensor_tensor(att3, att3, per_ch(lw), ALU.mult))
                    o.sync()
                    o.do(e.tensor_tensor(att3, att3, per_ch(lb), ALU.add))
                    o.sync()
                    wait(e, "t_x2", 256)
                    e.tensor_tensor(done.rearrange("p (c t) -> p t c", c=C), att3, tok3,
                                    ALU.add).then_inc(S("t_out").sem, 1)
                    own["dve"].n += o.k
            for n in names:
                S(n).n += {"t_x": 256, "t_x2": 256, "t_T": 4, "t_Tc": 4, "t_q": 16, "t_qc": 16, "t_oT": 4, "t_oTc": 4,
                           "t_pr": 4, "t_prc": 4, "t_st": 256 * C, "t_cv": 0, "t_lep": 0}.get(n, 1)

        for u in range(2):
            prepare(0, u)
            shared(0, u)
            routed()
            finish(0, u)
        for b in range(NIMG):
            attention(b)
        for u in range(2):
            add_attention(u)
            prepare(1, u)
            shared(1, u)
            routed()
            finish(1, u)


def kernel(L0_attn_x, L0_attn_qkv_w, L0_attn_conv_w0, L0_attn_conv_b0, L0_attn_conv_w1, L0_attn_conv_b1, L0_attn_proj_w,
           L0_attn_proj_b, L0_attn_ln_w, L0_attn_ln_b, L0_ffn_w12, L0_ffn_w3, L0_ffn_router_w, L0_ffn_expert_bias,
           L0_ffn_sw1, L0_ffn_sw2, L0_ffn_sw3):
    import numpy as np
    import concourse.bacc as bacc
    from concourse.bass_utils import run_bass_kernel_spmd

    A = np.asarray
    B, R, D = L0_attn_x.shape
    E = L0_ffn_w12.shape[0]
    NU = L0_ffn_sw1.shape[0] // 256

    def up_words(w, n):
        w = A(w).reshape(n, -1, D // P, P)
        return w.transpose(0, 3, 2, 1).reshape(n, P, -1)

    def down_words(w, n):
        w = w.reshape(n, D, 2, P)
        return w.transpose(0, 3, 2, 1).reshape(n, P, -1)

    sw3 = A(L0_ffn_sw3).reshape(D, NU, 256).transpose(1, 0, 2)
    arrays = {
        "x": A(L0_attn_x).reshape(B * R, D),
        "wsh": np.concatenate([up_words(L0_ffn_sw1, NU), up_words(L0_ffn_sw2, NU), down_words(sw3, NU)], 2),
        "wrt": np.concatenate([up_words(L0_ffn_w12, E), down_words(A(L0_ffn_w3), E)], 2),
        "rwT": A(L0_ffn_router_w).T,
        "ebias": A(L0_ffn_expert_bias),
        "qkvw": A(L0_attn_qkv_w),
        "projw": A(L0_attn_proj_w),
        "projb": A(L0_attn_proj_b),
        "convw": np.concatenate([A(L0_attn_conv_w0)[:, 0, 1, :].T, A(L0_attn_conv_w1)[:, 0, :, 1].T], 1),
        "convb": np.concatenate([A(L0_attn_conv_b0), A(L0_attn_conv_b1)]),
        "lnw": A(L0_attn_ln_w),
        "lnb": A(L0_attn_ln_b),
    }
    nc = bacc.Bacc("TRN2", target_bir_lowering=False, num_devices=1)
    arrays = {n: np.ascontiguousarray(a) for n, a in arrays.items()}
    aps = [nc.dram_tensor(n, a.shape, mybir.dt.from_np(a.dtype), kind="ExternalInput").ap() for n, a in arrays.items()]
    out = nc.dram_tensor("out", [B * R, D], F32, kind="ExternalOutput").ap()
    macaron(nc, *aps, out)
    got = run_bass_kernel_spmd(nc, [arrays], core_ids=[0])
    return got.results[0]["out"].reshape(B, R, D)
```

```python
from contextlib import ExitStack

import concourse.bass as bass
from concourse import mybir

ALU = mybir.AluOpType
ACT = mybir.ActivationFunctionType
AX = mybir.AxisListType
F32 = mybir.dt.float32
BF16 = mybir.dt.bfloat16
I32 = mybir.dt.int32

P = 128
EPS = 1e-5


class Count:

    def __init__(self, sem):
        self.sem = sem
        self.n = 0


class Own:

    def __init__(self, eng, count):
        self.eng, self.c, self.reg, self.k = eng, count, None, 0

    def do(self, ins):
        ins.then_inc(self.c.sem, 1)
        self.k += 1
        return ins

    def value(self):
        return self.c.n + self.k if self.reg is None else self.reg + (self.c.n + self.k)

    def sync(self):
        if self.reg is None and self.c.n + self.k == 0:
            return
        self.eng.wait_ge(self.c.sem, self.value())

    def loop(self, count, per_turn, body):
        self.c.n += self.k
        self.k = 0
        with self.eng.Fori(0, count) as i:
            self.reg = i * per_turn
            body(i)
            assert self.k == per_turn, (self.k, per_turn)
        self.reg, self.k = None, 0
        self.c.n += count * per_turn


def macaron(nc, x, wall, rwT, ebias, qkvw, projw, projb, convw, convb, lnw, lnb, out):
    ROWS, D = x.shape
    NDC = D // P
    E = rwT.shape[1]
    NU = (wall.shape[0] - 1) // 2
    WW = wall.shape[2]
    HC = 256
    KT = HC // P
    UROWS = 1024
    NT = UROWS // P
    HALF = 512
    TH = HALF // P
    NB = (2 * UROWS + E * (P - 1)) // P
    C = qkvw.shape[0]
    H = C // 2
    WL = 8
    NPI = 8
    NPJ = 16
    NTOK = NPI * NPJ
    NW = NTOK // WL
    SCALE = float(H) ** -0.5
    W3OFF = 2 * NDC * HC
    PASSES = ((0, 0), (0, 1), (1, 0))
    TURN = 8
    NSLOT = NU * 2 * KT
    assert W3OFF + KT * D == WW and NB == 23 and NSLOT == 32 and NU == E

    x1d = nc.dram_tensor("x1d", [ROWS, D], F32).ap()
    xln2 = nc.dram_tensor("xln2", [ROWS, D], F32).ap()
    attd = nc.dram_tensor("attd", [ROWS, D], F32).ap()
    x2d = nc.dram_tensor("x2d", [ROWS, D], F32).ap()
    sorted_x = [nc.dram_tensor(f"sorted_x{q}", [(NB + 1) * P, D], F32).ap() for q in range(2)]
    sorted_y = nc.dram_tensor("sorted_y", [NB * P, D], F32).ap()
    wsplit = nc.dram_tensor("wsplit", [NU + 1, P, 2 * WW], BF16).ap()

    ctx = ExitStack()
    with ctx:
        def sb(name, shape, dt=F32):
            return ctx.enter_context(nc.sbuf_tensor(name, shape, dt))

        def counter(name):
            return Count(ctx.enter_context(nc.semaphore(name)))

        banks = [ctx.enter_context(nc.psum_tensor(f"bank{i}", [P, 512], F32)) for i in range(8)]

        wr = sb("wr", [P, E, 2, WW], BF16)
        wb = sb("wb", [P, 2, 2, WW], BF16)
        acc = sb("acc", [P, NT, D])
        xT = sb("xT", [P, 2, NDC, UROWS], BF16)
        hs = sb("hs", [P, 2, 2, KT, HALF], BF16)
        TOKW, QKVW = NTOK * C, 3 * NTOK * C
        SMALL = 2 * NW * WL + NTOK
        region = sb("region", [P, 2 * TOKW + QKVW + SMALL + 2 * HALF])
        R_XN, R_QKV, R_SMALL, R_SGH = 0, 2 * TOKW, 2 * TOKW + QKVW, 2 * TOKW + QKVW + SMALL
        ident = sb("ident", [P, P])
        identb = sb("identb", [P, P], BF16)
        tri = sb("tri", [P, P])
        ones = sb("ones", [P, P])
        ones3 = sb("ones3", [3, P], BF16)
        rw = sb("rw", [P, NDC, E])
        eb = sb("eb", [P, E])
        iota8 = sb("iota8", [P, E])
        steps8 = sb("steps8", [P, NT])
        bidx = sb("bidx", [P, NB])
        wqkv = sb("wqkv", [P, 8 * 3 * C])
        wproj = sb("wproj", [P, 8, 2, C])
        bias3 = sb("bias3", [3, 4 * P], BF16)
        cw = sb("cw", [P, 3, C])
        lw = sb("lw", [P, C])
        lb = sb("lb", [P, C])
        nhalf = sb("nhalf", [P, NTOK])
        mv = sb("mv", [P, 2, 2])
        rstd = sb("rstd", [P, 2, 1])
        stats = sb("stats", [P, 2, 6])
        carrier = sb("carrier", [P, 1])
        scores = sb("scores", [P, NT, E])
        coef = sb("coef", [P, 2, 2, NT])
        slots = sb("slots", [P, 2, 2, NT], I32)
        bexp = sb("bexp", [P, 2, NB], I32)

        own = {n: counter(f"own_{n}") for n in ("dve", "act", "pool")}
        sems = {}

        def S(name):
            if name not in sems:
                sems[name] = counter(name)
            return sems[name]

        class Arrivals:

            def __init__(self, name, per=1, ways=2):
                self.all = [S(f"{name}_{q}") for q in range(ways)]
                self.ways, self.per = ways, 16 * per
                self.base = [c.n for c in self.all]

            def sem(self, k):
                return self.all[k % self.ways].sem

            def wait(self, e, k, i=None, step=2):
                n = self.base[k % self.ways] + self.per * (k // self.ways + 1)
                e.wait_ge(self.sem(k), n if i is None else i * (self.per * step // self.ways) + n)

            def wait_last(self, e, items):
                for k in range(max(0, items - self.ways), items):
                    self.wait(e, k)

            def end(self, items):
                for q in range(self.ways):
                    self.all[q].n += self.per * ((items + self.ways - 1 - q) // self.ways)

        class Stage:

            def __init__(self, **adds):
                self.base = {n: S(n).n for n in adds}
                self.adds = adds

            def sem(self, name):
                return S(name).sem

            def wait(self, e, name, k, i=None, per=2):
                n = self.base[name] + k
                e.wait_ge(S(name).sem, n if i is None else i * per + n)

            def end(self):
                for n, k in self.adds.items():
                    S(n).n += k

        hs_words = hs[:].rearrange("p a b c d -> p (a b c d)").bitcast(F32)

        def words(at, n, dt=F32):
            a = region[:, at:at + n]
            return a if dt == F32 else a.bitcast(dt)

        c_in, c_zero = counter("const_loaded"), counter("const_zeroed")
        c_c = counter("const_computed")
        raw = [words(R_QKV + q * WW, WW) for q in range(2)]
        raw_in = Arrivals("raw_loaded")
        w_hi, w_lo, w_out = counter("w_high"), counter("w_low"), Arrivals("w_stored")
        zero = words(R_XN, D)
        projf = words(R_XN + D, P)
        pbf = words(R_XN + D + P, P)
        cbcol = words(R_XN + D + 2 * P, 1)
        mean8 = words(R_XN + D + 2 * P + 8, 8)
        brow = words(R_XN + 2 * D, 4 * P)
        brest = words(R_XN + 3 * D, 4 * P)
        bpart = [words(R_XN + 4 * D + q * D, 2 * P, BF16) for q in range(3)]

        def split_high(e, n, dst, r=None):
            raw_in.wait(e, n, r, 4)
            e.activation(dst[:, 0, :], raw[n % 2], ACT.Copy).then_inc(w_hi.sem, 1)

        def split_low(e, n, dst, r=None):
            e.wait_ge(w_hi.sem, n + 1 if r is None else r * 4 + (n + 1))
            e.tensor_tensor(dst[:, 1, :], raw[n % 2], dst[:, 0, :], ALU.subtract).then_inc(w_lo.sem, 1)

        def load_raw(e, n, r=None):
            if r is not None or n >= 2:
                e.wait_ge(w_lo.sem, n - 1 if r is None else r * 4 + (n - 1))
            row = n if r is None else r * 4 + n
            e.dma_start(raw[n % 2], wall[bass.ds(row, 1)].rearrange("o p w -> (o p) w")).then_inc(raw_in.sem(n), 16)

        with nc.Block() as blk:
            @blk.gpsimd
            def _(e):
                o = Own(e, own["pool"])
                o.do(e.memset(wqkv[:], 0.0))
                o.do(e.memset(projf, 0.0))
                o.do(e.memset(zero, 0.0))
                o.do(e.memset(ones[:], 1.0))
                o.do(e.memset(ones3[:], 1.0))
                o.do(e.memset(nhalf[:], -0.5))
                o.do(e.iota(iota8[:], pattern=[[1, E]], base=-E, channel_multiplier=0, allow_small_or_imprecise_dtypes=True))
                o.do(e.iota(steps8[:], pattern=[[P, NT]], base=0, channel_multiplier=0, allow_small_or_imprecise_dtypes=True))
                o.do(e.iota(bidx[:], pattern=[[1, NB]], base=0, channel_multiplier=0, allow_small_or_imprecise_dtypes=True))
                o.sync()
                e.engine_nop().then_inc(c_zero.sem, 1)
                o.do(e.affine_select(out=ident[:], in_=ones[:], pattern=[[-1, P]], compare_op=ALU.is_equal,
                                     fill=0.0, base=0, channel_multiplier=1))
                o.do(e.affine_select(out=tri[:], in_=ones[:], pattern=[[1, P]], compare_op=ALU.is_gt,
                                     fill=0.0, base=0, channel_multiplier=-1))
                o.sync()
                o.do(e.tensor_copy(identb[:], ident[:]))
                o.sync()
                own["pool"].n += o.k

            @blk.sync
            def _(e):
                load_raw(e, 0)
                load_raw(e, 1)
                e.wait_ge(c_zero.sem, 1)
                n = 0
                for q in range(2):
                    for b in range(NB + 1):
                        e.dma_start(sorted_x[q][b * P:(b + 1) * P, :], zero).then_inc(S("zero_stored").sem, 16)
                        n += 16
                S("zero_stored").n += n
                e.wait_ge(S("zero_stored").sem, n)

            @blk.scalar
            def _(e):
                c = c_in

                def load(dst, src):
                    e.dma_start(dst, src).then_inc(c.sem, 16)
                    c.n += 16

                load(rw[:], rwT.rearrange("(c p) e -> p c e", p=P))
                for dst, src in ((eb[:], ebias), (lw[:], lnw), (lb[:], lnb)):
                    load(dst, src.partition_broadcast(P))
                load(cw[:].rearrange("p a c -> p (a c)"), convw.rearrange("a c -> (a c)").partition_broadcast(P))
                e.wait_ge(c_zero.sem, 1)
                for t in range(8):
                    rows = slice(C * t, C * t + C)
                    load(wqkv[rows, 3 * C * t:3 * C * t + 3 * C], qkvw)
                    load(projf[rows, rows], projw)
                    load(pbf[0:1, rows], projb.rearrange("(a c) -> a c", a=1))
                    load(cbcol[rows, :], convb.rearrange("(c a) -> c a", a=1))
                e.wait_ge(c.sem, c.n)
                split_high(e, 0, wb[:, 0])
                e.wait_ge(S("bias_parts").sem, 1)
                for q in range(3):
                    e.dma_start(bias3[q:q + 1, :], bpart[q][0:1, :]).then_inc(S("bias_moved").sem, 16)
                e.wait_ge(S("bias_moved").sem, 48)

            @blk.tensor
            def _(e):
                e.wait_ge(c_in.sem, c_in.n)
                e.matmul(banks[0][0:1, 0:P], cbcol, projf, start=True, stop=True).then_inc(S("bias_proj").sem, 1)

            @blk.vector
            def _(e):
                o = Own(e, own["dve"])
                e.wait_ge(c_in.sem, c_in.n)
                w4 = projf.rearrange("p (t c) -> p t c", t=8)
                full = [P, 8, C]

                def centre(dst, src, n, m):
                    o.do(e.tensor_reduce(m, src, AX.X, ALU.add))
                    o.sync()
                    o.do(e.tensor_scalar(m, m, 1.0 / C, None, ALU.mult))
                    o.sync()
                    o.do(e.tensor_tensor(dst, src, m[:, :, None].to_broadcast([n, 8, C]), ALU.subtract))
                    o.sync()

                e.wait_ge(S("bias_proj").sem, 1)
                o.do(e.tensor_tensor(pbf[0:1, :], pbf[0:1, :], banks[0][0:1, 0:P], ALU.add))
                o.sync()
                centre(wproj[:, :, 0, :], w4, P, mean8)
                o.do(e.tensor_tensor(wproj[:, :, 1, :], wproj[:, :, 0, :], lw[:][:, None, :].to_broadcast(full), ALU.mult))
                b4 = brow.rearrange("p (g t s c) -> p g t s c", g=2, t=8, s=2)
                for g in range(2):
                    centre(b4[0:1, g, :, 0, :], pbf[0:1, :].rearrange("p (t c) -> p t c", t=8), 1, mean8[0:1, :])
                    o.do(e.tensor_tensor(b4[0:1, g, :, 1, :], b4[0:1, g, :, 0, :],
                                         lw[0:1, :][:, None, :].to_broadcast([1, 8, C]), ALU.mult))
                    o.sync()
                src = brow
                for q in range(3):
                    o.do(e.tensor_copy(bpart[q][0:1, :], src[0:1, :]))
                    o.sync()
                    if q < 2:
                        o.do(e.tensor_tensor(brest[0:1, :], src[0:1, :], bpart[q][0:1, :], ALU.subtract))
                        o.sync()
                        src = brest
                e.engine_nop().then_inc(S("bias_parts").sem, 1)
                split_low(e, 0, wb[:, 0])
                own["dve"].n += o.k

        class Prepare:

            def __init__(self, f, u, par, bank_t, bank_r):
                self.f, self.r0, self.par = f, u * UROWS, par
                self.psT, self.psR = bank_t, bank_r
                self.msum = words(R_SMALL, NT * E).rearrange("p (t e) -> p t e", t=NT)
                self.xn = words(R_XN, NT * D).rearrange("p (t d) -> p t d", t=NT)
                self.xr, self.ar, self.xc, self.xT32 = (hs_words[:, q * D:(q + 1) * D] for q in range(4))
                self.st = Stage(p_x=32 * NT if f else 16 * NT, p_xs=16 * NT * f, p_var=NT, p_rstd=NT, p_xc=NT, p_xn=NT,
                                p_T=NT, p_t32=NT, p_hi=NT, p_lo=NT, p_R=NT, p_log=NT, p_x2=NT * f, p_sc=1, p_m=1,
                                p_k=1, p_slot=1)

            def at(self, t, per=1, plus=0):
                return t * per + plus

            def wait(self, e, name, t, per=1, plus=0):
                n = self.st.base[name] + per * (1 + plus)
                e.wait_ge(S(name).sem, t * per + n)

            def rows(self, t):
                return bass.ds(t * P + self.r0, P)

            def sync(self, e, t, first):
                if not first:
                    self.wait(e, "p_xc", t, 1, -1)
                    if self.f:
                        self.wait(e, "p_xs", t, 16, -1)
                src = x1d if self.f else x
                e.dma_start(self.xr, src[self.rows(t), :]).then_inc(S("p_x").sem, 16)
                if self.f:
                    e.dma_start(self.ar, attd[self.rows(t), :]).then_inc(S("p_x").sem, 16)

            def store(self, e, t):
                if self.f:
                    self.wait(e, "p_x2", t)
                    e.dma_start(x2d[self.rows(t), :], self.xr).then_inc(S("p_xs").sem, 16)

            def vector_stats(self, e, o, t):
                self.wait(e, "p_x", t, 32 if self.f else 16)
                if self.f:
                    e.tensor_tensor(self.xr, self.xr, self.ar, ALU.add).then_inc(S("p_x2").sem, 1)
                    self.wait(e, "p_x2", t)
                o.do(e.bn_stats(stats[:, 0, :], self.xr))
                o.sync()
                o.do(e.tensor_copy(carrier[:], stats[:, 0, 0:1]))
                o.do(e.bn_aggr(mv[:, 0, :], stats[:, 0, :]))
                o.sync()
                e.tensor_scalar(mv[:, 0, 1:2], mv[:, 0, 1:2], EPS, None, ALU.add).then_inc(S("p_var").sem, 1)

            def vector_norm(self, e, t, first):
                if not first:
                    self.wait(e, "p_T", t, 1, -1)
                    self.wait(e, "p_xn", t, 1, -1)
                self.wait(e, "p_rstd", t)
                e.tensor_scalar(self.xc, self.xr, mv[:, 0, 0:1], rstd[:, 0, :], ALU.subtract,
                                ALU.mult).then_inc(S("p_xc").sem, 1)

            def vector_low(self, e, t):
                self.wait(e, "p_hi", t)
                e.tensor_tensor(xT[:, 1, :, bass.ds(t * P, P)], self.psT[:].rearrange("p (c r) -> p c r", c=NDC),
                                xT[:, 0, :, bass.ds(t * P, P)], ALU.subtract).then_inc(S("p_lo").sem, 1)

            def vector_logits(self, e, t):
                self.wait(e, "p_R", t)
                e.tensor_copy(scores[:, bass.ds(t, 1), :].rearrange("p o e -> p (o e)"),
                              self.psR[:, 0:E]).then_inc(S("p_log").sem, 1)

            def pool(self, e, t):
                self.wait(e, "p_var", t)
                e.tensor_tensor(rstd[:, 0, :], mv[:, 0, 1:2], nhalf[:, 0:1], ALU.pow).then_inc(S("p_rstd").sem, 1)
                self.wait(e, "p_xc", t)
                e.tensor_copy(self.xn[:, bass.ds(t, 1), :].rearrange("p o d -> p (o d)"),
                              self.xc).then_inc(S("p_xn").sem, 1)

            def pe_transpose(self, e, t, first):
                self.wait(e, "p_xc", t)
                if not first:
                    self.wait(e, "p_lo", t, 1, -1)
                for c in range(NDC):
                    m = e.transpose(self.psT[:, c * P:(c + 1) * P], self.xc[:, c * P:(c + 1) * P], ident[:])
                m.then_inc(S("p_T").sem, 1)

            def act(self, e, t, first):
                self.wait(e, "p_T", t)
                if not first:
                    self.wait(e, "p_R", t, 1, -1)
                e.activation(self.xT32, self.psT[:], ACT.Copy).then_inc(S("p_t32").sem, 1)
                e.activation(xT[:, 0, :, bass.ds(t * P, P)], self.psT[:].rearrange("p (c r) -> p c r", c=NDC),
                             ACT.Copy).then_inc(S("p_hi").sem, 1)

            def pe_router(self, e, t, first):
                self.wait(e, "p_t32", t)
                if not first:
                    self.wait(e, "p_log", t, 1, -1)
                for c in range(NDC):
                    m = e.matmul(self.psR[:, 0:E], self.xT32[:, c * P:(c + 1) * P], rw[:, c, :],
                                 start=(c == 0), stop=(c == NDC - 1))
                m.then_inc(S("p_R").sem, 1)

            def act_scores(self, e):
                self.st.wait(e, "p_log", NT)
                e.activation(scores[:], scores[:], ACT.Sigmoid).then_inc(S("p_sc").sem, 1)

            def pe_ranks(self, e):
                self.st.wait(e, "p_m", 1)
                msum = self.msum.rearrange("p t e -> p (t e)")
                e.matmul(self.psR[:, 64:64 + NT * E], tri[:], msum, start=True, stop=True)
                e.matmul(self.psR[:, 128:128 + NT * E], ones[:], msum, start=True, stop=True,
                         skip_group_check=True).then_inc(S("p_k").sem, 1)

            def route(self, e, o):
                at = [R_SMALL + NT * E]

                def small(*shape):
                    n = 1
                    for k in shape:
                        n *= k
                    a = words(at[0], n)
                    at[0] += n
                    assert at[0] <= R_SGH + 2 * HALF
                    if len(shape) == 2:
                        return a.rearrange("p (a b) -> p a b", a=shape[0])
                    return a

                sel, eq, sel2, rank = (small(NT, E) for _ in range(4))
                oh = [small(NT, E) for _ in range(2)]
                msum = self.msum
                tp = small(NT + 1, E)
                mx, mn, den, slotf = (small(NT) for _ in range(4))
                wsel = [small(NT) for _ in range(2)]
                c8 = sel
                nblk, bend = small(E), small(E)
                cmpb = small(NB, E)
                bexpf = small(NB)
                big = [P, NT, E]
                par = self.par
                steps = []

                def over_e(a):
                    return a[:, None, :].to_broadcast(big)

                def over_t(a):
                    return a[:, :, None].to_broadcast(big)

                def step(fn):
                    steps.append(fn)

                def do(*ops):
                    for op in ops:
                        def one(op=op):
                            o.do(op())
                            o.sync()
                        steps.append(one)

                step(lambda: self.st.wait(e, "p_sc", 1))
                do(lambda: e.tensor_tensor(sel, scores[:], over_e(eb[:]), ALU.add))
                for k in range(2):
                    cur = (sel, sel2)[k]
                    do(lambda cur=cur: e.tensor_reduce(mx, cur, AX.X, ALU.max),
                       lambda cur=cur: e.tensor_tensor(eq, cur, over_t(mx), ALU.is_ge),
                       lambda: e.tensor_tensor(eq, eq, over_e(iota8[:]), ALU.mult),
                       lambda: e.tensor_reduce(mn, eq, AX.X, ALU.min),
                       lambda k=k: e.tensor_tensor(oh[k], over_e(iota8[:]), over_t(mn), ALU.is_equal),
                       lambda k=k: e.tensor_tensor(eq, oh[k], scores[:], ALU.mult),
                       lambda k=k: e.tensor_reduce(wsel[k], eq, AX.X, ALU.add))
                    if k == 0:
                        do(lambda: e.tensor_scalar(sel2, oh[0], -1e30, None, ALU.mult),
                           lambda: e.tensor_tensor(sel2, sel2, sel, ALU.add))
                step(lambda: e.tensor_tensor(msum, oh[0], oh[1], ALU.add).then_inc(S("p_m").sem, 1))
                do(lambda: e.tensor_tensor(den, wsel[0], wsel[1], ALU.add),
                   lambda: e.tensor_scalar(den, den, 1e-9, None, ALU.add),
                   lambda: e.reciprocal(den, den),
                   lambda: e.tensor_tensor(coef[:, par, 0, :], wsel[0], den, ALU.mult),
                   lambda: e.tensor_tensor(coef[:, par, 1, :], wsel[1], den, ALU.mult))
                tot = self.psR[:, 128:128 + NT * E].rearrange("p (t e) -> p t e", t=NT)
                inside = self.psR[:, 64:64 + NT * E].rearrange("p (t e) -> p t e", t=NT)
                do(lambda: e.memset(tp[:, 0, :], 0.0))
                step(lambda: self.st.wait(e, "p_k", 1))
                for t in range(NT):
                    do(lambda t=t: e.tensor_tensor(tp[:, t + 1, :], tp[:, t, :], tot[:, t, :], ALU.add))
                do(lambda: e.tensor_tensor(c8, tp[:, NT, :][:, :, None].to_broadcast([P, E, NT]),
                                           steps8[:][:, None, :].to_broadcast([P, E, NT]), ALU.is_gt),
                   lambda: e.tensor_reduce(nblk, c8, AX.X, ALU.add),
                   lambda: e.tensor_copy(bend[:, 0:1], nblk[:, 0:1]))
                for k in range(1, E):
                    do(lambda k=k: e.tensor_tensor(bend[:, k:k + 1], bend[:, k - 1:k], nblk[:, k:k + 1], ALU.add))
                do(lambda: e.tensor_tensor(cmpb, bidx[:][:, :, None].to_broadcast([P, NB, E]),
                                           bend[:, None, :].to_broadcast([P, NB, E]), ALU.is_ge),
                   lambda: e.tensor_reduce(bexpf, cmpb, AX.X, ALU.add),
                   lambda: e.tensor_scalar(bexp[:, par, :], bexpf, float(E - 1), None, ALU.min),
                   lambda: e.tensor_tensor(nblk, bend, nblk, ALU.subtract),
                   lambda: e.tensor_scalar(nblk, nblk, float(P), None, ALU.mult),
                   lambda: e.tensor_tensor(rank, tp[:, 0:NT, :], inside, ALU.add),
                   lambda: e.tensor_tensor(rank, rank, over_e(nblk), ALU.add))
                for k in range(2):
                    do(lambda k=k: e.tensor_tensor(eq, oh[k], rank, ALU.mult),
                       lambda: e.tensor_reduce(slotf, eq, AX.X, ALU.add),
                       lambda k=k: e.tensor_copy(slots[:, par, k, :], slotf))
                step(lambda: e.engine_nop().then_inc(S("p_slot").sem, 1))
                return steps

        def prepare_alone(f, u, par):
            p = Prepare(f, u, par, banks[0], banks[1])
            with nc.Block() as blk:
                @blk.sync
                def _(e):
                    p.sync(e, 0, True)
                    with e.Fori(1, NT) as t:
                        p.sync(e, t, False)

                @blk.tensor
                def _(e):
                    p.pe_transpose(e, 0, True)
                    p.pe_router(e, 0, True)
                    with e.Fori(1, NT) as t:
                        p.pe_transpose(e, t, False)
                        p.pe_router(e, t, False)
                    p.pe_ranks(e)

                @blk.scalar
                def _(e):
                    p.act(e, 0, True)
                    with e.Fori(1, NT) as t:
                        p.act(e, t, False)
                    p.act_scores(e)

                @blk.gpsimd
                def _(e):
                    with e.Fori(0, NT) as t:
                        p.pool(e, t)

                @blk.vector
                def _(e):
                    o = Own(e, own["dve"])

                    def tile(t, first):
                        p.vector_stats(e, o, t)
                        p.vector_norm(e, t, first)
                        p.vector_low(e, t)
                        p.vector_logits(e, t)

                    tile(0, True)
                    per = o.k
                    own["dve"].n += o.k
                    o.k = 0
                    with e.Fori(1, NT) as t:
                        o.reg = t * per - per
                        tile(t, False)
                        assert o.k == per
                    o.reg, o.k = None, 0
                    own["dve"].n += per * (NT - 1)
                    for s in p.route(e, o):
                        s()
                    own["dve"].n += o.k

            p.st.end()

        class Finish:
            WAYS = 4

            def __init__(self, f, u, par):
                self.f, self.r0, self.par = f, u * UROWS, par
                self.buf = [[words(R_QKV + (3 * q + k) * D, D) for k in range(3)] for q in range(self.WAYS)]
                self.src, self.dst = (x, x1d) if f == 0 else (x2d, out)
                self.rows_in = Arrivals("f_rows_loaded", 1, self.WAYS)
                self.y_in = Arrivals("f_y_gathered", 2, self.WAYS)
                self.rows_out = Arrivals("f_rows_stored", 1 if f else 2, self.WAYS)
                ln = NT * (f == 0)
                self.st = Stage(f_sum=NT, f_var=ln, f_rstd=ln, f_ln=ln)

            def rows(self, t):
                return slice(self.r0 + t * P, self.r0 + (t + 1) * P)

            def pool_gather(self, e, t):
                if t >= self.WAYS:
                    self.rows_out.wait(e, t - self.WAYS)
                for k in range(2):
                    e.indirect_dma_start(out=self.buf[t % self.WAYS][k], out_offset=None, in_=sorted_y,
                                         in_offset=bass.IndirectOffsetOnAxis(ap=slots[:, self.par, k, t:t + 1], axis=0)
                                         ).then_inc(self.y_in.sem(t), 16)

            def pool_rstd(self, e, t):
                if self.f == 0:
                    self.st.wait(e, "f_var", t + 1)
                    e.tensor_tensor(rstd[:, t % 2, :], mv[:, t % 2, 1:2], nhalf[:, 0:1],
                                    ALU.pow).then_inc(S("f_rstd").sem, 1)

            def sync_load(self, e, t):
                if t >= self.WAYS:
                    self.rows_out.wait(e, t - self.WAYS)
                e.dma_start(self.buf[t % self.WAYS][2], self.src[self.rows(t), :]).then_inc(self.rows_in.sem(t), 16)

            def store(self, e, t):
                self.st.wait(e, "f_sum", t + 1)
                e.dma_start(self.dst[self.rows(t), :], self.buf[t % self.WAYS][2]).then_inc(self.rows_out.sem(t), 16)
                if self.f == 0:
                    self.st.wait(e, "f_ln", t + 1)
                    e.dma_start(xln2[self.rows(t), :], self.buf[t % self.WAYS][0]).then_inc(self.rows_out.sem(t), 16)

            def vector_sum(self, e, o, t):
                a, b, r = self.buf[t % self.WAYS]
                self.y_in.wait(e, t)
                self.rows_in.wait(e, t)
                o.do(e.scalar_tensor_tensor(out=a, in0=a, scalar=coef[:, self.par, 0, t:t + 1], in1=acc[:, t, :],
                                            op0=ALU.mult, op1=ALU.add))
                o.sync()
                o.do(e.scalar_tensor_tensor(out=b, in0=b, scalar=coef[:, self.par, 1, t:t + 1], in1=a,
                                            op0=ALU.mult, op1=ALU.add))
                o.sync()
                e.scalar_tensor_tensor(out=r, in0=b, scalar=0.5, in1=r, op0=ALU.mult,
                                       op1=ALU.add).then_inc(S("f_sum").sem, 1)
                if self.f == 0:
                    self.st.wait(e, "f_sum", t + 1)
                    o.do(e.bn_stats(stats[:, t % 2, :], r))
                    o.sync()
                    o.do(e.bn_aggr(mv[:, t % 2, :], stats[:, t % 2, :]))
                    o.sync()
                    e.tensor_scalar(mv[:, t % 2, 1:2], mv[:, t % 2, 1:2], EPS, None, ALU.add).then_inc(S("f_var").sem, 1)

            def vector_norm(self, e, t):
                if self.f == 0:
                    a, _, r = self.buf[t % self.WAYS]
                    self.st.wait(e, "f_rstd", t + 1)
                    e.tensor_scalar(a, r, mv[:, t % 2, 0:1], rstd[:, t % 2, :], ALU.subtract,
                                    ALU.mult).then_inc(S("f_ln").sem, 1)

            def end(self):
                for a in (self.rows_in, self.y_in, self.rows_out):
                    a.end(NT)
                self.st.end()

        def finish_alone(f, u, par):
            fin = Finish(f, u, par)
            with nc.Block() as blk:
                @blk.gpsimd
                def _(e):
                    for t in range(NT):
                        fin.pool_gather(e, t)
                        if t >= 2:
                            fin.pool_rstd(e, t - 2)
                    fin.pool_rstd(e, NT - 2)
                    fin.pool_rstd(e, NT - 1)

                @blk.sync
                def _(e):
                    for t in range(NT):
                        fin.sync_load(e, t)
                    fin.rows_out.wait_last(e, NT)

                @blk.scalar
                def _(e):
                    for t in range(NT):
                        fin.store(e, t)

                @blk.vector
                def _(e):
                    o = Own(e, own["dve"])
                    for t in range(NT):
                        fin.vector_sum(e, o, t)
                        if t:
                            fin.vector_norm(e, t - 1)
                    fin.vector_norm(e, NT - 1)
                    own["dve"].n += o.k
            fin.end()


        class Attention:

            def __init__(self, b, first_slot, budget, ready):
                self.ready = ready
                self.tok = words(0, TOKW)
                self.sco = words(TOKW, TOKW)
                self.qkv = words(R_QKV, QKVW)
                self.small = words(R_SMALL, 2 * NW * WL)
                self.small2 = words(R_SMALL + 2 * NW * WL, NTOK)
                self.tmp = [self.tok[:, k * TOKW // 2:(k + 1) * TOKW // 2] for k in range(2)]
                self.sq, self.dl, self.done = (self.qkv[:, k * TOKW:(k + 1) * TOKW] for k in range(3))
                self.img = xln2[b * 512:(b + 1) * 512, :].rearrange("r c -> (r c)").rearrange(
                    "(s i g e) -> g s i e", s=16, i=NPI, g=8)
                self.res = attd[b * 512:(b + 1) * 512, :].rearrange("r c -> (r c)").rearrange(
                    "(c s i g j) -> g i s c j", c=C, s=16, i=NPI, g=8)
                self.q4 = self.qkv.rearrange("p (i j c) -> p i j c", i=NPI, j=NPJ)
                self.q3 = self.qkv.rearrange("p (t c) -> p t c", c=3 * C)
                self.s5 = self.sco.rearrange("p (r w a b) -> p r w a b", r=2, w=NW, a=WL)
                self.st = Stage(t_x=128, t_x2=128, t_T=4, t_Tc=4, t_q=16, t_qc=16, t_pp=16, t_rd=16, t_k=1, t_s=1, t_e=1,
                                t_cv=1, t_sum=1, t_oT=4, t_oTc=4, t_pr=8, t_prc=8, t_var=1, t_rstd=1, t_tb=1, t_out=1,
                                t_st=1024)
                self.b = b
                self.pe, self.act, self.vec, self.pool, self.sp = {}, {}, {}, {}, {}
                self.table = {"pe": self.pe, "act": self.act, "vec": self.vec, "pool": self.pool, "sp": self.sp}
                self.schedule(first_slot, budget)

            def window(self, r, lo, n):
                if r == 0:
                    return self.q3[:, :, lo:lo + n].rearrange("p (w a) c -> p w a c", a=WL)
                return self.q4[:, :, :, lo:lo + n].rearrange("p a w c -> p w a c")

            def put(self, table, slot, pos, fn):
                table.setdefault((slot, pos), []).append(fn)

            def schedule(self, s0, budget):
                T, M = self.pe_turn, self.pe_qkv
                order = [(T, 0), (T, 1)] + [(M, g) for g in range(4)] + [(T, 2)] + [(M, g) for g in range(4, 8)] + \
                        [(T, 3)] + [(M, g) for g in range(8, 16)]
                turn = {T: self.act_turn, M: self.act_qkv}
                self.put(self.sp, s0, 0, self.sp_load)
                for n, (fn, k) in enumerate(order):
                    at = (s0 + n // 8, n // 2 % 4)
                    self.put(self.pe, *at, lambda e, fn=fn, k=k: fn(e, k))
                    self.put(self.act, *at, lambda e, fn=fn, k=k: turn[fn](e, k))
                steps = [(3.5, lambda e, o, a=a: self.vec_scores(e, o, a), self.pool_scores, a) for a in range(WL)]
                steps += [(4.5, self.vec_softmax, None, 0), (2.6, self.vec_sums, None, 0)]
                steps += [(3.5, lambda e, o, a=a: self.vec_values(e, o, a), self.pool_values, a) for a in range(WL)]
                steps += [(4.6, self.vec_merge, None, 0)]
                slot, used = s0 + 3, 0.0
                for cost, vec, pool, a in steps:
                    if used + cost / 2 > budget:
                        slot, used = slot + 1, used - budget
                    if vec == self.vec_sums:
                        slot, used = slot + 1, 0.0
                        self.put(self.act, slot, 0, self.act_exp)
                        self.put(self.pool, slot, 0, self.pool_conv_centre)
                    used += cost
                    self.put(self.vec, slot, 0, vec)
                    if pool:
                        self.put(self.pool, slot, 0, lambda e, o, pool=pool, a=a: pool(e, o, a))
                        if pool == self.pool_values and a % 2:
                            self.put(self.pool, slot, 0, lambda e, o, a=a: self.pool_conv_tap(e, o, a // 2))
                slot += 1
                self.put(self.sp, slot, 0, self.sp_reload)
                order = [(self.pe_turn2, 0), (self.pe_turn2, 1), (self.pe_proj, 0), (self.pe_proj, 1), (self.pe_proj, 2),
                         (self.pe_proj, 3), (self.pe_turn2, 2), (self.pe_proj, 4), (self.pe_proj, 5),
                         (self.pe_turn2, 3), (self.pe_proj, 6), (self.pe_proj, 7)]
                turn2 = {self.pe_turn2: self.act_turn2, self.pe_proj: self.act_proj}
                for n, (fn, k) in enumerate(order):
                    at = (slot + n // 8, n // 2 % 4)
                    self.put(self.pe, *at, lambda e, fn=fn, k=k: fn(e, k))
                    self.put(self.act, *at, lambda e, fn=fn, k=k: turn2[fn](e, k))
                self.put(self.pool, slot, 0, self.pool_residual)
                slot += 2
                self.put(self.vec, slot, 0, self.vec_norm)
                self.put(self.pool, slot, 0, self.pool_rstd)
                self.put(self.sp, slot, 0, self.sp_store)
                self.last = slot

            def pe_turn(self, e, m):
                if m == 0:
                    self.st.wait(e, "t_x", 128)
                else:
                    self.st.wait(e, "t_Tc", m)
                for n in range(4):
                    g = 4 * m + n
                    mm = e.transpose(banks[6][:, n * P:(n + 1) * P], self.tok[:, g * P:(g + 1) * P], ident[:])
                mm.then_inc(S("t_T").sem, 1)

            def pe_qkv(self, e, g):
                self.st.wait(e, "t_Tc", g // 4 + 1)
                if g:
                    self.st.wait(e, "t_qc", g)
                e.matmul(banks[7][:, 0:24 * C], self.tokT(0, g // 4)[:, (g % 4) * P:(g % 4 + 1) * P], wqkv[:],
                         start=True, stop=True).then_inc(S("t_q").sem, 1)

            def tokT(self, phase, m):
                buf = self.done if phase else self.sco
                return buf[:, (m % 2) * 512:(m % 2) * 512 + 512]

            def pe_turn2(self, e, m):
                if m == 0:
                    self.st.wait(e, "t_sum", 1)
                else:
                    self.st.wait(e, "t_oTc", m)
                for n in range(4):
                    g = 4 * m + n
                    mm = e.transpose(banks[6][:, n * P:(n + 1) * P], self.sco[:, g * P:(g + 1) * P], ident[:])
                mm.then_inc(S("t_oT").sem, 1)

            def pe_proj(self, e, h):
                self.st.wait(e, "t_oTc", h // 2 + 1)
                if h:
                    self.st.wait(e, "t_prc", h)
                e.matmul(banks[7][:], ones3[:], bias3[:], start=True, stop=False)
                for n in range(2):
                    g = 2 * (h % 2) + n
                    mm = e.matmul(banks[7][:, n * 2 * P:(n + 1) * 2 * P], self.tokT(1, h // 2)[:, g * P:(g + 1) * P],
                                  wproj[:].rearrange("p t s c -> p (t s c)"), start=False, stop=(n == 1))
                mm.then_inc(S("t_pr").sem, 1)

            def sp_load(self, e):
                self.ready(e)
                for g in range(8):
                    e.dma_start(self.tok[g:P:8, :].rearrange("p (i e) -> p i e", i=NPI), self.img[g]).then_inc(S("t_x").sem, 16)

            def act_turn(self, e, m):
                self.st.wait(e, "t_T", m + 1)
                if m >= 2:
                    self.st.wait(e, "t_q", 4 * (m - 1))
                e.activation(self.tokT(0, m), banks[6][:], ACT.Copy).then_inc(S("t_Tc").sem, 1)

            def act_qkv(self, e, g):
                self.st.wait(e, "t_q", g + 1)
                e.activation(self.qkv[:, g * 24 * C:(g + 1) * 24 * C], banks[7][:, 0:24 * C],
                             ACT.Copy).then_inc(S("t_qc").sem, 1)

            def act_exp(self, e):
                self.st.wait(e, "t_s", 1)
                e.activation(self.sco, self.sco, ACT.Exp, scale=SCALE).then_inc(S("t_e").sem, 1)

            def sp_reload(self, e):
                self.st.wait(e, "t_sum", 1)
                for g in range(8):
                    e.dma_start(self.tok[g:P:8, :].rearrange("p (i e) -> p i e", i=NPI), self.img[g]).then_inc(S("t_x2").sem, 16)

            def act_turn2(self, e, m):
                self.st.wait(e, "t_oT", m + 1)
                if m >= 2:
                    self.st.wait(e, "t_pr", 2 * (m - 1))
                e.activation(self.tokT(1, m), banks[6][:], ACT.Copy).then_inc(S("t_oTc").sem, 1)

            def act_proj(self, e, h):
                self.st.wait(e, "t_pr", h + 1)
                two = banks[7][:].rearrange("p (t s c) -> p t s c", s=2, c=C)
                cols = slice(h * 2 * P, (h + 1) * 2 * P)
                e.activation(self.sq[:, cols].rearrange("p (t c) -> p t c", c=C), two[:, :, 0, :], ACT.Square)
                e.activation(self.dl[:, cols].rearrange("p (t c) -> p t c", c=C), two[:, :, 1, :],
                             ACT.Copy).then_inc(S("t_prc").sem, 1)

            def sp_store(self, e):
                self.st.wait(e, "t_out", 1)
                done = self.done.rearrange("p (c i j) -> p i c j", c=C, i=NPI)
                for g in range(8):
                    for i in range(NPI):
                        e.dma_start(self.res[g, i], done[g:P:8, i]).then_inc(S("t_st").sem, 16)

            def product(self, e, r, a, values):
                t = self.tmp[r]
                if values:
                    t = t.rearrange("p (w c b) -> p w c b", w=NW, c=H)
                    x0 = self.s5[:, r, :, a:a + 1, :].to_broadcast([P, NW, H, WL])
                    x1 = self.window(r, 2 * C + H * r, H).rearrange("p w b c -> p w c b")
                else:
                    t = t.rearrange("p (w b c) -> p w b c", w=NW, b=WL)
                    x0 = self.window(r, H * r, H)[:, :, a:a + 1, :].to_broadcast([P, NW, WL, H])
                    x1 = self.window(r, C + H * r, H)
                return e.tensor_tensor(t, x0, x1, ALU.mult)

            def vec_pair(self, e, o, a, values):
                o.sync()
                o.do(self.product(e, 0, a, values))
                o.sync()
                for r in range(2):
                    t = self.tmp[r].rearrange("p (w b c) -> p w b c", w=NW, b=WL)
                    dst = self.window(r, H * r, H)[:, :, a, :] if values else self.s5[:, r, :, a, :]
                    if r == 1:
                        self.st.wait(e, "t_pp", WL * values + a + 1)
                    ins = e.tensor_reduce(dst, t, AX.X, ALU.add)
                    if r == 0:
                        o.do(ins)
                    else:
                        ins.then_inc(S("t_rd").sem, 1)

            def vec_scores(self, e, o, a):
                if a == 0:
                    self.st.wait(e, "t_qc", 16)
                self.vec_pair(e, o, a, 0)
                if a == WL - 1:
                    o.sync()
                    e.engine_nop().then_inc(S("t_k").sem, 1)

            def rows(self, v):
                return v[:, :, None].to_broadcast([P, 2 * NW * WL, WL])

            def vec_softmax(self, e, o):
                s3 = self.sco.rearrange("p (n b) -> p n b", b=WL)
                self.st.wait(e, "t_rd", WL)
                o.do(e.tensor_reduce(self.small, s3, AX.X, ALU.max))
                o.sync()
                e.tensor_tensor(s3, s3, self.rows(self.small), ALU.subtract).then_inc(S("t_s").sem, 1)

            def vec_sums(self, e, o):
                self.st.wait(e, "t_e", 1)
                o.do(e.tensor_reduce(self.small, self.sco.rearrange("p (n b) -> p n b", b=WL), AX.X, ALU.add))
                o.sync()
                o.do(e.reciprocal(self.small, self.small))

            def vec_values(self, e, o, a):
                self.vec_pair(e, o, a, 1)

            def vec_merge(self, e, o):
                self.st.wait(e, "t_rd", 2 * WL)
                o.sync()
                inv = self.small.rearrange("p (r w a) -> p r w a", r=2, w=NW)
                for r in range(2):
                    w = self.window(r, H * r, H)
                    o.do(e.tensor_tensor(w, w, inv[:, r][:, :, :, None].to_broadcast([P, NW, WL, H]), ALU.mult))
                o.sync()
                self.st.wait(e, "t_cv", 1)
                e.tensor_tensor(self.sco.rearrange("p (t c) -> p t c", c=C), self.q3[:, :, 0:C], self.q3[:, :, C:2 * C],
                                ALU.add).then_inc(S("t_sum").sem, 1)

            def vec_norm(self, e, o):
                self.st.wait(e, "t_prc", 8)
                o.do(e.tensor_reduce(self.small2, self.sq.rearrange("p (t c) -> p t c", c=C), AX.X, ALU.add))
                o.sync()
                e.tensor_scalar(self.small2, self.small2, 1.0 / C, EPS, ALU.mult, ALU.add).then_inc(S("t_var").sem, 1)
                self.st.wait(e, "t_rstd", 1)
                dl = self.dl.rearrange("p (t c) -> p t c", c=C)
                o.do(e.tensor_tensor(dl, dl, self.small2[:, :, None].to_broadcast([P, NTOK, C]), ALU.mult))
                o.sync()
                self.st.wait(e, "t_tb", 1)
                self.st.wait(e, "t_pr", 8)
                e.tensor_tensor(self.done.rearrange("p (c t) -> p t c", c=C), dl,
                                self.tok.rearrange("p (t c) -> p t c", c=C), ALU.add).then_inc(S("t_out").sem, 1)

            def pool_scores(self, e, o, a):
                if a == 0:
                    self.st.wait(e, "t_qc", 16)
                else:
                    self.st.wait(e, "t_rd", a)
                self.product(e, 1, a, 0).then_inc(S("t_pp").sem, 1)

            def pool_values(self, e, o, a):
                if a == 0:
                    self.st.wait(e, "t_e", 1)
                self.st.wait(e, "t_rd", WL + a)
                o.sync()
                self.product(e, 1, a, 1).then_inc(S("t_pp").sem, 1)

            def pool_conv_centre(self, e, o):
                self.st.wait(e, "t_k", 1)
                self.st.wait(e, "t_rd", WL)
                o.do(e.tensor_tensor(self.q3[:, :, C:2 * C], self.q3[:, :, 2 * C:3 * C],
                                     cw[:, 1:2, :].to_broadcast([P, NTOK, C]), ALU.mult))

            def pool_conv_tap(self, e, o, k):
                r, tap = k // 2, 2 * (k % 2)
                n = WL - 1
                to, of = (slice(1, WL), slice(0, n)) if tap == 0 else (slice(0, n), slice(1, WL))
                kw, vw = self.window(r, C + H * r, H), self.window(r, 2 * C + H * r, H)
                t = self.tmp[1][:, 0:NW * n * H].rearrange("p (w b c) -> p w b c", w=NW, b=n)
                wt = cw[:, tap:tap + 1, H * r:H * r + H][:, None].to_broadcast([P, NW, n, H])
                self.st.wait(e, "t_rd", WL + 2 * k + 2)
                o.do(e.tensor_tensor(t, vw[:, :, of, :], wt, ALU.mult))
                o.sync()
                ins = e.tensor_tensor(kw[:, :, to, :], kw[:, :, to, :], t, ALU.add)
                o.do(ins)
                o.sync()
                if k == 3:
                    e.engine_nop().then_inc(S("t_cv").sem, 1)

            def pool_residual(self, e, o):
                self.st.wait(e, "t_x2", 128)
                t = self.tok.rearrange("p (t c) -> p t c", c=C)
                e.tensor_tensor(t, t, lb[:][:, None, :].to_broadcast([P, NTOK, C]), ALU.add).then_inc(S("t_tb").sem, 1)

            def pool_rstd(self, e, o):
                self.st.wait(e, "t_var", 1)
                e.tensor_tensor(self.small2, self.small2, nhalf[:], ALU.pow).then_inc(S("t_rstd").sem, 1)

        def shared(par, fin=None, images=None, split=False):
            sgh = [words(R_SGH + q * HALF, HALF) for q in range(2)]
            psG, psU, psD = banks[0:2], banks[2:4], banks[4:6]
            chunk_in = Arrivals("chunk_loaded")
            st = Stage(h_g=NSLOT, h_u=NSLOT, h_silu=NSLOT, h_mul=NSLOT, h_hi=NSLOT, h_lo=NSLOT, h_d=2 * NSLOT,
                       h_acc=2 * NSLOT, scat=256)
            xn = words(R_XN, NT * D).rearrange("p (t d) -> p t d", t=NT)
            fin_slots = NT // 2
            atts = []
            if images:
                def ready0(e):
                    st.wait(e, "scat", 256)
                    for t in range(NT):
                        if t >= NT - fin.WAYS:
                            fin.rows_out.wait(e, t)
                atts.append(Attention(images[0], fin_slots + 2, 5.6, ready0))
                first = atts[0]
                base_st = first.st.base["t_st"]
                base_out = first.st.base["t_out"]
                first.st.end()

                def ready1(e):
                    e.wait_ge(S("t_out").sem, base_out + 1)
                    e.wait_ge(S("t_st").sem, base_st + 1024)
                atts.append(Attention(images[1], first.last + 1, 5.6, ready1))
                atts[1].st.end()
            last = max([a.last for a in atts], default=-1)

            def extra(table, slot, pos, *args):
                for a in atts:
                    for fn in a.table[table].get((slot, pos), []):
                        fn(*args)

            def turns(body):
                if images:
                    for j in range(NSLOT):
                        body(j, None)
                    for j in range(NSLOT, last + 1):
                        body(j, None, True)
                else:
                    for j in range(TURN):
                        body(j, None)

            with nc.Block() as blk:
                @blk.sync
                def _(e):
                    if split:
                        def piece(n, i):
                            load_raw(e, 2 * n + 2, i)
                            if n < NU - 1:
                                load_raw(e, 2 * n + 3, i)
                            e.wait_ge(w_lo.sem, 2 * n + 3 if i is None else i * 4 + (2 * n + 3))
                            row = n if i is None else i * 2 + n
                            e.dma_start(wsplit[bass.ds(row, 1)].rearrange("o p w -> (o p) w"),
                                        wb[:, (n + 1) % 2].rearrange("p a w -> p (a w)")).then_inc(w_out.sem(n), 16)
                        with e.Fori(0, NU // 2 - 1) as i:
                            piece(0, i)
                            piece(1, i)
                        piece(NU - 2, None)
                        piece(NU - 1, None)
                        w_out.wait_last(e, NU)
                    else:
                        for n in range(NU):
                            for j in range(4 * n - 6, 4 * n - 2):
                                extra("sp", j, 0, e)
                            if n >= 2:
                                st.wait(e, "h_d", 8 * (n - 1))
                            e.dma_start(wb[:, n % 2].rearrange("p a w -> p (a w)"),
                                        wsplit[(n + NU - 1) % NU]).then_inc(chunk_in.sem(n), 16)
                            if fin and n == 0:
                                for t in range(fin.WAYS):
                                    fin.sync_load(e, t)
                            if fin and n == 1:
                                for t in range(NT):
                                    fin.store(e, t)
                                    if t + fin.WAYS < NT:
                                        fin.sync_load(e, t + fin.WAYS)
                    if fin:
                        fin.rows_out.wait_last(e, NT)
                    for j in range(NSLOT - 6, last + 1):
                        extra("sp", j, 0, e)
                    if images:
                        for a in atts:
                            e.wait_ge(S("t_st").sem, a.st.base["t_st"] + 1024)

                @blk.tensor
                def _(e):
                    def products(ps, j, gu, name):
                        q, half, k = (j // 4) % 2, (j // 2) % 2, j % 2
                        i = 0
                        for c in range(NDC):
                            for wp, xp in PASSES:
                                o = gu * NDC * HC + c * HC + k * P
                                m = e.matmul(ps[j % 2][:], wb[:, q, wp, o:o + P],
                                             xT[:, xp, c, half * HALF:(half + 1) * HALF],
                                             start=(i == 0), stop=(i == 3 * NDC - 1))
                                i += 1
                        m.then_inc(S(name).sem, 1)

                    def down(g, tt, r):
                        if 4 * g + tt >= 2:
                            st.wait(e, "h_acc", 4 * g + tt - 1, r, 16)
                        i = 0
                        for kt in range(KT):
                            for wp, hp in PASSES:
                                o = W3OFF + kt * D
                                m = e.matmul(psD[tt % 2][:], hs[:, g % 2, hp, kt, tt * P:(tt + 1) * P],
                                             wb[:, (g // 2) % 2, wp, o:o + D], start=(i == 0), stop=(i == 5))
                                i += 1
                        m.then_inc(S("h_d").sem, 1)

                    def slot(j, r, only_extra=False):
                        if only_extra:
                            for pos in range(4):
                                extra("pe", j, pos, e)
                            return
                        if j % 4 == 0:
                            if split:
                                n = 2 * (j // 4) + 1
                                e.wait_ge(w_lo.sem, n if r is None else r * 4 + n)
                            else:
                                chunk_in.wait(e, j // 4, r)
                        if j >= 2:
                            st.wait(e, "h_mul", j - 1, r, 8)
                        g = j // 2 - 1
                        products(psG, j, 0, "h_g")
                        extra("pe", j, 0, e)
                        products(psU, j, 1, "h_u")
                        extra("pe", j, 1, e)
                        if g >= 0 and j % 2 == 0:
                            st.wait(e, "h_lo", 2 * g + 2, r, 8)
                        if g >= 0:
                            down(g, 2 * (j % 2), r)
                        extra("pe", j, 2, e)
                        if g >= 0:
                            down(g, 2 * (j % 2) + 1, r)
                        extra("pe", j, 3, e)
                        if images and j == NSLOT - 1:
                            tail()

                    def tail():
                        st.wait(e, "h_lo", NSLOT)
                        for tt in range(4):
                            down(NSLOT // 2 - 1, tt, None)

                    turns(slot)
                    if not images:
                        with e.Fori(0, NSLOT // TURN - 1) as r:
                            for j in range(TURN, 2 * TURN):
                                slot(j, r)
                        tail()

                @blk.scalar
                def _(e):
                    def slot(j, r, only_extra=False):
                        if only_extra:
                            for pos in range(4):
                                extra("act", j, pos, e)
                            return
                        if j >= 2:
                            st.wait(e, "h_lo", j - 1, r, 8)
                        st.wait(e, "h_g", j + 1, r, 8)
                        e.activation(sgh[j % 2], psG[j % 2][:], ACT.Silu).then_inc(S("h_silu").sem, 1)
                        extra("act", j, 0, e)
                        st.wait(e, "h_mul", j + 1, r, 8)
                        if j >= 4:
                            st.wait(e, "h_d", 4 * (j // 2 - 1), r, 16)
                        e.activation(hs[:, (j // 2) % 2, 0, j % 2, :], sgh[j % 2], ACT.Copy).then_inc(S("h_hi").sem, 1)
                        if split and j % 2 == 0:
                            n = j // 4
                            if j % 4 == 0:
                                ex = n if r is None else r * 2 + n
                                split_high(e, 2 * n + 1, wr[:, bass.ds(ex, 1)].rearrange("p o a w -> p (o a) w"), r)
                            else:
                                if n:
                                    st.wait(e, "h_d", 8 * n, r, 16)
                                if n >= 2:
                                    w_out.wait(e, n - 2, r)
                                split_high(e, 2 * n + 2, wb[:, (n + 1) % 2], r)
                        for pos in range(1, 4):
                            extra("act", j, pos, e)

                    turns(slot)
                    if not images:
                        with e.Fori(0, NSLOT // TURN - 1) as r:
                            for j in range(TURN, 2 * TURN):
                                slot(j, r)

                @blk.gpsimd
                def _(e):
                    o = Own(e, own["pool"])

                    def scatter(t):
                        for k in range(2):
                            e.indirect_dma_start(out=sorted_x[par],
                                                 out_offset=bass.IndirectOffsetOnAxis(ap=slots[:, par, k, t:t + 1],
                                                                                      axis=0),
                                                 in_=xn[:, t, :], in_offset=None).then_inc(S("scat").sem, 16)

                    def slot(j, r, only_extra=False):
                        if only_extra:
                            extra("pool", j, 0, e, o)
                            return
                        st.wait(e, "h_hi", j + 1, r, 8)
                        e.tensor_tensor(hs[:, (j // 2) % 2, 1, j % 2, :], sgh[j % 2],
                                        hs[:, (j // 2) % 2, 0, j % 2, :], ALU.subtract).then_inc(S("h_lo").sem, 1)
                        if fin and r is None and j < fin_slots:
                            fin.pool_rstd(e, 2 * j)
                            fin.pool_rstd(e, 2 * j + 1)
                            if 2 * j + fin.WAYS - 2 < NT and j:
                                fin.pool_gather(e, 2 * j + fin.WAYS - 2)
                                fin.pool_gather(e, 2 * j + fin.WAYS - 1)
                        if r is None and j < 4:
                            scatter(2 * j)
                            scatter(2 * j + 1)
                        extra("pool", j, 0, e, o)

                    if fin:
                        for t in range(fin.WAYS):
                            fin.pool_gather(e, t)
                    turns(slot)
                    if not images:
                        with e.Fori(0, NSLOT // TURN - 1) as r:
                            for j in range(TURN, 2 * TURN):
                                slot(j, r)
                    st.wait(e, "scat", 256)
                    own["pool"].n += o.k

                @blk.vector
                def _(e):
                    o = Own(e, own["dve"])

                    def slot(j, r, only_extra=False):
                        if only_extra:
                            extra("vec", j, 0, e, o)
                            return
                        st.wait(e, "h_silu", j + 1, r, 8)
                        st.wait(e, "h_u", j + 1, r, 8)
                        e.tensor_tensor(sgh[j % 2], psU[j % 2][:], sgh[j % 2], ALU.mult).then_inc(S("h_mul").sem, 1)
                        if j >= 2:
                            g = j // 2 - 1
                            for tt in (2 * (j % 2), 2 * (j % 2) + 1):
                                add(g, tt, r)
                        if fin and r is None and j < fin_slots:
                            for t in (2 * j, 2 * j + 1):
                                fin.vector_sum(e, o, t)
                                if t:
                                    fin.vector_norm(e, t - 1)
                            if j == fin_slots - 1:
                                fin.vector_norm(e, NT - 1)
                        if split and j % 2 == 0:
                            n = j // 4
                            if j % 4 == 0:
                                ex = n if r is None else r * 2 + n
                                split_low(e, 2 * n + 1, wr[:, bass.ds(ex, 1)].rearrange("p o a w -> p (o a) w"), r)
                            else:
                                split_low(e, 2 * n + 2, wb[:, (n + 1) % 2], r)
                        extra("vec", j, 0, e, o)
                        if images and j == NSLOT - 1:
                            tail()

                    def add(g, tt, r):
                        st.wait(e, "h_d", 4 * g + tt + 1, r, 16)
                        a = acc[:, (g % 2) * TH + tt, :]
                        if r is None and g < 2:
                            e.tensor_copy(a, psD[tt % 2][:]).then_inc(S("h_acc").sem, 1)
                        else:
                            st.wait(e, "h_acc", 4 * (g - 2) + tt + 1, r, 16)
                            e.tensor_tensor(a, psD[tt % 2][:], a, ALU.add).then_inc(S("h_acc").sem, 1)

                    def tail():
                        for tt in range(4):
                            add(NSLOT // 2 - 1, tt, None)

                    turns(slot)
                    if not images:
                        with e.Fori(0, NSLOT // TURN - 1) as r:
                            for j in range(TURN, 2 * TURN):
                                slot(j, r)
                        tail()
                    own["dve"].n += o.k
            st.end()
            if not split:
                chunk_in.end(NU)
            if fin:
                fin.end()

        def routed(par, prep=None):
            at = [R_QKV]

            def take(n, dt=F32):
                a = words(at[0], n, dt)
                at[0] += n
                assert at[0] <= R_SMALL
                return a

            xs = [take(D) for _ in range(2)]
            xsT = [take(D, BF16).rearrange("p (a n) -> p a n", a=2) for _ in range(2)]
            sg = [take(HC) for _ in range(2)]
            hf = [take(HC) for _ in range(2)]
            hb = [take(HC, BF16).rearrange("p (a n) -> p a n", a=2) for _ in range(2)]
            hT = [take(HC, BF16).rearrange("p (a k n) -> p a k n", a=2, k=KT) for _ in range(2)]
            yo = [take(D) for _ in range(2)]
            psX, psH, psHT, psY = banks[0], banks[1:3], banks[3][:].bitcast(BF16)[:, 0:2 * HC], banks[4:6]
            rows_in, rows_out = Arrivals("rows_loaded"), Arrivals("rows_stored")
            st = Stage(r_T=NB + 1, r_hi=NB + 1, r_lo=NB + 1, r_wu=NB, r_wd=NB, r_h=NB, r_silu=NB, r_mul=NB, r_hbh=NB,
                       r_hbl=NB, r_HT=NB, r_hT=NB, r_y=NB, r_yo=NB)
            TILE_TURNS = NT - 1
            PEEL = 3

            def wait(e, name, k, i=None):
                st.wait(e, name, k, i)

            def program(e, block, hooks):
                nohook = lambda n: None
                use = hooks is not None and prep is not None

                def tile_hook(second, t, first):
                    return (lambda n: hooks(second, n, t, first)) if use else nohook

                block(0, None, nohook)
                block(1, None, tile_hook(0, 0, True))
                block(2, None, tile_hook(1, 0, True))
                if prep is None:
                    with e.Fori(0, (NB - PEEL) // 2) as i:
                        block(3, i, nohook)
                        block(4, i, nohook)
                    return
                with e.Fori(0, TILE_TURNS) as i:
                    block(3, i, tile_hook(0, i + 1, False))
                    block(4, i, tile_hook(1, i + 1, False))

            LATE = PEEL + 2 * TILE_TURNS
            late = range(LATE, NB) if prep else []

            with nc.Block() as blk:
                @blk.sync
                def _(e):
                    def load(k, i):
                        row = k * P if i is None else i * (2 * P) + k * P
                        if i is not None or k >= 2:
                            wait(e, "r_T", k - 1, i)
                        e.dma_start(xs[k % 2], sorted_x[par][bass.ds(row, P), :]).then_inc(rows_in.sem(k), 16)

                    def block(k, i, hook):
                        hook(0)
                        load(k + 1, i)

                    def hooks(second, n, t, first):
                        if not second:
                            prep.sync(e, t, first)

                    load(0, None)
                    program(e, block, hooks)
                    for k in late:
                        block(k, None, lambda n: None)
                    rows_out.wait_last(e, NB)

                @blk.tensor
                def _(e):
                    def rows_T(k, i):
                        rows_in.wait(e, k, i)
                        if i is not None or k >= 1:
                            wait(e, "r_lo", k, i)
                        for c in range(NDC):
                            m = e.transpose(psX[:, c * P:(c + 1) * P], xs[k % 2][:, c * P:(c + 1) * P], ident[:])
                        m.then_inc(S("r_T").sem, 1)

                    def up(k, i):
                        wait(e, "r_lo", k + 1, i)
                        wait(e, "r_wu", k + 1, i)
                        if i is not None or k >= 2:
                            wait(e, "r_mul", k - 1, i)
                        n = 0
                        for c in range(NDC):
                            for wp, xp in PASSES:
                                m = e.matmul(psH[k % 2][:], xsT[k % 2][:, xp, c * P:(c + 1) * P],
                                             wb[:, k % 2, wp, c * D:(c + 1) * D], start=(n == 0),
                                             stop=(n == 3 * NDC - 1))
                                n += 1
                        m.then_inc(S("r_h").sem, 1)

                    def hidden_T(k, i):
                        wait(e, "r_hbl", k + 1, i)
                        if i is not None or k >= 1:
                            wait(e, "r_hT", k, i)
                        for a in range(2):
                            for kt in range(KT):
                                n = a * KT + kt
                                m = e.transpose(psHT[:, n * P:(n + 1) * P], hb[k % 2][:, a, kt * P:(kt + 1) * P],
                                                identb[:])
                        m.then_inc(S("r_HT").sem, 1)

                    def down(k, i):
                        wait(e, "r_hT", k + 1, i)
                        wait(e, "r_wd", k + 1, i)
                        if i is not None or k >= 2:
                            wait(e, "r_yo", k - 1, i)
                        n = 0
                        for kt in range(KT):
                            for wp, hp in PASSES:
                                o = W3OFF + kt * D
                                m = e.matmul(psY[k % 2][:], hT[k % 2][:, hp, kt, :], wb[:, k % 2, wp, o:o + D],
                                             start=(n == 0), stop=(n == 3 * KT - 1))
                                n += 1
                        m.then_inc(S("r_y").sem, 1)

                    def block(k, i, hook):
                        rows_T(k + 1, i)
                        if i is not None or k:
                            hidden_T(k - 1, i)
                        up(k, i)
                        hook(0)
                        if i is not None or k:
                            down(k - 1, i)
                        hook(1)

                    def hooks(second, n, t, first):
                        if second and n == 0:
                            prep.pe_transpose(e, t, first)
                        if second and n == 1:
                            prep.pe_router(e, t, first)

                    rows_T(0, None)
                    program(e, block, hooks)
                    for k in late:
                        block(k, None, (lambda n: prep.pe_ranks(e) if n == 0 else None) if k == LATE + 2
                              else lambda n: None)
                    hidden_T(NB - 1, None)
                    down(NB - 1, None)

                @blk.scalar
                def _(e):
                    def rows_hi(k, i):
                        wait(e, "r_T", k + 1, i)
                        if i is not None or k >= 2:
                            wait(e, "r_h", k - 1, i)
                        e.activation(xsT[k % 2][:, 0, :], psX[:], ACT.Copy).then_inc(S("r_hi").sem, 1)

                    def weights_down(k, i):
                        col = k if i is None else i * 2 + k
                        ex = e.value_load(bexp[0:1, par, bass.ds(col, 1)], min_val=0, max_val=E - 1)
                        if i is not None or k >= 2:
                            wait(e, "r_y", k - 1, i)
                        e.activation(wb[:, k % 2, :, W3OFF:WW],
                                     wr[:, bass.ds(ex, 1), :, W3OFF:WW].rearrange("p o a w -> p (o a) w"),
                                     ACT.Copy).then_inc(S("r_wd").sem, 1)

                    def hidden(k, i):
                        wait(e, "r_h", k + 1, i)
                        if i is not None or k >= 2:
                            wait(e, "r_mul", k - 1, i)
                        e.activation(sg[k % 2], psH[k % 2][:, 0:HC], ACT.Silu).then_inc(S("r_silu").sem, 1)
                        wait(e, "r_mul", k + 1, i)
                        if i is not None or k >= 2:
                            wait(e, "r_HT", k - 1, i)
                        e.activation(hb[k % 2][:, 0, :], hf[k % 2], ACT.Copy).then_inc(S("r_hbh").sem, 1)

                    def result(k, i):
                        wait(e, "r_y", k + 1, i)
                        if i is not None or k >= 2:
                            rows_out.wait(e, k - 2, i)
                        e.activation(yo[k % 2], psY[k % 2][:], ACT.Copy).then_inc(S("r_yo").sem, 1)
                        wait(e, "r_yo", k + 1, i)
                        row = k * P if i is None else i * (2 * P) + k * P
                        e.dma_start(sorted_y[bass.ds(row, P), :], yo[k % 2]).then_inc(rows_out.sem(k), 16)

                    def block(k, i, hook):
                        rows_hi(k + 1, i)
                        weights_down(k, i)
                        hidden(k, i)
                        hook(0)
                        if i is not None or k:
                            result(k - 1, i)

                    def hooks(second, n, t, first):
                        if second:
                            prep.act(e, t, first)
                        else:
                            prep.store(e, t)

                    rows_hi(0, None)
                    program(e, block, hooks)
                    for k in late:
                        block(k, None, (lambda n: prep.act_scores(e)) if k == LATE else lambda n: None)
                    result(NB - 1, None)

                @blk.gpsimd
                def _(e):
                    if prep:
                        prep.pool(e, 0)
                        with e.Fori(0, TILE_TURNS) as i:
                            prep.pool(e, i + 1)

                @blk.vector
                def _(e):
                    o = Own(e, own["dve"])

                    def rows_lo(k, i):
                        wait(e, "r_hi", k + 1, i)
                        e.tensor_tensor(xsT[k % 2][:, 1, :], psX[:], xsT[k % 2][:, 0, :],
                                        ALU.subtract).then_inc(S("r_lo").sem, 1)

                    def weights_up(k, i):
                        col = k if i is None else i * 2 + k
                        ex = e.value_load(bexp[0:1, par, bass.ds(col, 1)], min_val=0, max_val=E - 1)
                        if i is not None or k >= 2:
                            wait(e, "r_h", k - 1, i)
                        e.tensor_copy(wb[:, k % 2, :, 0:W3OFF],
                                      wr[:, bass.ds(ex, 1), :, 0:W3OFF].rearrange("p o a w -> p (o a) w")
                                      ).then_inc(S("r_wu").sem, 1)

                    def hidden(k, i):
                        wait(e, "r_silu", k + 1, i)
                        if i is not None or k >= 2:
                            wait(e, "r_hbl", k - 1, i)
                        e.tensor_tensor(hf[k % 2], psH[k % 2][:, HC:2 * HC], sg[k % 2], ALU.mult).then_inc(
                            S("r_mul").sem, 1)
                        wait(e, "r_hbh", k + 1, i)
                        e.tensor_tensor(hb[k % 2][:, 1, :], hf[k % 2], hb[k % 2][:, 0, :],
                                        ALU.subtract).then_inc(S("r_hbl").sem, 1)

                    def hidden_T(k, i):
                        wait(e, "r_HT", k + 1, i)
                        if i is not None or k >= 2:
                            wait(e, "r_y", k - 1, i)
                        e.tensor_copy(hT[k % 2].rearrange("p a k n -> p (a k n)"), psHT).then_inc(S("r_hT").sem, 1)

                    def block(k, i, hook):
                        rows_lo(k + 1, i)
                        if i is not None or k:
                            hidden_T(k - 1, i)
                        if not (i is None and k == NB - 1):
                            weights_up(k + 1, i)
                        hook(0)
                        hidden(k, i)
                        hook(1)

                    def hooks(second, n, t, first):
                        if not second and n == 1:
                            if not first:
                                prep.vector_logits(e, t - 1)
                            prep.vector_stats(e, o, t)
                        if second and n == 0:
                            prep.vector_norm(e, t, first)
                        if second and n == 1:
                            prep.vector_low(e, t)

                    weights_up(0, None)
                    rows_lo(0, None)
                    if prep is None:
                        block(0, None, lambda n: None)
                        block(1, None, lambda n: None)
                        block(2, None, lambda n: None)
                        with e.Fori(0, (NB - PEEL) // 2 - 1) as i:
                            block(3, i, lambda n: None)
                            block(4, i, lambda n: None)
                        block(NB - 2, None, lambda n: None)
                        block(NB - 1, None, lambda n: None)
                    else:
                        nohook = lambda n: None
                        block(0, None, nohook)
                        block(1, None, lambda n: hooks(0, n, 0, True))
                        block(2, None, lambda n: hooks(1, n, 0, True))
                        per = o.k
                        own["dve"].n += per
                        o.k = 0
                        with e.Fori(0, TILE_TURNS) as i:
                            o.reg = i * per
                            block(3, i, lambda n: hooks(0, n, i + 1, False))
                            block(4, i, lambda n: hooks(1, n, i + 1, False))
                            assert o.k == per
                        o.reg, o.k = None, 0
                        own["dve"].n += per * TILE_TURNS
                        steps = prep.route(e, o)
                        part = -(-len(steps) // (NB - LATE))
                        for k in late:
                            if k == LATE:
                                prep.vector_logits(e, NT - 1)
                            mine = steps[(k - LATE) * part:(k - LATE + 1) * part]
                            block(k, None, lambda n: [s() for s in mine] if n == 1 else None)
                    hidden_T(NB - 1, None)
                    own["dve"].n += o.k
            st.end()
            rows_in.end(NB + 1)
            rows_out.end(NB)
            if prep:
                prep.st.end()

        prepare_alone(0, 0, 0)
        shared(0, split=True)
        routed(0, Prepare(0, 1, 1, banks[6], banks[7]))
        shared(1, fin=Finish(0, 0, 0), images=(0, 1))
        routed(1, Prepare(1, 0, 0, banks[6], banks[7]))
        shared(0, fin=Finish(0, 1, 1), images=(2, 3))
        routed(0, Prepare(1, 1, 1, banks[6], banks[7]))
        shared(1, fin=Finish(1, 0, 0))
        routed(1)
        finish_alone(1, 1, 1)


def kernel(L0_attn_x, L0_attn_qkv_w, L0_attn_conv_w0, L0_attn_conv_b0, L0_attn_conv_w1, L0_attn_conv_b1, L0_attn_proj_w,
           L0_attn_proj_b, L0_attn_ln_w, L0_attn_ln_b, L0_ffn_w12, L0_ffn_w3, L0_ffn_router_w, L0_ffn_expert_bias,
           L0_ffn_sw1, L0_ffn_sw2, L0_ffn_sw3):
    import numpy as np
    import concourse.bacc as bacc
    from concourse.bass_utils import run_bass_kernel_spmd

    A = np.asarray
    B, R, D = L0_attn_x.shape
    E = L0_ffn_w12.shape[0]
    NU = L0_ffn_sw1.shape[0] // 256

    def up_words(w, n):
        w = A(w).reshape(n, -1, D // P, P)
        return w.transpose(0, 3, 2, 1).reshape(n, P, -1)

    def down_words(w, n):
        w = w.reshape(n, D, 2, P)
        return w.transpose(0, 3, 2, 1).reshape(n, P, -1)

    sw3 = A(L0_ffn_sw3).reshape(D, NU, 256).transpose(1, 0, 2)
    wsh = np.concatenate([up_words(L0_ffn_sw1, NU), up_words(L0_ffn_sw2, NU), down_words(sw3, NU)], 2)
    wrt = np.concatenate([up_words(L0_ffn_w12, E), down_words(A(L0_ffn_w3), E)], 2)
    arrays = {
        "x": A(L0_attn_x).reshape(B * R, D),
        "wall": np.concatenate([np.stack([wsh, wrt], 1).reshape(2 * NU, P, -1), wsh[:1]], 0),
        "rwT": A(L0_ffn_router_w).T,
        "ebias": A(L0_ffn_expert_bias),
        "qkvw": A(L0_attn_qkv_w),
        "projw": A(L0_attn_proj_w),
        "projb": A(L0_attn_proj_b),
        "convw": np.concatenate([A(L0_attn_conv_w0)[:, 0, 1, :].T, A(L0_attn_conv_w1)[:, 0, :, 1].T], 1),
        "convb": np.concatenate([A(L0_attn_conv_b0), A(L0_attn_conv_b1)]),
        "lnw": A(L0_attn_ln_w),
        "lnb": A(L0_attn_ln_b),
    }
    nc = bacc.Bacc("TRN2", target_bir_lowering=False, num_devices=1, dynamic_dma_scratch_size=8192)
    arrays = {n: np.ascontiguousarray(a) for n, a in arrays.items()}
    aps = [nc.dram_tensor(n, a.shape, mybir.dt.from_np(a.dtype), kind="ExternalInput").ap() for n, a in arrays.items()]
    out = nc.dram_tensor("out", [B * R, D], F32, kind="ExternalOutput").ap()
    macaron(nc, *aps, out)
    got = run_bass_kernel_spmd(nc, [arrays], core_ids=[0])
    return got.results[0]["out"].reshape(B, R, D)
```

```python
from contextlib import ExitStack

import concourse.bass as bass
from concourse import mybir

ALU = mybir.AluOpType
ACT = mybir.ActivationFunctionType
AX = mybir.AxisListType
F32 = mybir.dt.float32
BF16 = mybir.dt.bfloat16
I32 = mybir.dt.int32

P = 128
EPS = 1e-5


class Count:

    def __init__(self, sem):
        self.sem = sem
        self.n = 0


class Own:

    def __init__(self, eng, count):
        self.eng, self.c, self.k = eng, count, 0

    def do(self, ins):
        ins.then_inc(self.c.sem, 1)
        self.k += 1
        return ins

    def value(self):
        return self.c.n + self.k

    def sync(self):
        if self.value() == 0:
            return
        self.eng.wait_ge(self.c.sem, self.value())


def macaron(nc, x, wall, rwT, ebias, qkvw, projw, projb, convw, convb, lnw, lnb, out):
    ROWS, D = x.shape
    NDC = D // P
    E = rwT.shape[1]
    NU = (wall.shape[0] - 1) // 2
    WW = wall.shape[2]
    HC = 256
    KT = HC // P
    UROWS = 1024
    NT = UROWS // P
    HALF = 512
    TH = HALF // P
    NB = (2 * UROWS + E * (P - 1)) // P
    C = qkvw.shape[0]
    H = C // 2
    WL = 8
    NPI = 8
    NPJ = 16
    NTOK = NPI * NPJ
    NW = NTOK // WL
    SCALE = float(H) ** -0.5
    W3OFF = 2 * NDC * HC
    PASSES = ((0, 0), (0, 1), (1, 0))
    TURN = 8
    NSLOT = NU * 2 * KT
    assert W3OFF + KT * D == WW and NB == 23 and NSLOT == 32 and NU == E

    x1d = nc.dram_tensor("x1d", [ROWS, D], F32).ap()
    xln2 = nc.dram_tensor("xln2", [ROWS, D], F32).ap()
    attd = nc.dram_tensor("attd", [ROWS, D], F32).ap()
    x2d = nc.dram_tensor("x2d", [ROWS, D], F32).ap()
    sorted_x = nc.dram_tensor("sorted_x", [(NB + 1) * P, D], F32).ap()
    sorted_y = nc.dram_tensor("sorted_y", [NB * P, D], F32).ap()
    wsplit = nc.dram_tensor("wsplit", [NU + 1, P, 2 * WW], BF16).ap()

    ctx = ExitStack()
    with ctx:
        def sb(name, shape, dt=F32):
            return ctx.enter_context(nc.sbuf_tensor(name, shape, dt))

        def counter(name):
            return Count(ctx.enter_context(nc.semaphore(name)))

        banks = [ctx.enter_context(nc.psum_tensor(f"bank{i}", [P, 512], F32)) for i in range(8)]

        wr = sb("wr", [P, E, 2, WW], BF16)
        wb = sb("wb", [P, 2, 2, WW], BF16)
        acc = sb("acc", [P, NT, D])
        xT = sb("xT", [P, 2, NDC, UROWS], BF16)
        hs = sb("hs", [P, 2, 2, KT, HALF], BF16)
        TOKW, QKVW = NTOK * C, 3 * NTOK * C
        SMALL = 2 * NW * WL + NTOK
        region = sb("region", [P, 2 * TOKW + QKVW + SMALL + 2 * HALF])
        R_XN, R_QKV, R_SMALL, R_SGH = 0, 2 * TOKW, 2 * TOKW + QKVW, 2 * TOKW + QKVW + SMALL
        ident = sb("ident", [P, P])
        identb = sb("identb", [P, P], BF16)
        tri = sb("tri", [P, P])
        ones = sb("ones", [P, P])
        ones3 = sb("ones3", [3, P], BF16)
        rw = sb("rw", [P, NDC, E])
        eb = sb("eb", [P, E])
        iota8 = sb("iota8", [P, E])
        steps8 = sb("steps8", [P, NT])
        bidx = sb("bidx", [P, NB])
        wqkv = sb("wqkv", [P, 8 * 3 * C])
        wproj = sb("wproj", [P, 8, 2, C])
        bias3 = sb("bias3", [3, 4 * P], BF16)
        cw = sb("cw", [P, 3, C])
        lw = sb("lw", [P, C])
        lb = sb("lb", [P, C])
        nhalf = sb("nhalf", [P, 1])
        mv = sb("mv", [P, 2, 2])
        rstd = sb("rstd", [P, 2, 1])
        stats = sb("stats", [P, 2, 6])
        conv_tmp = sb("conv_tmp", [P, (NW // 2) * (WL - 1) * H])
        scores = sb("scores", [P, NT, E])
        coef = sb("coef", [P, 2, 2, NT])
        slots = sb("slots", [P, 2, 2, NT], I32)
        bexp = sb("bexp", [P, 2, NB], I32)

        own = {n: counter(f"own_{n}") for n in ("dve", "pool")}
        sems = {}

        def S(name):
            if name not in sems:
                sems[name] = counter(name)
            return sems[name]

        class Arrivals:

            def __init__(self, name, per=1, ways=2):
                self.all = [S(f"{name}_{q}") for q in range(ways)]
                self.ways, self.per = ways, 16 * per
                self.base = [c.n for c in self.all]

            def sem(self, k):
                return self.all[k % self.ways].sem

            def wait(self, e, k, i=None, step=2):
                n = self.base[k % self.ways] + self.per * (k // self.ways + 1)
                e.wait_ge(self.sem(k), n if i is None else i * (self.per * step // self.ways) + n)

            def wait_last(self, e, items):
                for k in range(max(0, items - self.ways), items):
                    self.wait(e, k)

            def end(self, items):
                for q in range(self.ways):
                    self.all[q].n += self.per * ((items + self.ways - 1 - q) // self.ways)

        class Stage:

            def __init__(self, **adds):
                self.base = {n: S(n).n for n in adds}
                self.adds = adds

            def sem(self, name):
                return S(name).sem

            def wait(self, e, name, k, i=None, per=2):
                n = self.base[name] + k
                e.wait_ge(S(name).sem, n if i is None else i * per + n)

            def end(self):
                for n, k in self.adds.items():
                    S(n).n += k

        hs_words = hs[:].rearrange("p a b c d -> p (a b c d)").bitcast(F32)

        def words(at, n, dt=F32):
            a = region[:, at:at + n]
            return a if dt == F32 else a.bitcast(dt)

        def buffer_of(n):
            return (n + 1) % 2

        c_in, c_zero = counter("const_loaded"), counter("const_zeroed")
        z_out = counter("zeros_stored")
        raw = [words(R_QKV + q * WW, WW) for q in range(2)]
        raw_in = Arrivals("raw_loaded")
        w_hi, w_lo, w_out = counter("w_high"), counter("w_low"), Arrivals("w_stored")
        x_in, r_in = counter("first_rows_loaded"), counter("router_loaded")
        spare = [wr[:, E - 2 + k].rearrange("p a w -> p (a w)").bitcast(F32) for k in range(2)]
        zero, first_smalls = spare[1][:, 0:D], spare[1][:, D:D + SMALL + 2 * HALF]
        projf, pbf, cbcol, mean8, brow, brest = (spare[0][:, a:a + n] for a, n in (
            (0, P), (P, P), (2 * P, 1), (2 * P + 8, 8), (D, 4 * P), (2 * D, 4 * P)))
        bpart = [spare[0][:, (3 + q) * D:(3 + q) * D + 2 * P].bitcast(BF16) for q in range(3)]

        def split_high(e, n, dst, r=None):
            raw_in.wait(e, n, r, 4)
            e.activation(dst[:, 0, :], raw[n % 2], ACT.Copy).then_inc(w_hi.sem, 1)

        def split_low(e, n, dst, r=None):
            e.wait_ge(w_hi.sem, n + 1 if r is None else r * 4 + (n + 1))
            e.tensor_tensor(dst[:, 1, :], raw[n % 2], dst[:, 0, :], ALU.subtract).then_inc(w_lo.sem, 1)

        def load_raw(e, n, r=None):
            if r is not None or n >= 2:
                e.wait_ge(w_lo.sem, n - 1 if r is None else r * 4 + (n - 1))
            row = n if r is None else r * 4 + n
            e.dma_start(raw[n % 2], wall[bass.ds(row, 1)].rearrange("o p w -> (o p) w")).then_inc(raw_in.sem(n), 16)

        with nc.Block() as blk:
            @blk.gpsimd
            def _(e):
                o = Own(e, own["pool"])
                o.do(e.memset(wqkv[:], 0.0))
                o.do(e.memset(projf, 0.0))
                o.do(e.memset(zero, 0.0))
                o.do(e.memset(ones[:], 1.0))
                o.do(e.memset(ones3[:], 1.0))
                o.do(e.memset(nhalf[:], -0.5))
                o.do(e.iota(iota8[:], pattern=[[1, E]], base=-E, channel_multiplier=0, allow_small_or_imprecise_dtypes=True))
                o.do(e.iota(steps8[:], pattern=[[P, NT]], base=0, channel_multiplier=0, allow_small_or_imprecise_dtypes=True))
                o.do(e.iota(bidx[:], pattern=[[1, NB]], base=0, channel_multiplier=0, allow_small_or_imprecise_dtypes=True))
                o.sync()
                e.engine_nop().then_inc(c_zero.sem, 1)
                o.do(e.affine_select(out=ident[:], in_=ones[:], pattern=[[-1, P]], compare_op=ALU.is_equal,
                                     fill=0.0, base=0, channel_multiplier=1))
                o.do(e.affine_select(out=tri[:], in_=ones[:], pattern=[[1, P]], compare_op=ALU.is_gt,
                                     fill=0.0, base=0, channel_multiplier=-1))
                o.sync()
                o.do(e.tensor_copy(identb[:], ident[:]))
                o.sync()
                own["pool"].n += o.k

            @blk.sync
            def _(e):
                e.dma_start(acc[:], x[0:UROWS, :].rearrange("(t p) d -> p t d", p=P)).then_inc(x_in.sem, 16)
                load_raw(e, 0)
                load_raw(e, 1)

            @blk.scalar
            def _(e):
                c = c_in

                def load(dst, src):
                    e.dma_start(dst, src).then_inc(c.sem, 16)
                    c.n += 16

                e.dma_start(rw[:], rwT.rearrange("(c p) e -> p c e", p=P)).then_inc(r_in.sem, 16)
                for dst, src in ((eb[:], ebias), (lw[:], lnw), (lb[:], lnb)):
                    load(dst, src.partition_broadcast(P))
                load(cw[:].rearrange("p a c -> p (a c)"), convw.rearrange("a c -> (a c)").partition_broadcast(P))
                e.wait_ge(c_zero.sem, 1)
                for t in range(8):
                    rows = slice(C * t, C * t + C)
                    load(wqkv[rows, 3 * C * t:3 * C * t + 3 * C], qkvw)
                    load(projf[rows, rows], projw)
                load(pbf[0:1, :], projb)
                load(cbcol, convb)

        def bias_product(e):
            e.wait_ge(c_in.sem, c_in.n)
            e.matmul(banks[6][0:1, 0:P], cbcol, projf, start=True, stop=True).then_inc(S("bias_proj").sem, 1)

        def bias_move(e):
            e.wait_ge(S("bias_parts").sem, 1)
            for q in range(3):
                e.dma_start(bias3[q:q + 1, :], bpart[q][0:1, :]).then_inc(S("bias_moved").sem, 16)
            e.wait_ge(S("bias_moved").sem, 48)

        def attention_constants(e, o):
            w4 = projf.rearrange("p (t c) -> p t c", t=8)
            full = [P, 8, C]

            def centre(dst, src, n, m):
                o.do(e.tensor_reduce(m, src, AX.X, ALU.add))
                o.sync()
                o.do(e.tensor_scalar(m, m, 1.0 / C, None, ALU.mult))
                o.sync()
                o.do(e.tensor_tensor(dst, src, m[:, :, None].to_broadcast([n, 8, C]), ALU.subtract))
                o.sync()

            e.wait_ge(S("bias_proj").sem, 1)
            o.do(e.tensor_tensor(pbf[0:1, :], pbf[0:1, :], banks[6][0:1, 0:P], ALU.add))
            o.sync()
            centre(wproj[:, :, 0, :], w4, P, mean8)
            o.do(e.tensor_tensor(wproj[:, :, 1, :], wproj[:, :, 0, :], lw[:][:, None, :].to_broadcast(full), ALU.mult))
            b4 = brow.rearrange("p (g t s c) -> p g t s c", g=2, t=8, s=2)
            for g in range(2):
                centre(b4[0:1, g, :, 0, :], pbf[0:1, :].rearrange("p (t c) -> p t c", t=8), 1, mean8[0:1, :])
                o.do(e.tensor_tensor(b4[0:1, g, :, 1, :], b4[0:1, g, :, 0, :],
                                     lw[0:1, :][:, None, :].to_broadcast([1, 8, C]), ALU.mult))
                o.sync()
            src = brow
            for q in range(3):
                o.do(e.tensor_copy(bpart[q][0:1, :], src[0:1, :]))
                o.sync()
                if q < 2:
                    o.do(e.tensor_tensor(brest[0:1, :], src[0:1, :], bpart[q][0:1, :], ALU.subtract))
                    o.sync()
                    src = brest
            e.engine_nop().then_inc(S("bias_parts").sem, 1)

        class Prepare:

            def __init__(self, f, u, par, banks_t, bank_r, preloaded=False):
                self.f, self.r0, self.par = f, u * UROWS, par
                self.psT, self.psR = banks_t, bank_r
                self.preloaded = preloaded
                if preloaded:
                    self.smalls = first_smalls
                else:
                    self.smalls = words(R_SMALL, SMALL + 2 * HALF)
                self.msum = self.smalls[:, 0:NT * E].rearrange("p (t e) -> p t e", t=NT)
                self.att, self.pool_att = S("t_st").n - 1024, S("t_pst").n
                self.xn = words(R_XN, NT * D).rearrange("p (t d) -> p t d", t=NT)
                self.xr, self.ar, self.xc, self.xT32 = (hs_words[:, q * D:(q + 1) * D] for q in range(4))
                self.st = Stage(p_x=0 if preloaded else 32 * NT if f else 16 * NT, p_xs=16 * NT * f, p_var=NT, p_rstd=NT, p_xc=NT, p_xn=NT,
                                p_T=NT, p_t32=NT, p_hi=NT, p_lo=NT, p_R=NT, p_log=NT, p_x2=NT * f, p_sc=1, p_m=1,
                                p_k=1, p_slot=1)

            def at(self, t, per=1, plus=0):
                return t * per + plus

            def wait(self, e, name, t, per=1, plus=0):
                n = self.st.base[name] + per * (1 + plus)
                e.wait_ge(S(name).sem, t * per + n)

            def rows(self, t):
                return bass.ds(t * P + self.r0, P)

            def sync(self, e, t, first):
                if first and self.f:
                    e.wait_ge(S("t_st").sem, self.att)
                    e.wait_ge(S("t_pst").sem, self.pool_att)
                if not first:
                    self.wait(e, "p_xc", t, 1, -1)
                    if self.f:
                        self.wait(e, "p_xs", t, 16, -1)
                src = x1d if self.f else x
                e.dma_start(self.xr, src[self.rows(t), :]).then_inc(S("p_x").sem, 16)
                if self.f:
                    e.dma_start(self.ar, attd[self.rows(t), :]).then_inc(S("p_x").sem, 16)

            def store(self, e, t):
                if self.f:
                    self.wait(e, "p_x2", t)
                    e.dma_start(x2d[self.rows(t), :], self.xr).then_inc(S("p_xs").sem, 16)

            def vector_stats(self, e, o, t):
                if self.preloaded:
                    e.wait_ge(x_in.sem, 16)
                else:
                    self.wait(e, "p_x", t, 32 if self.f else 16)
                if self.f:
                    e.tensor_tensor(self.xr, self.xr, self.ar, ALU.add).then_inc(S("p_x2").sem, 1)
                    self.wait(e, "p_x2", t)
                q = t % 2
                o.do(e.bn_stats(stats[:, q, :], self.row(t)))
                o.sync()
                o.do(e.bn_aggr(mv[:, q, :], stats[:, q, :]))
                o.sync()
                e.tensor_scalar(mv[:, q, 1:2], mv[:, q, 1:2], EPS, None, ALU.add).then_inc(S("p_var").sem, 1)

            def row(self, t):
                return acc[:, t, :] if self.preloaded else self.xr

            def vector_norm(self, e, t, first):
                if not first:
                    self.wait(e, "p_T", t, 1, -1)
                    self.wait(e, "p_xn", t, 1, -1)
                self.wait(e, "p_rstd", t)
                e.tensor_scalar(self.xc, self.row(t), mv[:, t % 2, 0:1], rstd[:, t % 2, :], ALU.subtract,
                                ALU.mult).then_inc(S("p_xc").sem, 1)

            def vector_low(self, e, t):
                self.wait(e, "p_hi", t)
                e.tensor_tensor(xT[:, 1, :, bass.ds(t * P, P)], self.psT[t % len(self.psT)][:].rearrange("p (c r) -> p c r", c=NDC),
                                xT[:, 0, :, bass.ds(t * P, P)], ALU.subtract).then_inc(S("p_lo").sem, 1)

            def vector_logits(self, e, t):
                self.wait(e, "p_R", t)
                e.tensor_copy(scores[:, bass.ds(t, 1), :].rearrange("p o e -> p (o e)"),
                              self.psR[:, 0:E]).then_inc(S("p_log").sem, 1)

            def pool(self, e, t):
                self.pool_rstd(e, t)
                self.pool_keep(e, t)

            def pool_rstd(self, e, t):
                self.wait(e, "p_var", t)
                e.tensor_tensor(rstd[:, t % 2, :], mv[:, t % 2, 1:2], nhalf[:], ALU.pow).then_inc(S("p_rstd").sem, 1)

            def pool_keep(self, e, t):
                self.wait(e, "p_xc", t)
                e.tensor_copy(self.xn[:, bass.ds(t, 1), :].rearrange("p o d -> p (o d)"),
                              self.xc).then_inc(S("p_xn").sem, 1)

            def pe_transpose(self, e, t, first):
                self.wait(e, "p_xc", t)
                if not first:
                    self.wait(e, "p_lo", t, 1, -len(self.psT))
                for c in range(NDC):
                    m = e.transpose(self.psT[t % len(self.psT)][:, c * P:(c + 1) * P], self.xc[:, c * P:(c + 1) * P], ident[:])
                m.then_inc(S("p_T").sem, 1)

            def act(self, e, t, first):
                self.wait(e, "p_T", t)
                if not first:
                    self.wait(e, "p_R", t, 1, -1)
                e.activation(self.xT32, self.psT[t % len(self.psT)][:], ACT.Copy).then_inc(S("p_t32").sem, 1)
                e.activation(xT[:, 0, :, bass.ds(t * P, P)], self.psT[t % len(self.psT)][:].rearrange("p (c r) -> p c r", c=NDC),
                             ACT.Copy).then_inc(S("p_hi").sem, 1)

            def pe_router(self, e, t, first):
                self.wait(e, "p_t32", t)
                if not first:
                    self.wait(e, "p_log", t, 1, -1)
                for c in range(NDC):
                    m = e.matmul(self.psR[:, 0:E], self.xT32[:, c * P:(c + 1) * P], rw[:, c, :],
                                 start=(c == 0), stop=(c == NDC - 1))
                m.then_inc(S("p_R").sem, 1)

            def act_scores(self, e):
                self.st.wait(e, "p_log", NT)
                e.activation(scores[:], scores[:], ACT.Sigmoid).then_inc(S("p_sc").sem, 1)

            def pe_ranks(self, e):
                self.st.wait(e, "p_m", 1)
                msum = self.msum.rearrange("p t e -> p (t e)")
                e.matmul(self.psR[:, 64:64 + NT * E], tri[:], msum, start=True, stop=True)
                e.matmul(self.psR[:, 128:128 + NT * E], ones[:], msum, start=True, stop=True,
                         skip_group_check=True).then_inc(S("p_k").sem, 1)

            def route(self, e, o):
                at = [NT * E]

                def small(*shape):
                    n = 1
                    for k in shape:
                        n *= k
                    a = self.smalls[:, at[0]:at[0] + n]
                    at[0] += n
                    assert at[0] <= SMALL + 2 * HALF
                    if len(shape) == 2:
                        return a.rearrange("p (a b) -> p a b", a=shape[0])
                    return a

                sel, eq, sel2, rank = (small(NT, E) for _ in range(4))
                oh = [small(NT, E) for _ in range(2)]
                msum = self.msum
                tp = small(NT + 1, E)
                mx, mn, den, slotf = (small(NT) for _ in range(4))
                wsel = [small(NT) for _ in range(2)]
                c8 = sel
                nblk, bend = small(E), small(E)
                cmpb = small(NB, E)
                bexpf = small(NB)
                big = [P, NT, E]
                par = self.par
                steps, parts = [], []

                def over_e(a):
                    return a[:, None, :].to_broadcast(big)

                def over_t(a):
                    return a[:, :, None].to_broadcast(big)

                def step(fn):
                    steps.append(fn)

                def do(*ops):
                    for op in ops:
                        def one(op=op):
                            o.do(op())
                            o.sync()
                        steps.append(one)

                step(lambda: self.st.wait(e, "p_sc", 1))
                do(lambda: e.tensor_tensor(sel, scores[:], over_e(eb[:]), ALU.add))
                for k in range(2):
                    cur = (sel, sel2)[k]
                    do(lambda cur=cur: e.tensor_reduce(mx, cur, AX.X, ALU.max),
                       lambda cur=cur: e.tensor_tensor(eq, cur, over_t(mx), ALU.is_ge),
                       lambda: e.tensor_tensor(eq, eq, over_e(iota8[:]), ALU.mult),
                       lambda: e.tensor_reduce(mn, eq, AX.X, ALU.min),
                       lambda k=k: e.tensor_tensor(oh[k], over_e(iota8[:]), over_t(mn), ALU.is_equal),
                       lambda k=k: e.tensor_tensor(eq, oh[k], scores[:], ALU.mult),
                       lambda k=k: e.tensor_reduce(wsel[k], eq, AX.X, ALU.add))
                    if k == 0:
                        do(lambda: e.tensor_scalar(sel2, oh[0], -1e30, None, ALU.mult),
                           lambda: e.tensor_tensor(sel2, sel2, sel, ALU.add))
                step(lambda: e.tensor_tensor(msum, oh[0], oh[1], ALU.add).then_inc(S("p_m").sem, 1))
                parts.append(len(steps))
                do(lambda: e.tensor_tensor(den, wsel[0], wsel[1], ALU.add),
                   lambda: e.tensor_scalar(den, den, 1e-9, None, ALU.add),
                   lambda: e.reciprocal(den, den),
                   lambda: e.tensor_tensor(coef[:, par, 0, :], wsel[0], den, ALU.mult),
                   lambda: e.tensor_tensor(coef[:, par, 1, :], wsel[1], den, ALU.mult))
                tot = self.psR[:, 128:128 + NT * E].rearrange("p (t e) -> p t e", t=NT)
                inside = self.psR[:, 64:64 + NT * E].rearrange("p (t e) -> p t e", t=NT)
                do(lambda: e.memset(tp[:, 0, :], 0.0))
                parts.append(len(steps))
                step(lambda: self.st.wait(e, "p_k", 1))
                for t in range(NT):
                    do(lambda t=t: e.tensor_tensor(tp[:, t + 1, :], tp[:, t, :], tot[:, t, :], ALU.add))
                do(lambda: e.tensor_tensor(c8, tp[:, NT, :][:, :, None].to_broadcast([P, E, NT]),
                                           steps8[:][:, None, :].to_broadcast([P, E, NT]), ALU.is_gt),
                   lambda: e.tensor_reduce(nblk, c8, AX.X, ALU.add),
                   lambda: e.tensor_copy(bend[:, 0:1], nblk[:, 0:1]))
                for k in range(1, E):
                    do(lambda k=k: e.tensor_tensor(bend[:, k:k + 1], bend[:, k - 1:k], nblk[:, k:k + 1], ALU.add))
                do(lambda: e.tensor_tensor(cmpb, bidx[:][:, :, None].to_broadcast([P, NB, E]),
                                           bend[:, None, :].to_broadcast([P, NB, E]), ALU.is_ge),
                   lambda: e.tensor_reduce(bexpf, cmpb, AX.X, ALU.add),
                   lambda: e.tensor_scalar(bexp[:, par, :], bexpf, float(E - 1), None, ALU.min),
                   lambda: e.tensor_tensor(nblk, bend, nblk, ALU.subtract),
                   lambda: e.tensor_scalar(nblk, nblk, float(P), None, ALU.mult),
                   lambda: e.tensor_tensor(rank, tp[:, 0:NT, :], inside, ALU.add),
                   lambda: e.tensor_tensor(rank, rank, over_e(nblk), ALU.add))
                for k in range(2):
                    do(lambda k=k: e.tensor_tensor(eq, oh[k], rank, ALU.mult),
                       lambda: e.tensor_reduce(slotf, eq, AX.X, ALU.add),
                       lambda k=k: e.tensor_copy(slots[:, par, k, :], slotf))
                step(lambda: e.engine_nop().then_inc(S("p_slot").sem, 1))
                return steps[:parts[0]], steps[parts[0]:parts[1]], steps[parts[1]:]

        def prepare_alone():
            p = Prepare(0, 0, 0, banks[0:2], banks[7], preloaded=True)
            with nc.Block() as blk:
                @blk.sync
                def _(e):
                    for b in range(NB + 1):
                        e.dma_start(sorted_x[b * P:(b + 1) * P, :], zero).then_inc(z_out.sem, 16)
                        z_out.n += 16

                @blk.tensor
                def _(e):
                    e.wait_ge(r_in.sem, 16)
                    for t in range(NT):
                        p.pe_transpose(e, t, t < 2)
                        if t:
                            p.pe_router(e, t - 1, t == 1)
                    p.pe_router(e, NT - 1, False)

                @blk.scalar
                def _(e):
                    split_high(e, 0, wb[:, buffer_of(0)])
                    for t in range(NT):
                        p.act(e, t, t == 0)

                @blk.gpsimd
                def _(e):
                    for t in range(NT):
                        p.pool_rstd(e, t)
                        if t:
                            p.pool_keep(e, t - 1)
                    p.pool_keep(e, NT - 1)

                @blk.vector
                def _(e):
                    o = Own(e, own["dve"])
                    p.vector_stats(e, o, 0)
                    for t in range(NT):
                        p.vector_norm(e, t, t == 0)
                        if t < NT - 1:
                            p.vector_stats(e, o, t + 1)
                        p.vector_low(e, t)
                        if t:
                            p.vector_logits(e, t - 1)
                    p.vector_logits(e, NT - 1)
                    split_low(e, 0, wb[:, buffer_of(0)])
                    own["dve"].n += o.k

            return p

        class Finish:
            WAYS = 4

            def __init__(self, f, u, par):
                self.f, self.r0, self.par = f, u * UROWS, par
                self.buf = [[words(R_QKV + (3 * q + k) * D, D) for k in range(3)] for q in range(self.WAYS)]
                self.src, self.dst = (x, x1d) if f == 0 else (x2d, out)
                self.rows_in = Arrivals("f_rows_loaded", 1, self.WAYS)
                self.y_in = Arrivals("f_y_gathered", 2, self.WAYS)
                self.rows_out = Arrivals("f_rows_stored", 1 if f else 2, self.WAYS)
                ln = NT * (f == 0)
                self.st = Stage(f_sum=NT, f_var=ln, f_rstd=ln, f_ln=ln)

            def rows(self, t):
                return slice(self.r0 + t * P, self.r0 + (t + 1) * P)

            def pool_gather(self, e, t):
                if t >= self.WAYS:
                    self.rows_out.wait(e, t - self.WAYS)
                for k in range(2):
                    e.indirect_dma_start(out=self.buf[t % self.WAYS][k], out_offset=None, in_=sorted_y,
                                         in_offset=bass.IndirectOffsetOnAxis(ap=slots[:, self.par, k, t:t + 1], axis=0)
                                         ).then_inc(self.y_in.sem(t), 16)

            def pool_rstd(self, e, t):
                if self.f == 0:
                    self.st.wait(e, "f_var", t + 1)
                    e.tensor_tensor(rstd[:, t % 2, :], mv[:, t % 2, 1:2], nhalf[:],
                                    ALU.pow).then_inc(S("f_rstd").sem, 1)

            def sync_load(self, e, t):
                if t >= self.WAYS:
                    self.rows_out.wait(e, t - self.WAYS)
                e.dma_start(self.buf[t % self.WAYS][2], self.src[self.rows(t), :]).then_inc(self.rows_in.sem(t), 16)

            def store(self, e, t):
                self.st.wait(e, "f_sum", t + 1)
                e.dma_start(self.dst[self.rows(t), :], self.buf[t % self.WAYS][2]).then_inc(self.rows_out.sem(t), 16)
                if self.f == 0:
                    self.st.wait(e, "f_ln", t + 1)
                    e.dma_start(xln2[self.rows(t), :], self.buf[t % self.WAYS][0]).then_inc(self.rows_out.sem(t), 16)

            def vector_sum(self, e, o, t):
                a, b, r = self.buf[t % self.WAYS]
                self.y_in.wait(e, t)
                self.rows_in.wait(e, t)
                o.do(e.scalar_tensor_tensor(out=a, in0=a, scalar=coef[:, self.par, 0, t:t + 1], in1=acc[:, t, :],
                                            op0=ALU.mult, op1=ALU.add))
                o.sync()
                o.do(e.scalar_tensor_tensor(out=b, in0=b, scalar=coef[:, self.par, 1, t:t + 1], in1=a,
                                            op0=ALU.mult, op1=ALU.add))
                o.sync()
                e.scalar_tensor_tensor(out=r, in0=b, scalar=0.5, in1=r, op0=ALU.mult,
                                       op1=ALU.add).then_inc(S("f_sum").sem, 1)
                if self.f == 0:
                    self.st.wait(e, "f_sum", t + 1)
                    o.do(e.bn_stats(stats[:, t % 2, :], r))
                    o.sync()
                    o.do(e.bn_aggr(mv[:, t % 2, :], stats[:, t % 2, :]))
                    o.sync()
                    e.tensor_scalar(mv[:, t % 2, 1:2], mv[:, t % 2, 1:2], EPS, None, ALU.add).then_inc(S("f_var").sem, 1)

            def vector_norm(self, e, t):
                if self.f == 0:
                    a, _, r = self.buf[t % self.WAYS]
                    self.st.wait(e, "f_rstd", t + 1)
                    e.tensor_scalar(a, r, mv[:, t % 2, 0:1], rstd[:, t % 2, :], ALU.subtract,
                                    ALU.mult).then_inc(S("f_ln").sem, 1)

            def end(self):
                for a in (self.rows_in, self.y_in, self.rows_out):
                    a.end(NT)
                self.st.end()

        def finish_alone(f, u, par):
            fin = Finish(f, u, par)
            with nc.Block() as blk:
                @blk.gpsimd
                def _(e):
                    for t in range(NT):
                        fin.pool_gather(e, t)
                        if t >= 2:
                            fin.pool_rstd(e, t - 2)
                    fin.pool_rstd(e, NT - 2)
                    fin.pool_rstd(e, NT - 1)

                @blk.sync
                def _(e):
                    for t in range(NT):
                        fin.sync_load(e, t)
                    fin.rows_out.wait_last(e, NT)

                @blk.scalar
                def _(e):
                    for t in range(NT):
                        fin.store(e, t)

                @blk.vector
                def _(e):
                    o = Own(e, own["dve"])
                    for t in range(NT):
                        fin.vector_sum(e, o, t)
                        if t:
                            fin.vector_norm(e, t - 1)
                    fin.vector_norm(e, NT - 1)
                    own["dve"].n += o.k
            fin.end()


        QUEUED = 44
        PROJ_AT, SCORES, SOFTMAX, VALUES, MERGE = 3, 0.5, 1.5, 0.7, 1.0

        class Attention:

            def __init__(self, b, first_slot, raw_at, load_at, ready, turn_ready, qkv_ready, scores_ready, store):
                self.ready, self.turn_ready = ready, turn_ready
                self.qkv_ready, self.scores_ready = qkv_ready, scores_ready
                self.tok = words(0, TOKW)
                self.sco = words(TOKW, TOKW)
                self.qkv = words(R_QKV, QKVW)
                self.small = words(R_SMALL, 2 * NW * WL)
                self.small2 = words(R_SMALL + 2 * NW * WL, NTOK)
                self.tmp = [self.tok[:, k * TOKW // 2:(k + 1) * TOKW // 2] for k in range(2)]
                self.sq, self.dl = (self.qkv[:, k * TOKW:(k + 1) * TOKW] for k in range(2))
                self.done = self.sco
                self.raw = self.qkv[:, raw_at:raw_at + TOKW]
                self.img = xln2[b * 512:(b + 1) * 512, :].rearrange("r c -> (r c)").rearrange(
                    "(s i g e) -> g s i e", s=16, i=NPI, g=8)
                self.res = attd[b * 512:(b + 1) * 512, :].rearrange("r c -> (r c)").rearrange(
                    "(c s i g j) -> g i s c j", c=C, s=16, i=NPI, g=8)
                self.q4 = self.qkv.rearrange("p (i j c) -> p i j c", i=NPI, j=NPJ)
                self.q3 = self.qkv.rearrange("p (t c) -> p t c", c=3 * C)
                self.s5 = self.sco.rearrange("p (r w a b) -> p r w a b", r=2, w=NW, a=WL)
                self.st = Stage(t_x=128, t_x2=128, t_T=4, t_Tc=4, t_q=16, t_qc=16, t_pp=16, t_rd=16, t_k=1, t_s=1, t_e=1,
                                t_cv=1, t_sum=1, t_oT=4, t_oTc=4, t_pr=8, t_prc=8, t_var=1, t_std=1, t_tb=1, t_out=1,
                                t_st=16 * (QUEUED if store else 64), t_pst=16 * (64 - QUEUED if store else 0))
                self.pe, self.act, self.vec, self.pool, self.sp = {}, {}, {}, {}, {}
                self.table = {"pe": self.pe, "act": self.act, "vec": self.vec, "pool": self.pool, "sp": self.sp}
                self.schedule(first_slot, raw_at, load_at, store)

            def window(self, r, lo, n):
                if r == 0:
                    return self.q3[:, :, lo:lo + n].rearrange("p (w a) c -> p w a c", a=WL)
                return self.q4[:, :, :, lo:lo + n].rearrange("p a w c -> p w a c")

            def put(self, table, slot, pos, fn):
                table.setdefault((slot, pos), []).append(fn)

            def schedule(self, s0, raw_at, load_at, store):
                def pair(steps, places):
                    for n, (pe, act, k) in enumerate(steps):
                        at = places[n * len(places) // len(steps)]
                        self.put(self.pe, *at, lambda e, pe=pe, k=k: pe(e, k))
                        self.put(self.act, *at, lambda e, act=act, k=k: act(e, k))

                places = [(s0, 3)] if raw_at == 0 else [(s0, 1), (s0, 2), (s0, 3)]
                self.put(self.sp, *load_at, self.sp_load)
                pair([(self.pe_turn, self.act_turn, m) for m in range(4)] +
                     [(self.pe_qkv, self.act_qkv, g) for g in range(16)], places)
                steps = [(SCORES, [lambda e, o, a=a: self.vec_scores(e, o, a)],
                          [lambda e, o, a=a: self.pool_scores(e, o, a)]) for a in range(WL)]
                steps += [(SOFTMAX, [self.vec_softmax, self.vec_sums],
                           [self.pool_conv_centre] + [lambda e, o, k=k: self.pool_conv(e, o, k) for k in range(2)])]
                for a in range(WL):
                    steps += [(VALUES, [lambda e, o, a=a: self.vec_values(e, o, a)],
                               [lambda e, o, a=a: self.pool_values(e, o, a)] +
                               [lambda e, o, k=k: self.pool_conv(e, o, k) for k in range(a + 2, a + 3) if k < 8])]
                steps += [(MERGE, [self.vec_merge], [])]
                slot, used = (s0, 0.7)
                for share, vec, pool in steps:
                    if used + share / 2 > 1:
                        slot, used = slot + 1, used - 1
                    used += share
                    for fn in vec:
                        self.put(self.vec, slot, 0, fn)
                    for fn in pool:
                        self.put(self.pool, slot, 0, fn)
                    if share == SOFTMAX:
                        self.put(self.act, slot, 1, self.act_exp)
                self.merged = slot
                slot += 1
                self.put(self.sp, slot, 0, self.sp_reload)
                self.put(self.pool, slot, 0, self.pool_residual)
                pair([(self.pe_turn2, self.act_turn2, m) for m in range(4)] +
                     [(self.pe_proj, self.act_proj, h) for h in range(8)], [(slot, PROJ_AT)])
                self.put(self.vec, slot, 0, self.vec_norm)
                self.put(self.act, slot, 3, self.act_std)
                if store:
                    half = (QUEUED + 64) // 2
                    self.put(self.sp, slot, 0, lambda e: self.store(e, 0, QUEUED))
                    self.put(self.pool, slot, 0, lambda e, o: self.store(e, QUEUED, half, "t_pst"))
                    self.put(self.pool, slot + 1, 0, lambda e, o: self.store(e, half, 64, "t_pst"))
                self.last = slot

            def pe_turn(self, e, m):
                if m == 0:
                    self.st.wait(e, "t_x", 128)
                    e.wait_ge(S("t_prc").sem, self.st.base["t_prc"])
                if m >= 2:
                    self.st.wait(e, "t_Tc", m - 1)
                for n in range(4):
                    g = 4 * m + n
                    mm = e.transpose(self.ps(m)[:, n * P:(n + 1) * P], self.raw[:, g * P:(g + 1) * P], ident[:])
                mm.then_inc(S("t_T").sem, 1)

            def pe_qkv(self, e, g):
                self.st.wait(e, "t_Tc", max(g // 4 + 1, min(g + 3, 4)))
                if g >= 2:
                    self.st.wait(e, "t_qc", g - 1)
                e.matmul(self.ps(g)[:, 0:24 * C], self.tokT(0, g // 4)[:, (g % 4) * P:(g % 4 + 1) * P], wqkv[:],
                         start=True, stop=True).then_inc(S("t_q").sem, 1)

            def ps(self, n):
                return banks[6 + n % 2]

            def tokT(self, phase, m):
                buf = self.sco if phase else self.tok
                return buf[:, m * 512:(m + 1) * 512]

            def pe_turn2(self, e, m):
                if m == 0:
                    self.st.wait(e, "t_sum", 1)
                if m >= 2:
                    self.st.wait(e, "t_oTc", m - 1)
                for n in range(4):
                    g = 4 * m + n
                    mm = e.transpose(self.ps(m)[:, n * P:(n + 1) * P], self.sco[:, g * P:(g + 1) * P], ident[:])
                mm.then_inc(S("t_oT").sem, 1)

            def pe_proj(self, e, h):
                self.st.wait(e, "t_oTc", max(h // 2 + 1, min(h + 3, 4)))
                if h >= 2:
                    self.st.wait(e, "t_prc", h - 1)
                e.matmul(self.ps(h)[:], ones3[:], bias3[:], start=True, stop=False)
                for n in range(2):
                    g = 2 * (h % 2) + n
                    mm = e.matmul(self.ps(h)[:, n * 2 * P:(n + 1) * 2 * P], self.tokT(1, h // 2)[:, g * P:(g + 1) * P],
                                  wproj[:].rearrange("p t s c -> p (t s c)"), start=False, stop=(n == 1))
                mm.then_inc(S("t_pr").sem, 1)

            def sp_load(self, e):
                self.ready(e)
                for g in range(8):
                    e.dma_start(self.raw[g:P:8, :].rearrange("p (i e) -> p i e", i=NPI), self.img[g]).then_inc(S("t_x").sem, 16)

            def act_turn(self, e, m):
                self.st.wait(e, "t_T", m + 1)
                if m == 0:
                    self.turn_ready(e)
                e.activation(self.tokT(0, m), self.ps(m)[:], ACT.Copy).then_inc(S("t_Tc").sem, 1)

            def act_qkv(self, e, g):
                if g == 0:
                    self.qkv_ready(e)
                self.st.wait(e, "t_q", g + 1)
                e.activation(self.qkv[:, g * 24 * C:(g + 1) * 24 * C], self.ps(g)[:, 0:24 * C],
                             ACT.Copy).then_inc(S("t_qc").sem, 1)

            def act_exp(self, e):
                self.st.wait(e, "t_s", 1)
                e.activation(self.sco, self.sco, ACT.Exp, scale=SCALE).then_inc(S("t_e").sem, 1)

            def sp_reload(self, e):
                self.st.wait(e, "t_sum", 1)
                for g in range(8):
                    e.dma_start(self.tok[g:P:8, :].rearrange("p (i e) -> p i e", i=NPI), self.img[g]).then_inc(S("t_x2").sem, 16)

            def act_std(self, e):
                self.st.wait(e, "t_var", 1)
                e.activation(self.small2, self.small2, ACT.Sqrt).then_inc(S("t_std").sem, 1)

            def act_turn2(self, e, m):
                self.st.wait(e, "t_oT", m + 1)
                e.activation(self.tokT(1, m), self.ps(m)[:], ACT.Copy).then_inc(S("t_oTc").sem, 1)

            def act_proj(self, e, h):
                self.st.wait(e, "t_pr", h + 1)
                two = self.ps(h)[:].rearrange("p (t s c) -> p t s c", s=2, c=C)
                cols = slice(h * 2 * P, (h + 1) * 2 * P)
                e.activation(self.sq[:, cols].rearrange("p (t c) -> p t c", c=C), two[:, :, 0, :], ACT.Square)
                e.activation(self.dl[:, cols].rearrange("p (t c) -> p t c", c=C), two[:, :, 1, :],
                             ACT.Copy).then_inc(S("t_prc").sem, 1)

            def store(self, e, lo, hi, name="t_st"):
                self.st.wait(e, "t_out", 1)
                done = self.done.rearrange("p (c i j) -> p i c j", c=C, i=NPI)
                for n in range(lo, hi):
                    g, i = n // NPI, n % NPI
                    e.dma_start(self.res[g, i], done[g:P:8, i]).then_inc(S(name).sem, 16)

            def product(self, e, r, a, values):
                t = self.tmp[r]
                if values:
                    t = t.rearrange("p (w c b) -> p w c b", w=NW, c=H)
                    x0 = self.s5[:, r, :, a:a + 1, :].to_broadcast([P, NW, H, WL])
                    x1 = self.window(r, 2 * C + H * r, H).rearrange("p w b c -> p w c b")
                else:
                    t = t.rearrange("p (w b c) -> p w b c", w=NW, b=WL)
                    x0 = self.window(r, H * r, H)[:, :, a:a + 1, :].to_broadcast([P, NW, WL, H])
                    x1 = self.window(r, C + H * r, H)
                return e.tensor_tensor(t, x0, x1, ALU.mult)

            def vec_pair(self, e, o, a, values):
                o.sync()
                o.do(self.product(e, 0, a, values))
                o.sync()
                for r in range(2):
                    t = self.tmp[r].rearrange("p (w b c) -> p w b c", w=NW, b=WL)
                    dst = self.window(r, H * r, H)[:, :, a, :] if values else self.s5[:, r, :, a, :]
                    if r == 1:
                        self.st.wait(e, "t_pp", WL * values + a + 1)
                    ins = e.tensor_reduce(dst, t, AX.X, ALU.add)
                    if r == 0:
                        o.do(ins)
                    else:
                        ins.then_inc(S("t_rd").sem, 1)

            def vec_scores(self, e, o, a):
                if a == 0:
                    self.st.wait(e, "t_qc", 16)
                    self.scores_ready(e)
                self.vec_pair(e, o, a, 0)
                if a == WL - 1:
                    o.sync()
                    e.engine_nop().then_inc(S("t_k").sem, 1)

            def rows(self, v):
                return v[:, :, None].to_broadcast([P, 2 * NW * WL, WL])

            def vec_softmax(self, e, o):
                s3 = self.sco.rearrange("p (n b) -> p n b", b=WL)
                self.st.wait(e, "t_rd", WL)
                o.do(e.tensor_reduce(self.small, s3, AX.X, ALU.max))
                o.sync()
                e.tensor_tensor(s3, s3, self.rows(self.small), ALU.subtract).then_inc(S("t_s").sem, 1)

            def vec_sums(self, e, o):
                self.st.wait(e, "t_e", 1)
                o.do(e.tensor_reduce(self.small, self.sco.rearrange("p (n b) -> p n b", b=WL), AX.X, ALU.add))
                o.sync()
                o.do(e.reciprocal(self.small, self.small))

            def vec_values(self, e, o, a):
                self.vec_pair(e, o, a, 1)

            def vec_merge(self, e, o):
                self.st.wait(e, "t_rd", 2 * WL)
                o.sync()
                inv = self.small.rearrange("p (r w a) -> p r w a", r=2, w=NW)
                for r in range(2):
                    w = self.window(r, H * r, H)
                    o.do(e.tensor_tensor(w, w, inv[:, r][:, :, :, None].to_broadcast([P, NW, WL, H]), ALU.mult))
                o.sync()
                self.st.wait(e, "t_cv", 1)
                e.tensor_tensor(self.sco.rearrange("p (t c) -> p t c", c=C), self.q3[:, :, 0:C], self.q3[:, :, C:2 * C],
                                ALU.add).then_inc(S("t_sum").sem, 1)

            def vec_norm(self, e, o):
                self.st.wait(e, "t_prc", 8)
                o.do(e.tensor_reduce(self.small2, self.sq.rearrange("p (t c) -> p t c", c=C), AX.X, ALU.add))
                o.sync()
                e.tensor_scalar(self.small2, self.small2, 1.0 / C, EPS, ALU.mult, ALU.add).then_inc(S("t_var").sem, 1)
                self.st.wait(e, "t_std", 1)
                o.do(e.reciprocal(self.small2, self.small2))
                o.sync()
                dl = self.dl.rearrange("p (t c) -> p t c", c=C)
                o.do(e.tensor_tensor(dl, dl, self.small2[:, :, None].to_broadcast([P, NTOK, C]), ALU.mult))
                o.sync()
                self.st.wait(e, "t_tb", 1)
                self.st.wait(e, "t_pr", 8)
                e.tensor_tensor(self.done.rearrange("p (c t) -> p t c", c=C), dl,
                                self.tok.rearrange("p (t c) -> p t c", c=C), ALU.add).then_inc(S("t_out").sem, 1)

            def pool_scores(self, e, o, a):
                if a == 0:
                    self.st.wait(e, "t_qc", 16)
                else:
                    self.st.wait(e, "t_rd", a)
                self.product(e, 1, a, 0).then_inc(S("t_pp").sem, 1)

            def pool_values(self, e, o, a):
                if a == 0:
                    self.st.wait(e, "t_e", 1)
                self.st.wait(e, "t_rd", WL + a)
                o.sync()
                self.product(e, 1, a, 1).then_inc(S("t_pp").sem, 1)

            def pool_conv_centre(self, e, o):
                self.st.wait(e, "t_k", 1)
                self.st.wait(e, "t_rd", WL)
                o.do(e.tensor_tensor(self.q3[:, :, C:2 * C], self.q3[:, :, 2 * C:3 * C],
                                     cw[:, 1:2, :].to_broadcast([P, NTOK, C]), ALU.mult))

            def pool_conv(self, e, o, k):
                r, tap, w = k // 4, 2 * (k // 2 % 2), slice((k % 2) * NW // 2, (k % 2 + 1) * NW // 2)
                n = WL - 1
                to, of = (slice(1, WL), slice(0, n)) if tap == 0 else (slice(0, n), slice(1, WL))
                kw, vw = self.window(r, C + H * r, H)[:, w], self.window(r, 2 * C + H * r, H)[:, w]
                t = conv_tmp[:].rearrange("p (w b c) -> p w b c", w=NW // 2, b=n)
                wt = cw[:, tap:tap + 1, H * r:H * r + H][:, None].to_broadcast([P, NW // 2, n, H])
                o.sync()
                o.do(e.tensor_tensor(t, vw[:, :, of, :], wt, ALU.mult))
                o.sync()
                ins = e.tensor_tensor(kw[:, :, to, :], kw[:, :, to, :], t, ALU.add)
                o.do(ins)
                o.sync()
                if k == 7:
                    e.engine_nop().then_inc(S("t_cv").sem, 1)

            def pool_residual(self, e, o):
                self.st.wait(e, "t_x2", 128)
                t = self.tok.rearrange("p (t c) -> p t c", c=C)
                e.tensor_tensor(t, t, lb[:][:, None, :].to_broadcast([P, NTOK, C]), ALU.add).then_inc(S("t_tb").sem, 1)

        def transfer_chunk(e, n, arrivals):
            e.dma_start(wb[:, buffer_of(n)].rearrange("p a w -> p (a w)"),
                        wsplit[(n + NU - 1) % NU]).then_inc(arrivals.sem(n), 16)

        def shared(par, fin=None, images=None, prep=None):
            split = prep is not None
            sgh = [words(R_SGH + q * HALF, HALF) for q in range(2)]
            psG, psU, psD = banks[0:2], banks[2:4], banks[4:6]
            chunk_in = Arrivals("chunk_loaded")
            st = Stage(h_g=NSLOT, h_u=NSLOT, h_silu=NSLOT, h_mul=NSLOT, h_hi=NSLOT, h_lo=NSLOT, h_d=2 * NSLOT,
                       h_acc=2 * NSLOT, scat_0=128, scat_1=128)
            xn = words(R_XN, NT * D).rearrange("p (t d) -> p t d", t=NT)
            FIN = {j: [2 * j, 2 * j + 1] for j in range(4)}
            GATHER = {1: [4, 5], 2: [6, 7]}
            SCATTER = {0: [0, 1], 3: [2, 3], 4: [4, 5], 5: [6, 7]}
            SCATTER_FIRST = {j + 5: [4 * j, 4 * j + 1, 4 * j + 2, 4 * j + 3] for j in range(2)}
            for table in (FIN, GATHER, SCATTER, SCATTER_FIRST):
                for j in range(NSLOT):
                    table.setdefault(j, [])
            fin_slots = 4
            atts = []
            if images:
                def rows_ready(e):
                    for t in (2, 3, 4, 5):
                        fin.rows_out.wait(e, t)

                def finished(e):
                    for t in (6, 7):
                        fin.rows_out.wait(e, t)

                def scattered(e):
                    st.wait(e, "scat_0", 128)

                one = Attention(images[0], fin_slots + 1, 0, (fin_slots, 0), rows_ready, scattered, finished,
                                lambda e: st.wait(e, "scat_1", 128), store=True)
                merged, result, stored = (one.st.base[n] + k for n, k in (("t_sum", 1), ("t_out", 1), ("t_st", 16 * QUEUED)))
                pool_stored = one.st.base["t_pst"] + 16 * (64 - QUEUED)

                def first_stored(e):
                    e.wait_ge(S("t_st").sem, stored)
                    e.wait_ge(S("t_pst").sem, pool_stored)

                one.st.end()
                two = Attention(images[1], one.last + 1, 2 * TOKW, (one.merged, 1), lambda e: e.wait_ge(S("t_sum").sem, merged),
                                lambda e: e.wait_ge(S("t_out").sem, result), lambda e: None,
                                first_stored, store=False)
                two.st.end()
                atts = [one, two]
            last = max([a.last for a in atts], default=-1)

            def extra(table, slot, pos, *args):
                for a in atts:
                    for fn in a.table[table].get((slot, pos), []):
                        fn(*args)

            def turns(body):
                if images:
                    for j in range(NSLOT):
                        body(j, None)
                    for j in range(NSLOT, last + 1):
                        body(j, None, True)
                else:
                    for j in range(TURN):
                        body(j, None)

            def load_chunk(e, n):
                if n >= 2:
                    st.wait(e, "h_d", 8 * (n - 1))
                transfer_chunk(e, n, chunk_in)

            with nc.Block() as blk:
                @blk.sync
                def _(e):
                    if split:
                        def piece(n, i):
                            load_raw(e, 2 * n + 2, i)
                            if n < NU - 1:
                                load_raw(e, 2 * n + 3, i)
                            e.wait_ge(w_lo.sem, 2 * n + 3 if i is None else i * 4 + (2 * n + 3))
                            row = n if i is None else i * 2 + n
                            e.dma_start(wsplit[bass.ds(row, 1)].rearrange("o p w -> (o p) w"),
                                        wb[:, buffer_of(n + 1)].rearrange("p a w -> p (a w)")).then_inc(w_out.sem(n), 16)
                        with e.Fori(0, NU // 2 - 1) as i:
                            piece(0, i)
                            piece(1, i)
                        piece(NU - 2, None)
                        piece(NU - 1, None)
                        w_out.wait_last(e, NU)
                    else:
                        if fin:
                            for t in range(fin.WAYS):
                                fin.sync_load(e, t)
                        load_chunk(e, 1)
                        if fin:
                            for t in range(NT):
                                fin.store(e, t)
                                if t + fin.WAYS < NT:
                                    fin.sync_load(e, t + fin.WAYS)
                        if not images:
                            for n in range(2, NU):
                                load_chunk(e, n)
                    for j in range(last + 1):
                        for pos in (0, 1):
                            extra("sp", j, pos, e)
                    if fin:
                        fin.rows_out.wait_last(e, NT)

                @blk.tensor
                def _(e):
                    def products(ps, j, gu, name):
                        q, half, k = buffer_of(j // 4), (j // 2) % 2, j % 2
                        i = 0
                        for c in range(NDC):
                            for wp, xp in PASSES:
                                o = gu * NDC * HC + c * HC + k * P
                                m = e.matmul(ps[j % 2][:], wb[:, q, wp, o:o + P],
                                             xT[:, xp, c, half * HALF:(half + 1) * HALF],
                                             start=(i == 0), stop=(i == 3 * NDC - 1))
                                i += 1
                        m.then_inc(S(name).sem, 1)

                    def down(g, tt, r):
                        if 4 * g + tt >= 2:
                            st.wait(e, "h_acc", 4 * g + tt - 1, r, 16)
                        i = 0
                        for kt in range(KT):
                            for wp, hp in PASSES:
                                o = W3OFF + kt * D
                                m = e.matmul(psD[tt % 2][:], hs[:, g % 2, hp, kt, tt * P:(tt + 1) * P],
                                             wb[:, buffer_of(g // 2), wp, o:o + D], start=(i == 0), stop=(i == 5))
                                i += 1
                        m.then_inc(S("h_d").sem, 1)

                    def slot(j, r, only_extra=False):
                        if only_extra:
                            for pos in range(4):
                                extra("pe", j, pos, e)
                            return
                        if j % 4 == 0:
                            if split:
                                n = 2 * (j // 4) + 1
                                e.wait_ge(w_lo.sem, n if r is None else r * 4 + n)
                            else:
                                chunk_in.wait(e, j // 4, r)
                        if j >= 2:
                            st.wait(e, "h_mul", j - 1, r, 8)
                        g = j // 2 - 1
                        products(psG, j, 0, "h_g")
                        extra("pe", j, 0, e)
                        products(psU, j, 1, "h_u")
                        extra("pe", j, 1, e)
                        if g >= 0 and j % 2 == 0:
                            st.wait(e, "h_lo", 2 * g + 2, r, 8)
                        if g >= 0:
                            down(g, 2 * (j % 2), r)
                        extra("pe", j, 2, e)
                        if g >= 0:
                            down(g, 2 * (j % 2) + 1, r)
                        extra("pe", j, 3, e)
                        if split and r is None and j == 3:
                            prep.pe_ranks(e)
                            bias_product(e)
                        if images and j == NSLOT - 1:
                            tail()

                    def tail():
                        st.wait(e, "h_lo", NSLOT)
                        for tt in range(4):
                            down(NSLOT // 2 - 1, tt, None)

                    turns(slot)
                    if not images:
                        with e.Fori(0, NSLOT // TURN - 1) as r:
                            for j in range(TURN, 2 * TURN):
                                slot(j, r)
                        tail()

                @blk.scalar
                def _(e):
                    def slot(j, r, only_extra=False):
                        if only_extra:
                            for pos in range(4):
                                extra("act", j, pos, e)
                            return
                        if j >= 2:
                            st.wait(e, "h_lo", j - 1, r, 8)
                        st.wait(e, "h_g", j + 1, r, 8)
                        e.activation(sgh[j % 2], psG[j % 2][:], ACT.Silu).then_inc(S("h_silu").sem, 1)
                        extra("act", j, 0, e)
                        st.wait(e, "h_mul", j + 1, r, 8)
                        if j >= 4:
                            st.wait(e, "h_d", 4 * (j // 2 - 1), r, 16)
                        e.activation(hs[:, (j // 2) % 2, 0, j % 2, :], sgh[j % 2], ACT.Copy).then_inc(S("h_hi").sem, 1)
                        if split and j % 2 == 0:
                            n = j // 4
                            if j % 4 == 0:
                                ex = n if r is None else r * 2 + n
                                split_high(e, 2 * n + 1, wr[:, bass.ds(ex, 1)].rearrange("p o a w -> p (o a) w"), r)
                            else:
                                if n:
                                    st.wait(e, "h_d", 8 * n, r, 16)
                                if n >= 2:
                                    w_out.wait(e, n - 2, r)
                                split_high(e, 2 * n + 2, wb[:, buffer_of(n + 1)], r)
                        if split and r is None and j == 0:
                            prep.act_scores(e)
                        if split and r is None and j == TURN - 1:
                            bias_move(e)
                        if images and j % 4 == 2 and 4 <= j < NSLOT - 4:
                            load_chunk(e, j // 4 + 1)
                        for pos in range(1, 4):
                            extra("act", j, pos, e)

                    turns(slot)
                    if not images:
                        with e.Fori(0, NSLOT // TURN - 1) as r:
                            for j in range(TURN, 2 * TURN):
                                slot(j, r)

                @blk.gpsimd
                def _(e):
                    o = Own(e, own["pool"])
                    def scatter(t):
                        for k in range(2):
                            e.indirect_dma_start(out=sorted_x,
                                                 out_offset=bass.IndirectOffsetOnAxis(ap=slots[:, par, k, t:t + 1],
                                                                                      axis=0),
                                                 in_=xn[:, t, :], in_offset=None).then_inc(S(f"scat_{t // TH}").sem, 16)

                    def slot(j, r, only_extra=False):
                        if only_extra:
                            extra("pool", j, 0, e, o)
                            return
                        st.wait(e, "h_hi", j + 1, r, 8)
                        e.tensor_tensor(hs[:, (j // 2) % 2, 1, j % 2, :], sgh[j % 2],
                                        hs[:, (j // 2) % 2, 0, j % 2, :], ALU.subtract).then_inc(S("h_lo").sem, 1)
                        if r is None:
                            if fin:
                                for t in FIN[j]:
                                    fin.pool_rstd(e, t)
                                for t in GATHER[j]:
                                    fin.pool_gather(e, t)
                            if split and j == 5:
                                prep.st.wait(e, "p_slot", 1)
                                e.wait_ge(z_out.sem, z_out.n)
                            for t in (SCATTER if fin else SCATTER_FIRST)[j]:
                                scatter(t)
                        extra("pool", j, 0, e, o)

                    if fin:
                        for t in range(fin.WAYS):
                            fin.pool_gather(e, t)
                    turns(slot)
                    if not images:
                        with e.Fori(0, NSLOT // TURN - 1) as r:
                            for j in range(TURN, 2 * TURN):
                                slot(j, r)
                    for q in range(2):
                        st.wait(e, f"scat_{q}", 128)
                    own["pool"].n += o.k

                @blk.vector
                def _(e):
                    o = Own(e, own["dve"])
                    routing = prep.route(e, o) if split else None

                    def slot(j, r, only_extra=False):
                        if only_extra:
                            extra("vec", j, 0, e, o)
                            return
                        st.wait(e, "h_silu", j + 1, r, 8)
                        st.wait(e, "h_u", j + 1, r, 8)
                        e.tensor_tensor(sgh[j % 2], psU[j % 2][:], sgh[j % 2], ALU.mult).then_inc(S("h_mul").sem, 1)
                        if j >= 2:
                            g = j // 2 - 1
                            for tt in (2 * (j % 2), 2 * (j % 2) + 1):
                                add(g, tt, r)
                        if fin and r is None:
                            for t in FIN[j]:
                                fin.vector_sum(e, o, t)
                                if len(FIN[j]) == 2 and t % 2:
                                    fin.vector_norm(e, t - 1)
                            if FIN[j]:
                                fin.vector_norm(e, t)
                        if split and j % 2 == 0:
                            n = j // 4
                            if j % 4 == 0:
                                ex = n if r is None else r * 2 + n
                                split_low(e, 2 * n + 1, wr[:, bass.ds(ex, 1)].rearrange("p o a w -> p (o a) w"), r)
                            else:
                                split_low(e, 2 * n + 2, wb[:, buffer_of(n + 1)], r)
                        if split and r is None and j == 1:
                            e.wait_ge(c_in.sem, c_in.n)
                        if split and r is None and j == 5:
                            attention_constants(e, o)
                        if split and r is None and 1 <= j <= 4:
                            part = -(-len(routing[2]) // 2)
                            for step in (routing[0], routing[1], routing[2][:part], routing[2][part:])[j - 1]:
                                step()
                        extra("vec", j, 0, e, o)
                        if images and j == NSLOT - 1:
                            tail()

                    def add(g, tt, r):
                        st.wait(e, "h_d", 4 * g + tt + 1, r, 16)
                        a = acc[:, (g % 2) * TH + tt, :]
                        if r is None and g < 2:
                            e.tensor_copy(a, psD[tt % 2][:]).then_inc(S("h_acc").sem, 1)
                        else:
                            st.wait(e, "h_acc", 4 * (g - 2) + tt + 1, r, 16)
                            e.tensor_tensor(a, psD[tt % 2][:], a, ALU.add).then_inc(S("h_acc").sem, 1)

                    def tail():
                        for tt in range(4):
                            add(NSLOT // 2 - 1, tt, None)

                    turns(slot)
                    if not images:
                        with e.Fori(0, NSLOT // TURN - 1) as r:
                            for j in range(TURN, 2 * TURN):
                                slot(j, r)
                        tail()
                    own["dve"].n += o.k
            st.end()
            if not split:
                chunk_in.end(NU)
            if fin:
                fin.end()
            if split:
                prep.st.end()
            return atts[-1] if atts else None

        def routed(par, prep=None, att=None):
            at = [R_QKV]

            def take(n, dt=F32):
                a = words(at[0], n, dt)
                at[0] += n
                assert at[0] <= R_SMALL
                return a

            xs = [take(D) for _ in range(2)]
            xsT = [take(D, BF16).rearrange("p (a n) -> p a n", a=2) for _ in range(2)]
            sg = [take(HC) for _ in range(2)]
            hf = [take(HC) for _ in range(2)]
            hb = [take(HC, BF16).rearrange("p (a n) -> p a n", a=2) for _ in range(2)]
            hT = [take(HC, BF16).rearrange("p (a k n) -> p a k n", a=2, k=KT) for _ in range(2)]
            yo = [take(D) for _ in range(2)]
            psX, psH, psHT, psY = banks[0], banks[1:3], banks[3][:].bitcast(BF16)[:, 0:2 * HC], banks[4:6]
            rows_in, rows_out = Arrivals("rows_loaded"), Arrivals("rows_stored")
            st = Stage(r_T=NB + 1, r_hi=NB + 1, r_lo=NB + 1, r_wu=NB, r_wd=NB, r_h=NB, r_silu=NB, r_mul=NB, r_hbh=NB,
                       r_hbl=NB, r_HT=NB, r_hT=NB, r_y=NB, r_yo=NB)

            def wait(e, name, k):
                st.wait(e, name, k)

            def program(e, block, hooks):
                for k in range(LATE if prep else NB):
                    if prep and k:
                        t = (k - 1) // 2
                        block(k, lambda n: hooks(k % 2 == 0, n, t, t == 0))
                    else:
                        block(k, lambda n: None)

            LATE = 2 * NT + 1
            late = range(LATE, NB) if prep else []

            with nc.Block() as blk:
                @blk.sync
                def _(e):
                    def load(k):
                        if k >= 2:
                            wait(e, "r_T", k - 1)
                        e.dma_start(xs[k % 2], sorted_x[k * P:(k + 1) * P, :]).then_inc(rows_in.sem(k), 16)

                    def block(k, hook):
                        load(k + 1)
                        hook(0)

                    def hooks(second, n, t, first):
                        if not second:
                            prep.sync(e, t, first)

                    load(0)
                    if att:
                        blocks = NT + 1
                        for k in range(blocks):
                            load(k + 1)
                            att.store(e, k * 64 // blocks, (k + 1) * 64 // blocks)
                            if k in (1, 3, 5, 7):
                                prep.sync(e, k // 2, k == 1)
                        e.wait_ge(S("t_st").sem, S("t_st").n)
                        for k in range(blocks, LATE):
                            block(k, lambda n: hooks(k % 2 == 0, n, (k - 1) // 2, False))
                    else:
                        program(e, block, hooks)
                    for k in late:
                        block(k, lambda n: None)
                    if prep:
                        wait(e, "r_y", NB - 1)
                        transfer_chunk(e, 0, Arrivals("chunk_loaded"))
                    rows_out.wait_last(e, NB)

                @blk.tensor
                def _(e):
                    def rows_T(k):
                        rows_in.wait(e, k)
                        if k >= 1:
                            wait(e, "r_lo", k)
                        for c in range(NDC):
                            m = e.transpose(psX[:, c * P:(c + 1) * P], xs[k % 2][:, c * P:(c + 1) * P], ident[:])
                        m.then_inc(S("r_T").sem, 1)

                    def up(k, between):
                        wait(e, "r_lo", k + 1)
                        wait(e, "r_wu", k + 1)
                        if k >= 2:
                            wait(e, "r_mul", k - 1)
                        n = 0
                        for c in range(NDC):
                            if c == NDC // 2:
                                between()
                            for wp, xp in PASSES:
                                m = e.matmul(psH[k % 2][:], xsT[k % 2][:, xp, c * P:(c + 1) * P],
                                             wb[:, k % 2, wp, c * D:(c + 1) * D], start=(n == 0),
                                             stop=(n == 3 * NDC - 1))
                                n += 1
                        m.then_inc(S("r_h").sem, 1)

                    def hidden_T(k):
                        wait(e, "r_hbl", k + 1)
                        if k >= 1:
                            wait(e, "r_hT", k)
                        for a in range(2):
                            for kt in range(KT):
                                n = a * KT + kt
                                m = e.transpose(psHT[:, n * P:(n + 1) * P], hb[k % 2][:, a, kt * P:(kt + 1) * P],
                                                identb[:])
                        m.then_inc(S("r_HT").sem, 1)

                    def down(k):
                        wait(e, "r_hT", k + 1)
                        wait(e, "r_wd", k + 1)
                        if k >= 2:
                            wait(e, "r_yo", k - 1)
                        n = 0
                        for kt in range(KT):
                            for wp, hp in PASSES:
                                o = W3OFF + kt * D
                                m = e.matmul(psY[k % 2][:], hT[k % 2][:, hp, kt, :], wb[:, k % 2, wp, o:o + D],
                                             start=(n == 0), stop=(n == 3 * KT - 1))
                                n += 1
                        m.then_inc(S("r_y").sem, 1)

                    def block(k, hook):
                        rows_T(k + 1)
                        up(k, lambda: hidden_T(k - 1) if k else None)
                        hook(0)
                        if k:
                            down(k - 1)
                        hook(1)

                    def hooks(second, n, t, first):
                        if second and n == 0 and not first:
                            prep.pe_router(e, t - 1, False)
                        if second and n == 1:
                            prep.pe_transpose(e, t, first)

                    rows_T(0)
                    program(e, block, hooks)
                    for k in late:
                        def hook(n):
                            if n == 0 and k == LATE + 1:
                                prep.pe_router(e, NT - 1, False)
                            if n == 0 and k == LATE + 3:
                                prep.pe_ranks(e)
                        block(k, hook)
                    hidden_T(NB - 1)
                    down(NB - 1)

                @blk.scalar
                def _(e):
                    def rows_hi(k):
                        wait(e, "r_T", k + 1)
                        if k >= 2:
                            wait(e, "r_h", k - 1)
                        e.activation(xsT[k % 2][:, 0, :], psX[:], ACT.Copy).then_inc(S("r_hi").sem, 1)

                    def weights_down(k):
                        ex = e.value_load(bexp[0:1, par, k:k + 1], min_val=0, max_val=E - 1)
                        if k >= 2:
                            wait(e, "r_y", k - 1)
                        e.activation(wb[:, k % 2, :, W3OFF:WW],
                                     wr[:, bass.ds(ex, 1), :, W3OFF:WW].rearrange("p o a w -> p (o a) w"),
                                     ACT.Copy).then_inc(S("r_wd").sem, 1)

                    def hidden(k):
                        wait(e, "r_h", k + 1)
                        if k >= 2:
                            wait(e, "r_mul", k - 1)
                        e.activation(sg[k % 2], psH[k % 2][:, 0:HC], ACT.Silu).then_inc(S("r_silu").sem, 1)
                        wait(e, "r_mul", k + 1)
                        if k >= 2:
                            wait(e, "r_HT", k - 1)
                        e.activation(hb[k % 2][:, 0, :], hf[k % 2], ACT.Copy).then_inc(S("r_hbh").sem, 1)

                    def result(k):
                        wait(e, "r_y", k + 1)
                        if k >= 2:
                            rows_out.wait(e, k - 2)
                        e.activation(yo[k % 2], psY[k % 2][:], ACT.Copy).then_inc(S("r_yo").sem, 1)
                        wait(e, "r_yo", k + 1)
                        e.dma_start(sorted_y[k * P:(k + 1) * P, :], yo[k % 2]).then_inc(rows_out.sem(k), 16)

                    def block(k, hook):
                        rows_hi(k + 1)
                        weights_down(k)
                        hidden(k)
                        hook(0)
                        if k:
                            result(k - 1)

                    def hooks(second, n, t, first):
                        if second:
                            prep.store(e, t)
                        elif not first:
                            prep.act(e, t - 1, False)

                    rows_hi(0)
                    program(e, block, hooks)
                    for k in late:
                        def hook(n):
                            if k == LATE:
                                prep.act(e, NT - 1, False)
                            if k == LATE + 1:
                                prep.act_scores(e)
                        block(k, hook)
                    result(NB - 1)

                @blk.gpsimd
                def _(e):
                    if prep:
                        prep.pool(e, 0)
                        for t in range(1, NT):
                            prep.pool(e, t)

                @blk.vector
                def _(e):
                    o = Own(e, own["dve"])

                    def rows_lo(k):
                        wait(e, "r_hi", k + 1)
                        e.tensor_tensor(xsT[k % 2][:, 1, :], psX[:], xsT[k % 2][:, 0, :],
                                        ALU.subtract).then_inc(S("r_lo").sem, 1)

                    def weights_up(k):
                        ex = e.value_load(bexp[0:1, par, k:k + 1], min_val=0, max_val=E - 1)
                        if k >= 2:
                            wait(e, "r_h", k - 1)
                        e.tensor_copy(wb[:, k % 2, :, 0:W3OFF],
                                      wr[:, bass.ds(ex, 1), :, 0:W3OFF].rearrange("p o a w -> p (o a) w")
                                      ).then_inc(S("r_wu").sem, 1)

                    def hidden(k):
                        wait(e, "r_silu", k + 1)
                        if k >= 2:
                            wait(e, "r_hbl", k - 1)
                        e.tensor_tensor(hf[k % 2], psH[k % 2][:, HC:2 * HC], sg[k % 2], ALU.mult).then_inc(
                            S("r_mul").sem, 1)
                        wait(e, "r_hbh", k + 1)
                        e.tensor_tensor(hb[k % 2][:, 1, :], hf[k % 2], hb[k % 2][:, 0, :],
                                        ALU.subtract).then_inc(S("r_hbl").sem, 1)

                    def hidden_T(k):
                        wait(e, "r_HT", k + 1)
                        if k >= 2:
                            wait(e, "r_y", k - 1)
                        e.tensor_copy(hT[k % 2].rearrange("p a k n -> p (a k n)"), psHT).then_inc(S("r_hT").sem, 1)

                    def block(k, hook):
                        rows_lo(k + 1)
                        if k:
                            hidden_T(k - 1)
                        if k < NB - 1:
                            weights_up(k + 1)
                        hook(0)
                        hidden(k)
                        hook(1)

                    def hooks(second, n, t, first):
                        if not second and n == 1:
                            if not first:
                                prep.vector_low(e, t - 1)
                            prep.vector_stats(e, o, t)
                        if second and n == 0:
                            prep.vector_norm(e, t, first)
                        if second and n == 1 and not first:
                            prep.vector_logits(e, t - 1)

                    weights_up(0)
                    rows_lo(0)
                    program(e, block, hooks)
                    if prep:
                        chosen, weights, slot_steps = prep.route(e, o)
                        few, many = len(slot_steps) // 5, 3 * len(slot_steps) // 5
                        steps = [[lambda: prep.vector_low(e, NT - 1)], [lambda: prep.vector_logits(e, NT - 1)],
                                 chosen, weights + slot_steps[:few], slot_steps[few:many], slot_steps[many:]]
                        for k in late:
                            block(k, lambda n: [s() for s in steps[k - LATE]] if n == 1 else None)
                    hidden_T(NB - 1)
                    own["dve"].n += o.k
            st.end()
            rows_in.end(NB + 1)
            rows_out.end(NB)
            if prep:
                prep.st.end()

        shared(0, prep=prepare_alone())
        routed(0, Prepare(0, 1, 1, banks[6:7], banks[7]))
        att = shared(1, fin=Finish(0, 0, 0), images=(0, 1))
        routed(1, Prepare(1, 0, 0, banks[6:7], banks[7]), att)
        att = shared(0, fin=Finish(0, 1, 1), images=(2, 3))
        routed(0, Prepare(1, 1, 1, banks[6:7], banks[7]), att)
        shared(1, fin=Finish(1, 0, 0))
        routed(1)
        finish_alone(1, 1, 1)


def kernel(L0_attn_x, L0_attn_qkv_w, L0_attn_conv_w0, L0_attn_conv_b0, L0_attn_conv_w1, L0_attn_conv_b1, L0_attn_proj_w,
           L0_attn_proj_b, L0_attn_ln_w, L0_attn_ln_b, L0_ffn_w12, L0_ffn_w3, L0_ffn_router_w, L0_ffn_expert_bias,
           L0_ffn_sw1, L0_ffn_sw2, L0_ffn_sw3):
    import numpy as np
    import concourse.bacc as bacc
    from concourse.bass_utils import run_bass_kernel_spmd

    A = np.asarray
    B, R, D = L0_attn_x.shape
    E = L0_ffn_w12.shape[0]
    NU = L0_ffn_sw1.shape[0] // 256

    def up_words(w, n):
        w = A(w).reshape(n, -1, D // P, P)
        return w.transpose(0, 3, 2, 1).reshape(n, P, -1)

    def down_words(w, n):
        w = w.reshape(n, D, 2, P)
        return w.transpose(0, 3, 2, 1).reshape(n, P, -1)

    sw3 = A(L0_ffn_sw3).reshape(D, NU, 256).transpose(1, 0, 2)
    wsh = np.concatenate([up_words(L0_ffn_sw1, NU), up_words(L0_ffn_sw2, NU), down_words(sw3, NU)], 2)
    wrt = np.concatenate([up_words(L0_ffn_w12, E), down_words(A(L0_ffn_w3), E)], 2)
    arrays = {
        "x": A(L0_attn_x).reshape(B * R, D),
        "wall": np.concatenate([np.stack([wsh, wrt], 1).reshape(2 * NU, P, -1), wsh[:1]], 0),
        "rwT": A(L0_ffn_router_w).T,
        "ebias": A(L0_ffn_expert_bias),
        "qkvw": A(L0_attn_qkv_w),
        "projw": A(L0_attn_proj_w),
        "projb": np.tile(A(L0_attn_proj_b), 8)[None],
        "convw": np.concatenate([A(L0_attn_conv_w0)[:, 0, 1, :].T, A(L0_attn_conv_w1)[:, 0, :, 1].T], 1),
        "convb": np.tile(np.concatenate([A(L0_attn_conv_b0), A(L0_attn_conv_b1)]), 8)[:, None],
        "lnw": A(L0_attn_ln_w),
        "lnb": A(L0_attn_ln_b),
    }
    nc = bacc.Bacc("TRN2", target_bir_lowering=False, num_devices=1, dynamic_dma_scratch_size=8192)
    arrays = {n: np.ascontiguousarray(a) for n, a in arrays.items()}
    aps = [nc.dram_tensor(n, a.shape, mybir.dt.from_np(a.dtype), kind="ExternalInput").ap() for n, a in arrays.items()]
    out = nc.dram_tensor("out", [B * R, D], F32, kind="ExternalOutput").ap()
    macaron(nc, *aps, out)
    got = run_bass_kernel_spmd(nc, [arrays], core_ids=[0])
    return got.results[0]["out"].reshape(B, R, D)
```
